# Optimizing a Trainium2 kernel written in Bass

```python
import numpy as np
import jax
import jax.numpy as jnp

def _softmax(x, axis=-1):
    return jax.nn.softmax(x, axis=axis)

def _gelu(x):
    return jax.nn.gelu(x, approximate=True)

def _silu(x):
    return jax.nn.silu(x)

def _sigmoid(x):
    return jax.nn.sigmoid(x)

def _layernorm(x, axis=-1, eps=1e-05):
    m = jnp.mean(x, axis=axis, keepdims=True)
    v = jnp.var(x, axis=axis, keepdims=True)
    return (x - m) / jnp.sqrt(v + eps)

def _scatter_add(tgt, idx, src, axis=0):
    return tgt.at[idx].add(src)

def _segment_sum(src, seg, n):
    return jax.ops.segment_sum(src, seg, n)
kernel_name = 'mk_gnn_resnorm_d4_gnn_r8_40c523'

def setup_inputs(seed: int=0):
    np.random.seed(seed)
    _w = jnp.asarray

    def _rec_inputs():
        import jax
        import jax.numpy as jnp
        _gk = jax.random.key(seed)
        x = -0.0001006 + 1 * jax.random.normal(jax.random.fold_in(_gk, 1), (6250, 96), jnp.float32)
        _s = jax.random.randint(jax.random.fold_in(_gk, 2), (50000,), 0, 6250, jnp.int32)
        _d = jax.random.randint(jax.random.fold_in(_gk, 3), (50000,), 0, 6250, jnp.int32)
        _loop = jnp.arange(6250, dtype=jnp.int32)
        src = jnp.concatenate([_s, _d, _loop])
        dst = jnp.concatenate([_d, _s, _loop])
        _o = jnp.argsort(dst, stable=True)
        src = src[_o]
        dst = dst[_o]
        edge_attr_96 = 5.93493e-05 + 1.00006 * jax.random.normal(jax.random.fold_in(_gk, 12), (106250, 96), jnp.float32)
        edge_weight = jax.random.uniform(jax.random.fold_in(_gk, 14), (106250,), jnp.float32, 0.0, 0.999998)
        return (x, src, dst, edge_attr_96, edge_weight)
    x, src, dst, edge_attr_96, edge_weight = _rec_inputs()

    def _L0_gnn_setup():
        import jax, jax.numpy as jnp
        import numpy as np
        N_NODES = 6250
        N_EDGES = 100000
        IN_DIM = 96
        NUM_HEADS = 8
        HEAD_DIM = IN_DIM // NUM_HEADS
        key = jax.random.key(seed)
        ks = jax.random.split(key, 11)
        s = 1.0 / np.sqrt(IN_DIM)
        return {'x': jax.random.normal(ks[0], (N_NODES, IN_DIM), dtype=jnp.float32), 'edge_index': jax.random.randint(ks[1], (2, N_EDGES), 0, N_NODES, dtype=jnp.int64), 'edge_attr': jax.random.normal(ks[2], (N_EDGES, IN_DIM), dtype=jnp.float32), 'Wq': jax.random.normal(ks[3], (IN_DIM, IN_DIM), dtype=jnp.float32) * s, 'bq': jax.random.normal(ks[4], (IN_DIM,), dtype=jnp.float32) * s, 'Wk': jax.random.normal(ks[5], (IN_DIM, IN_DIM), dtype=jnp.float32) * s, 'bk': jax.random.normal(ks[6], (IN_DIM,), dtype=jnp.float32) * s, 'We': jax.random.normal(ks[7], (IN_DIM, IN_DIM), dtype=jnp.float32) * s, 'be': jax.random.normal(ks[8], (IN_DIM,), dtype=jnp.float32) * s, 'Wv': jax.random.normal(ks[9], (IN_DIM, IN_DIM), dtype=jnp.float32) * s, 'bv': jax.random.normal(ks[10], (IN_DIM,), dtype=jnp.float32) * s}
    _L0_gnn_all = _L0_gnn_setup()
    _L0_gnn_in = {k: v for k, v in _L0_gnn_all.items() if k in ('Wq', 'bq', 'Wk', 'bk', 'We', 'be', 'Wv', 'bv')}
    del _L0_gnn_all

    def _L1_gnn_setup():
        import jax, jax.numpy as jnp
        import numpy as np
        N_NODES = 12500
        N_EDGES = 100000
        D = 96
        BN_EPS = 1e-05
        LEAKY_SLOPE = 0.01

        def _batch_norm(h, gamma, beta):
            mu = h.mean(axis=0)
            var = jnp.mean(jnp.square(h - mu), axis=0)
            return gamma * (h - mu) * jax.lax.rsqrt(var + BN_EPS) + beta

        def _forward(x, edge_index, W_self1, W_neigh1, W_pool, b_pool, W_self2, W_neigh2, g1, beta1, g2, beta2):
            src, dst = (edge_index[0], edge_index[1])
            n = x.shape[0]
            deg = jax.ops.segment_sum(jnp.ones((src.shape[0],), x.dtype), dst, num_segments=n)
            agg_sum = jax.ops.segment_sum(x[src], dst, num_segments=n)
            h_mean = agg_sum / jnp.maximum(deg, 1.0)[:, None]
            out1 = x @ W_self1 + h_mean @ W_neigh1
            out1 = _batch_norm(out1, g1, beta1)
            hp = jax.nn.relu(x @ W_pool + b_pool)
            agg_max = jax.ops.segment_max(hp[src], dst, num_segments=n)
            h_max = jnp.where(deg[:, None] > 0, agg_max, 0.0)
            out2 = x @ W_self2 + h_max @ W_neigh2
            out2 = _batch_norm(out2, g2, beta2)
            return jax.nn.leaky_relu(out1 + out2, negative_slope=LEAKY_SLOPE)
        key = jax.random.key(seed)
        ks = jax.random.split(key, 9)
        x = jax.random.normal(ks[0], (N_NODES, D), dtype=jnp.float32)
        edge_index = jax.random.randint(ks[1], (2, N_EDGES), 0, N_NODES, dtype=jnp.int64)
        s = 0.05
        return {'x': x, 'edge_index': edge_index, 'W_self1': jax.random.normal(ks[2], (D, D), dtype=jnp.float32) * s, 'W_neigh1': jax.random.normal(ks[3], (D, D), dtype=jnp.float32) * s, 'W_pool': jax.random.normal(ks[4], (D, D), dtype=jnp.float32) * s, 'b_pool': jax.random.normal(ks[5], (D,), dtype=jnp.float32) * s, 'W_self2': jax.random.normal(ks[6], (D, D), dtype=jnp.float32) * s, 'W_neigh2': jax.random.normal(ks[7], (D, D), dtype=jnp.float32) * s, 'g1': jnp.ones((D,), jnp.float32), 'beta1': jnp.zeros((D,), jnp.float32), 'g2': jnp.ones((D,), jnp.float32), 'beta2': jnp.zeros((D,), jnp.float32)}
    _L1_gnn_all = _L1_gnn_setup()
    _L1_gnn_in = {k: v for k, v in _L1_gnn_all.items() if k in ('W_self1', 'W_neigh1', 'W_pool', 'b_pool', 'W_self2', 'W_neigh2', 'g1', 'beta1', 'g2', 'beta2')}
    del _L1_gnn_all

    def _L2_gnn_setup():
        import jax, jax.numpy as jnp
        import numpy as np
        N_NODES = 6250
        N_EDGES = 100000
        D_IN = 96
        D_OUT = 96
        key = jax.random.key(seed)
        k1, k2, k3, k4 = jax.random.split(key, 4)
        feat = jax.random.normal(k1, (N_NODES, D_IN), dtype=jnp.float32)
        std = (2.0 / (D_IN + D_OUT)) ** 0.5
        weight = jax.random.normal(k2, (D_IN, D_OUT), dtype=jnp.float32) * std
        bias = jnp.zeros((D_OUT,), dtype=jnp.float32)
        src = jax.random.randint(k3, (N_EDGES,), 0, N_NODES, dtype=jnp.int64)
        dst = jax.random.randint(k4, (N_EDGES,), 0, N_NODES, dtype=jnp.int64)
        return {'feat': feat, 'weight': weight, 'bias': bias, 'src': src, 'dst': dst}
    _L2_gnn_all = _L2_gnn_setup()
    _L2_gnn_in = {k: v for k, v in _L2_gnn_all.items() if k in ('weight', 'bias')}
    del _L2_gnn_all

    def _L3_gnn_setup():
        import jax, jax.numpy as jnp
        import numpy as np
        LN_EPS = 1e-05
        N_NODES = 6250
        N_EDGES = 100000
        IN_DIM = 96
        OUT_DIM = 96
        key = jax.random.key(seed)
        k = jax.random.split(key, 5)
        x = jax.random.normal(k[0], (N_NODES, IN_DIM), dtype=jnp.float32)
        edge_index = jax.random.randint(k[1], (2, N_EDGES), 0, N_NODES, dtype=jnp.int64 if jax.config.read('jax_enable_x64') else jnp.int32)
        edge_weight = jax.random.uniform(k[2], (N_EDGES,), dtype=jnp.float32)
        W = jax.random.normal(k[3], (IN_DIM, OUT_DIM), dtype=jnp.float32) / np.sqrt(IN_DIM)
        bias = jnp.zeros((OUT_DIM,), dtype=jnp.float32)
        gamma = jnp.ones((OUT_DIM,), dtype=jnp.float32)
        beta = jnp.zeros((OUT_DIM,), dtype=jnp.float32)
        return {'x': x, 'edge_index': edge_index, 'edge_weight': edge_weight, 'W': W, 'bias': bias, 'gamma': gamma, 'beta': beta}
    _L3_gnn_all = _L3_gnn_setup()
    _L3_gnn_in = {k: v for k, v in _L3_gnn_all.items() if k in ('W', 'bias', 'gamma', 'beta')}
    del _L3_gnn_all
    return {'x': x, 'src': src, 'dst': dst, 'edge_attr_96': edge_attr_96, 'edge_weight': edge_weight, 'L0_gnn_Wq': _L0_gnn_in['Wq'], 'L0_gnn_bq': _L0_gnn_in['bq'], 'L0_gnn_Wk': _L0_gnn_in['Wk'], 'L0_gnn_bk': _L0_gnn_in['bk'], 'L0_gnn_We': _L0_gnn_in['We'], 'L0_gnn_be': _L0_gnn_in['be'], 'L0_gnn_Wv': _L0_gnn_in['Wv'], 'L0_gnn_bv': _L0_gnn_in['bv'], 'L1_gnn_W_self1': _L1_gnn_in['W_self1'], 'L1_gnn_W_neigh1': _L1_gnn_in['W_neigh1'], 'L1_gnn_W_pool': _L1_gnn_in['W_pool'], 'L1_gnn_b_pool': _L1_gnn_in['b_pool'], 'L1_gnn_W_self2': _L1_gnn_in['W_self2'], 'L1_gnn_W_neigh2': _L1_gnn_in['W_neigh2'], 'L1_gnn_g1': _L1_gnn_in['g1'], 'L1_gnn_beta1': _L1_gnn_in['beta1'], 'L1_gnn_g2': _L1_gnn_in['g2'], 'L1_gnn_beta2': _L1_gnn_in['beta2'], 'L2_gnn_weight': _L2_gnn_in['weight'], 'L2_gnn_bias': _L2_gnn_in['bias'], 'L3_gnn_W': _L3_gnn_in['W'], 'L3_gnn_bias': _L3_gnn_in['bias'], 'L3_gnn_gamma': _L3_gnn_in['gamma'], 'L3_gnn_beta': _L3_gnn_in['beta']}

def reference(x, src, dst, edge_attr_96, edge_weight, L0_gnn_Wq, L0_gnn_bq, L0_gnn_Wk, L0_gnn_bk, L0_gnn_We, L0_gnn_be, L0_gnn_Wv, L0_gnn_bv, L1_gnn_W_self1, L1_gnn_W_neigh1, L1_gnn_W_pool, L1_gnn_b_pool, L1_gnn_W_self2, L1_gnn_W_neigh2, L1_gnn_g1, L1_gnn_beta1, L1_gnn_g2, L1_gnn_beta2, L2_gnn_weight, L2_gnn_bias, L3_gnn_W, L3_gnn_bias, L3_gnn_gamma, L3_gnn_beta):
    import jax
    import jax.numpy as jnp

    def _L0_gnn_ref(x, edge_index, edge_attr, Wq, bq, Wk, bk, We, be, Wv, bv):
        import jax, jax.numpy as jnp
        import numpy as np
        N_NODES = 6250
        N_EDGES = 100000
        IN_DIM = 96
        NUM_HEADS = 8
        HEAD_DIM = IN_DIM // NUM_HEADS
        N = x.shape[0]
        H, D = (NUM_HEADS, HEAD_DIM)
        Q_h = (x @ Wq + bq).reshape(N, H, D)
        K_h = (x @ Wk + bk).reshape(N, H, D)
        V_h = (x @ Wv + bv).reshape(N, H, D)
        E = (edge_attr @ We + be).reshape(-1, H, D)
        src_idx = edge_index[0]
        dst_idx = edge_index[1]
        src = K_h[src_idx]
        dest = Q_h[dst_idx]
        score = src * dest / jnp.sqrt(jnp.asarray(D, x.dtype))
        score = score * E
        score = jnp.exp(jnp.clip(score.sum(-1, keepdims=True), -5.0, 5.0))
        msg = V_h[src_idx] * score
        wV = jax.ops.segment_sum(msg, dst_idx, num_segments=N)
        Z = jax.ops.segment_sum(score, dst_idx, num_segments=N)
        h_out = wV / (Z + 1e-06)
        return h_out.reshape(N, H * D)

    def _L1_gnn_ref(x, edge_index, W_self1, W_neigh1, W_pool, b_pool, W_self2, W_neigh2, g1, beta1, g2, beta2):
        import jax, jax.numpy as jnp
        import numpy as np
        N_NODES = 12500
        N_EDGES = 100000
        D = 96
        BN_EPS = 1e-05
        LEAKY_SLOPE = 0.01

        def _batch_norm(h, gamma, beta):
            mu = h.mean(axis=0)
            var = jnp.mean(jnp.square(h - mu), axis=0)
            return gamma * (h - mu) * jax.lax.rsqrt(var + BN_EPS) + beta

        def _forward(x, edge_index, W_self1, W_neigh1, W_pool, b_pool, W_self2, W_neigh2, g1, beta1, g2, beta2):
            src, dst = (edge_index[0], edge_index[1])
            n = x.shape[0]
            deg = jax.ops.segment_sum(jnp.ones((src.shape[0],), x.dtype), dst, num_segments=n)
            agg_sum = jax.ops.segment_sum(x[src], dst, num_segments=n)
            h_mean = agg_sum / jnp.maximum(deg, 1.0)[:, None]
            out1 = x @ W_self1 + h_mean @ W_neigh1
            out1 = _batch_norm(out1, g1, beta1)
            hp = jax.nn.relu(x @ W_pool + b_pool)
            agg_max = jax.ops.segment_max(hp[src], dst, num_segments=n)
            h_max = jnp.where(deg[:, None] > 0, agg_max, 0.0)
            out2 = x @ W_self2 + h_max @ W_neigh2
            out2 = _batch_norm(out2, g2, beta2)
            return jax.nn.leaky_relu(out1 + out2, negative_slope=LEAKY_SLOPE)
        return _forward(x, edge_index, W_self1, W_neigh1, W_pool, b_pool, W_self2, W_neigh2, g1, beta1, g2, beta2)

    def _L2_gnn_ref(feat, weight, bias, src, dst):
        import jax, jax.numpy as jnp
        import numpy as np
        N_NODES = 6250
        N_EDGES = 100000
        D_IN = 96
        D_OUT = 96
        N = feat.shape[0]
        ones = jnp.ones(src.shape[0], dtype=feat.dtype)
        out_deg = jax.ops.segment_sum(ones, src, num_segments=N)
        in_deg = jax.ops.segment_sum(ones, dst, num_segments=N)
        ci = jnp.clip(out_deg, 1.0, None) ** (-0.5)
        cj = jnp.clip(in_deg, 1.0, None) ** (-0.5)
        msg = feat[src] * ci[src, None]
        agg = jax.ops.segment_sum(msg, dst, num_segments=N) * cj[:, None]
        h = jnp.where(in_deg[:, None] > 0, agg, feat)
        return jnp.matmul(h, weight) + bias

    def _L3_gnn_ref(x, edge_index, edge_weight, W, bias, gamma, beta):
        import jax, jax.numpy as jnp
        import numpy as np
        LN_EPS = 1e-05
        N_NODES = 6250
        N_EDGES = 100000
        IN_DIM = 96
        OUT_DIM = 96
        h = x @ W
        src, dst = (edge_index[0], edge_index[1])
        msgs = h[src] * edge_weight[:, None]
        agg = jax.ops.segment_sum(msgs, dst, num_segments=x.shape[0])
        y = agg + bias
        mu = jnp.mean(y, axis=-1, keepdims=True)
        var = jnp.mean(jnp.square(y - mu), axis=-1, keepdims=True)
        y = (y - mu) * jax.lax.rsqrt(var + LN_EPS)
        return y * gamma + beta
    edge_index = jnp.stack([src, dst])
    x = _layernorm(x + _L0_gnn_ref(x, edge_index, edge_attr_96, L0_gnn_Wq, L0_gnn_bq, L0_gnn_Wk, L0_gnn_bk, L0_gnn_We, L0_gnn_be, L0_gnn_Wv, L0_gnn_bv), axis=-1)
    x = _layernorm(x + _L1_gnn_ref(x, edge_index, L1_gnn_W_self1, L1_gnn_W_neigh1, L1_gnn_W_pool, L1_gnn_b_pool, L1_gnn_W_self2, L1_gnn_W_neigh2, L1_gnn_g1, L1_gnn_beta1, L1_gnn_g2, L1_gnn_beta2), axis=-1)
    x = _layernorm(x + _L2_gnn_ref(x, L2_gnn_weight, L2_gnn_bias, src, dst), axis=-1)
    x = _layernorm(x + _L3_gnn_ref(x, edge_index, edge_weight, L3_gnn_W, L3_gnn_bias, L3_gnn_gamma, L3_gnn_beta), axis=-1)
    return x

_drawn_inputs = setup_inputs


def setup_inputs(seed=0):
    import zlib

    import numpy as np

    out = dict(_drawn_inputs(seed))
    spreads = {'L1_gnn_g1': (1.0, 0.2),
     'L1_gnn_beta1': (0.0, 0.1),
     'L1_gnn_g2': (1.0, 0.2),
     'L1_gnn_beta2': (0.0, 0.1),
     'L2_gnn_bias': (0.0, 0.1),
     'L3_gnn_bias': (0.0, 0.349),
     'L3_gnn_gamma': (1.0, 0.2),
     'L3_gnn_beta': (0.0, 0.1)}
    factors = {'L1_gnn_b_pool': 24.0}
    for name, (base, spread) in spreads.items():
        noise = np.random.default_rng([zlib.crc32(name.encode()), seed]).standard_normal(out[name].shape)
        drawn = base * np.exp(spread * noise) if base else spread * noise
        out[name] = jnp.asarray(drawn.astype(out[name].dtype))
    for name, factor in factors.items():
        out[name] = (out[name] * factor).astype(out[name].dtype)
    return out
```

```python
from contextlib import ExitStack

import concourse.bass as bass
from concourse import mybir

P = 128
TQ = 4
QE = TQ * P
GQ = 4
GT = GQ * TQ
CT = 5
CN = CT * P
CB = 2
HEADS = 8
RJ = 8
PARTS = 3
LN_EPS = 1e-5
BN_EPS = 1e-5
BN_DIM = 6

ALU = mybir.AluOpType
ACT = mybir.ActivationFunctionType
F32 = mybir.dt.float32
BF16 = mybir.dt.bfloat16
I32 = mybir.dt.int32
AX_X = mybir.AxisListType.X


def node_tiles(n):
    body = CT * CB * P
    return -(-(n + P) // body) * CT * CB


def edge_tiles(e):
    return -(-e // (P * GT)) * GT


class Signal:

    def __init__(self, sem, base):
        self.sem, self.base = sem, base


def wait(eng, signal, value):
    if not isinstance(value, int) or value > 0:
        eng.wait_ge(signal.sem, value + signal.base)


def groups(eng, body, n):
    body(0, n == 1)
    if n > 2:
        with eng.Fori(1, n - 1) as i:
            body(i, False)
    if n > 1:
        body(n - 1, True)


class Steps:

    def __init__(self, eng, signal, base, pin):
        self.eng, self.sem, self.base, self.n, self.pin = eng, signal.sem, base + signal.base, 0, pin

    def did(self, ins):
        ins.then_inc(self.sem, 1)
        self.n += 1

    def settle(self, pinned=False):
        self.eng.wait_ge(self.sem, self.base + self.n)
        if pinned:
            self.eng.sem_inc(self.pin, 1)


def gnn_kernel(nc, N, E, dims, a):
    F = dims["F"]
    NT, ET = node_tiles(N), edge_tiles(E)
    NP, EP = NT * P, ET * P
    NQ, NG = ET // TQ, ET // GT
    NCH, NB = NT // CT, NT // CT // CB
    RP = ET // RJ
    D = F // HEADS
    KV, AGG, PAIR = 2 * F, F + HEADS, 2 * F
    HALF = CN // 2
    assert RP <= P and F % 32 == 0 and F + 1 <= P and NG >= 3 and NB >= 3 and N + P <= NP

    ctx = ExitStack()
    with ctx:
        def sb(name, shape, dt=F32):
            return ctx.enter_context(nc.sbuf_tensor(name, shape, dt))

        def sem(name):
            return ctx.enter_context(nc.semaphore(name))

        def dram(name, shape, dt=F32):
            return nc.dram_tensor(name, shape, dt, kind="Internal").ap()

        kv_table = dram("kv_table", (NP, KV))
        q_table = dram("q_table", (NP, PARTS * F), BF16)
        pair_table = dram("pair_table", (NP, PAIR))
        ci_table = dram("ci_table", (NP, F))
        h_table = dram("h_table", (NP, F))
        sums = [dram(f"sums{n}", (EP, w)) for n, w in enumerate((AGG, PAIR, F, F))]
        rank_rows = dram("rank_rows", (NQ, QE), BF16)
        keep_rows = dram("keep_rows", (NQ, QE), BF16)
        carry_rows = dram("carry_rows", (NQ, QE))
        count_rows = dram("count_rows", (NP + P,))

        ident = sb("ident", [P, P])
        iota_row = sb("iota_row", [P, P], BF16)
        zeros = sb("zeros", [P, P], BF16)
        iota_col = sb("iota_col", [P, 1])
        node_id = sb("node_id", [P, NT])
        x_nodes = sb("x_nodes", [P, NT, F])
        rank_col = sb("rank_col", [P, ET])
        weight_col = sb("weight_col", [P, ET])
        src_all = sb("src_all", [P, ET], I32)
        src_lo = sb("src_lo", [P, ET])
        src_hi = sb("src_hi", [P, ET])
        first_f = sb("first_f", [P, ET])
        starts = sb("starts", [1, ET], I32)
        wide = sb("wide", [P, 2, NP])
        w_qkv = sb("w_qkv", [F + 1, 3 * F])
        w_e = sb("w_e", [F + 1, F])
        w_pool = sb("w_pool", [F + 1, F])
        w_s1 = sb("w_s1", [F, F])
        w_s2 = sb("w_s2", [F, F])
        w_n1 = sb("w_n1", [F, F])
        w_n2 = sb("w_n2", [F, F])
        w_2 = sb("w_2", [F + 1, F])
        w_3 = sb("w_3", [F, F])
        bn_par = sb("bn_par", [F, 4])
        row_par = sb("row_par", [P, 3, F])
        src_idx = sb("src_idx", [P, GQ, TQ], I32)
        rows = sb("rows", [P, GQ, TQ, KV])
        attr = sb("attr", [F + 1, GQ, QE])
        rank_row = sb("rank_row", [P, GQ, QE], BF16)
        keep_row = sb("keep_row", [F, GQ, QE], BF16)
        carry = sb("carry", [P, GQ, QE])
        q_win = sb("q_win", [P, GQ, TQ, PARTS * F], BF16)
        out_rows = sb("out_rows", [P, GQ, TQ, KV])
        pick = sb("pick", [P, 2, QE], BF16)
        same = sb("same", [P, 2, TQ, P])
        prod = sb("prod", [P, TQ, F])
        score = sb("score", [P, TQ, HEADS])
        msg = sb("msg", [P, 2, TQ, AGG])
        scanned = sb("scanned", [F, 2, QE])
        hot_lo = sb("hot_lo", [P, 2, TQ, P], BF16)
        hot_hi = sb("hot_hi", [P, 2, TQ, NT], BF16)
        node_idx = sb("node_idx", [P, CB, CT], I32)
        got = sb("got", [P, CB, CT, KV])
        table = sb("table", [P, CB, CT, KV])
        q_parts = [got[:, b].bitcast(BF16)[:, :, 0:PARTS * F] for b in range(CB)]
        z_inv = sb("z_inv", [P, CT, HEADS])
        h_a = sb("h_a", [P, CT, F])
        h_b = sb("h_b", [P, CT, F])
        x_new = sb("x_new", [P, CB, CT, F])
        stats = sb("stats", [P, CT, BN_DIM])
        mean_var = sb("mean_var", [P, CT, 2])
        dev = sb("dev", [P, CT])
        rdev = sb("rdev", [P, CT])
        h_cols = sb("h_cols", [F + 1, 2, CN])
        bn_stat = sb("bn_stat", [F, 2, NCH * 2, BN_DIM])
        bn_mv = sb("bn_mv", [F, 2, 2])
        bn_a = sb("bn_a", [F, 8])
        tiles_le = sb("tiles_le", [P, NT])
        tile_idx = sb("tile_idx", [P, NT], I32)
        inside = sb("inside", [P, NT])
        tile_dst = got[:, :, :, 0:P].bitcast(I32)
        junk = sb("junk", [P, max(ET, P)], BF16)
        count = sb("count", [P, NT])
        before = sb("before", [P, NT])
        degree = sb("degree", [P, 8, NT])
        last_edge = sb("last_edge", [P, 4, NT], I32)
        eps_z = sb("eps_z", [P, 1])
        has_in, no_in, r_mean, c_in, c_out, deg_in, tmp_a, tmp_b = (degree[:, n, :] for n in range(8))
        row_of_node = last_edge[:, 3, :]

        bank = [ctx.enter_context(nc.psum_tensor(f"bank{n}", [P, 512], F32)) for n in range(8)]

        W = RJ * P
        flat = wide[0:RP].rearrange("p a n -> p (a n)")
        edge_i = flat[:, 0:W].bitcast(I32)
        prev_i = flat[:, W:2 * W].bitcast(I32)
        carry_f = flat[:, W:2 * W]
        rank_f, new_f, hold_f, keep_f = (flat[:, m * W:(m + 1) * W] for m in range(2, 6))
        rank_b = flat[:, 6 * W:13 * W // 2].bitcast(BF16)
        keep_b = flat[:, 13 * W // 2:7 * W].bitcast(BF16)

        def quad(b, w):
            return b[:, 0:TQ * w].rearrange("p (j f) -> p j f", j=TQ)

        def five(b):
            return b[:, 0:CT * F].rearrange("p (j f) -> p j f", j=CT)

        made = sem("made")
        made_steps = sem("made_steps")
        ready = sem("ready")
        pin = sem("pin")
        held = sem("held")
        s_edges = sem("s_edges")
        s_first = sem("s_first")
        s_src = sem("s_src")
        s_weights = sem("s_weights")
        s_nodes = sem("s_nodes")
        prep = Signal(sem("prep"), 0)
        rows_out = sem("rows_out")
        turned = sem("turned")
        search = Signal(sem("search"), 0)
        counted = sem("counted")
        count_out = sem("count_out")
        count_back = sem("count_back")
        last_found = sem("last_found")
        ranked = sem("ranked")
        junk_free = Signal(sem("junk_free"), 0)
        src_step = sem("src_step")
        deg_step = Signal(sem("deg_step"), 0)
        deg_ready = sem("deg_ready")
        deg_root = sem("deg_root")
        deg_done = sem("deg_done")
        bn_step = Signal(sem("bn_step"), 0)
        bn_ready = sem("bn_ready")
        bn_root = sem("bn_root")

        sems = {}

        def shared(name, n, totals, slots=0):
            if name not in sems:
                sems[name] = [sem(f"{name}{b}" if slots else name) for b in range(max(slots, 1))]
            found = [Signal(x, sum(totals[:n])) for x in sems[name]]
            return found if slots else found[0]

        class Pass:

            def __init__(self, n):
                def each(name, total):
                    return shared(name, n, [total] * 4, GQ)

                self.idx_in = each("idx_in", NG * 16)
                self.rows_in = each("rows_in", NG * 16 * TQ)
                self.edge_in = each("edge_in", NG * 32)
                self.out = each("out", NG * 16)
                self.same_done = shared("same_done", n, [NQ] * 4)
                self.agg_done = shared("agg_done", n, [ET] * 4)
                self.copied = shared("copied", n, [ET] * 4)
                if n == 0:
                    self.attr_in = shared("attr_in", 0, [0], GQ)
                    self.win_in = shared("win_in", 0, [0], GQ)
                    self.pick_done = shared("pick_done", 0, [0])
                    self.e_done = shared("e_done", 0, [0])
                    self.q_done = shared("q_done", 0, [0])
                    self.prod_step = shared("prod_step", 0, [0])
                    self.prod_done = shared("prod_done", 0, [0])
                    self.score_step = shared("score_step", 0, [0])
                    self.clip_done = shared("clip_done", 0, [0])
                    self.exp_done = shared("exp_done", 0, [0])
                    self.msg_done = shared("msg_done", 0, [0])
                if n == 1:
                    self.keep_in = shared("keep_in", 0, [0], GQ)
                    self.turn_done = shared("turn_done", 0, [0])
                    self.scan_done = shared("scan_done", 0, [0])
                    self.back_done = shared("back_done", 0, [0])
                    self.max_copied = shared("max_copied", 0, [0])
                    self.hot_done = shared("hot_done", 0, [0])
                    self.hist_done = shared("hist_done", 0, [0])

        class Phase:

            def __init__(self, n):
                def two(name, total, steps):
                    return shared(name, n, [NB * total * m for m in steps], CB)

                def one(name, steps):
                    return shared(name, n, [NCH * m for m in steps])

                self.node_idx_in = two("node_idx_in", 16,         (1, 1, 1, 1, 0, 1, 1))
                self.got_in = two("got_in", 16 * CT,              (0, 1, 1, 1, 0, 1, 1))
                self.chunk_out = two("chunk_out", 16,             (2, 0, 1, 0, 1, 1, 1))
                self.dve = one("dve",                             (5, 0, 7, 0, 6, 6, 11))
                self.used = one("used",                           (1, 1, 1, 1, 1, 1, 1))
                self.x_done = one("x_done",                       (1, 0, 1, 1, 1, 1, 1))
                self.pe = one("pe",                               (1, 0, 2, 2, 1, 4, 0))
                self.act = one("act",                             (1, 0, 7, 1, 1, 4, 0))
                self.h_done = one("h_done",                       (0, 0, 0, 1, 1, 1, 0))
                self.var_done = one("var_done",                   (0, 0, 1, 0, 1, 1, 2))
                self.dev_done = one("dev_done",                   (0, 0, 1, 0, 1, 1, 2))

        passes = [Pass(n) for n in range(4)]
        phases = {name: Phase(n) for n, name in enumerate((0, "search", 1, 2, 3, 4, 5))}

        W_LOADS = 6 + 6 + 5 + 4 + 3
        PREP = 9
        SEARCH = 2
        ACT_STEPS = {1: 7, 4: 4}

        block = ctx.enter_context(nc.Block())

        def rows_of(t, c):
            return t.rearrange("(t p) w -> p t w", p=P)[:, bass.ds(c * CT, CT), :]

        def quad_rows(t, q):
            return t.rearrange("(q p j) w -> q p (j w)", p=P, j=TQ)[bass.ds(q, 1)].rearrange("o p w -> (o p) w")

        def edge_pass_sp(sp, n):
            s = passes[n]
            width = (AGG, PAIR, F, F)[n]

            def load_idx(q, k):
                sp.dma_start(src_idx[:, k, :], a["src_cols"][bass.ds(q, 1)].rearrange("o p t -> (o p) t")).then_inc(s.idx_in[k].sem, 16)

            def load_edges(q, k):
                sp.dma_start(rank_row[:, k, :], rank_rows[bass.ds(q, 1), :].to_broadcast([P, QE])).then_inc(s.edge_in[k].sem, 16)
                sp.dma_start(carry[P - 1:P, k, :], carry_rows[bass.ds(q, 1), :]).then_inc(s.edge_in[k].sem, 16)
                if n == 1:
                    sp.dma_start(keep_row[:, k, :], keep_rows[bass.ds(q, 1), :].to_broadcast([F, QE])).then_inc(s.keep_in[k].sem, 16)
                if n == 0:
                    sp.dma_start(attr[0:F, k, :], a["attr_cols"][:, bass.ds(q * QE, QE)]).then_inc(s.attr_in[k].sem, 16)
                    for j in range(TQ):
                        start = sp.value_load(starts[0:1, bass.ds(q * TQ + j, 1)], min_val=0, max_val=NP - P)
                        sp.dma_start(q_win[:, k, j, :], q_table[bass.ds(start, P), :]).then_inc(s.win_in[k].sem, 16)

            if n == 0:
                sp.wait_ge(s_first, 32)
                sp.wait_ge(rows_out, 48)
                for b in range(CB):
                    wait(sp, phases[0].chunk_out[b], 32 * NB)
            for k in range(GQ):
                load_idx(k, k)
                load_edges(k, k)

            def body(i, last):
                for k in range(GQ):
                    q = i * GQ + k
                    if not last:
                        wait(sp, s.rows_in[k], (i + 1) * 16 * TQ)
                        load_idx(q + GQ, k)
                    wait(sp, s.copied, (q + 1) * TQ)
                    if n == 1:
                        wait(sp, s.max_copied, q + 1)
                    sp.dma_start(quad_rows(sums[n], q), out_rows[:, k, :, 0:width]).then_inc(s.out[k].sem, 16)
                    if not last:
                        load_edges(q + GQ, k)

            groups(sp, body, NG)

        def count_sp(sp):
            with nc.allow_non_contiguous_dma(reason="6400 counts, once"):
                sp.wait_ge(counted, 1)
                sp.dma_start(count_rows[1:1 + NP].rearrange("(t p o) -> p t o", p=P, o=1), count[:].rearrange("p (t o) -> p t o", o=1)).then_inc(count_out, 16)
                sp.dma_start(count_rows[0:1].rearrange("(o e) -> o e", o=1), carry[0:1, 0, 0:1]).then_inc(count_out, 16)
                sp.wait_ge(count_out, 32)
                sp.dma_start(before[:].rearrange("p (t o) -> p t o", o=1), count_rows[0:NP].rearrange("(t p o) -> p t o", p=P, o=1)).then_inc(count_back, 16)
            sp.wait_ge(last_found, 1)

        def node_phase_sp(sp, n, index, out_table, width):
            ph = phases[n]

            def load(c, b):
                sp.dma_start(node_idx[:, b, :], index[:, bass.ds(c * CT, CT)]).then_inc(ph.node_idx_in[b].sem, 16)

            if index is not None:
                for b in range(CB):
                    load(b, b)

            def body(i, last):
                for b in range(CB):
                    c = i * CB + b
                    if index is not None and not last:
                        wait(sp, ph.got_in[b], (i + 1) * 16 * CT)
                        load(c + CB, b)
                    if out_table is not None:
                        wait(sp, ph.x_done, c + 1)
                        if n in (1, 4):
                            wait(sp, ph.act, (c + 1) * ACT_STEPS[n])
                        dst = out_table[:, bass.ds(c * CT, CT), :] if n == 5 else rows_of(out_table, c)
                        sp.dma_start(dst, table[:, b, :, 0:width]).then_inc(ph.chunk_out[b].sem, 16)

            if index is not None or out_table is not None:
                groups(sp, body, NB)

        @block.sync
        def _(sp):
            sp.dma_start(edge_i, a["dst_tiles"].rearrange("(p j) e -> p (j e)", j=RJ)).then_inc(s_edges, 16)
            sp.dma_start(prev_i, a["dst_before"].rearrange("(p j) e -> p (j e)", j=RJ)).then_inc(s_edges, 16)
            F1 = F + 1
            n = 0
            for m, (w, b) in enumerate((("L0_gnn_Wq", "L0_gnn_bq"), ("L0_gnn_Wk", "L0_gnn_bk"),
                                        ("L0_gnn_Wv", "L0_gnn_bv"))):
                sp.dma_start(w_qkv[0:F, m * F:(m + 1) * F], a[w]).then_inc(s_weights, 16)
                sp.dma_start(w_qkv[F:F1, m * F:(m + 1) * F], a[b].rearrange("(o f) -> o f", o=1)).then_inc(s_weights, 16)
                n += 2
            for t, w, b in ((w_e, "L0_gnn_We", "L0_gnn_be"), (w_pool, "L1_gnn_W_pool", "L1_gnn_b_pool"),
                            (w_2, "L2_gnn_weight", "L2_gnn_bias"), (w_s1, "L1_gnn_W_self1", None),
                            (w_s2, "L1_gnn_W_self2", None), (w_n1, "L1_gnn_W_neigh1", None),
                            (w_n2, "L1_gnn_W_neigh2", None), (w_3, "L3_gnn_W", None)):
                sp.dma_start(t[0:F, :], a[w]).then_inc(s_weights, 16)
                n += 1
                if b:
                    sp.dma_start(t[F:F1, :], a[b].rearrange("(o f) -> o f", o=1)).then_inc(s_weights, 16)
                    n += 1
            for m, v in enumerate(("L1_gnn_g1", "L1_gnn_g2", "L1_gnn_beta1", "L1_gnn_beta2")):
                sp.dma_start(bn_par[:, m:m + 1], a[v].rearrange("(f o) -> f o", o=1)).then_inc(s_weights, 16)
                n += 1
            for m, v in enumerate(("L3_gnn_bias", "L3_gnn_gamma", "L3_gnn_beta")):
                sp.dma_start(row_par[:, m, :], a[v].rearrange("(o f) -> o f", o=1).to_broadcast([P, F])).then_inc(s_weights, 16)
                n += 1
            assert n == W_LOADS

            ph = phases[0]

            def load_x(c, b):
                sp.dma_start(h_cols[0:F, b, :], a["x_cols"][:, bass.ds(c * CN, CN)]).then_inc(ph.node_idx_in[b].sem, 16)

            for b in range(CB):
                load_x(b, b)
            sp.dma_start(first_f[:].bitcast(I32), a["tile_first"].to_broadcast([P, ET])).then_inc(s_first, 16)
            sp.dma_start(starts[:], a["tile_first"]).then_inc(s_first, 16)
            sp.dma_start(src_all[:].rearrange("p (g t) -> p g t", t=TQ), a["src_cols"].rearrange("g p t -> p g t")).then_inc(s_src, 16)
            sp.dma_start(weight_col[:], a["weight_cols"]).then_inc(s_src, 16)
            sp.dma_start(x_nodes[:], a["x_nodes"]).then_inc(s_nodes, 16)
            wait(sp, prep, PREP)
            for t, s in ((rank_rows, rank_b), (keep_rows, keep_b), (carry_rows, carry_f)):
                sp.dma_start(t.rearrange("q (o e) -> (q o) e", o=1).rearrange("(p r) e -> p (r e)", p=RP), s).then_inc(rows_out, 16)

            def qkv_out(i, last):
                for b in range(CB):
                    c = i * CB + b
                    wait(sp, ph.x_done, c + 1)
                    wait(sp, ph.act, c + 1)
                    if not last:
                        load_x(c + CB, b)
                    sp.dma_start(rows_of(q_table, c), q_parts[b]).then_inc(ph.chunk_out[b].sem, 16)
                    sp.dma_start(rows_of(kv_table, c), table[:, b]).then_inc(ph.chunk_out[b].sem, 16)

            groups(sp, qkv_out, NB)

            edge_pass_sp(sp, 0)
            node_phase_sp(sp, "search", tile_idx, None, P)
            count_sp(sp)
            node_phase_sp(sp, 1, row_of_node, pair_table, PAIR)
            edge_pass_sp(sp, 1)
            node_phase_sp(sp, 2, row_of_node, None, PAIR)
            node_phase_sp(sp, 3, None, ci_table, F)
            edge_pass_sp(sp, 2)
            node_phase_sp(sp, 4, row_of_node, h_table, F)
            edge_pass_sp(sp, 3)
            node_phase_sp(sp, 5, row_of_node, a["out"], F)
            for b in range(CB):
                wait(sp, phases[5].chunk_out[b], 16 * NB)

        def gather(pool, out, src, idx, done):
            pool.indirect_dma_start(out, None, src, bass.IndirectOffsetOnAxis(ap=idx, axis=0)).then_inc(done, 16)

        def edge_pass_pool(pool, n):
            s = passes[n]
            src = (kv_table, pair_table, ci_table, h_table)[n]
            width = (KV, PAIR, F, F)[n]
            ph = phases[(0, 1, 3, 4)[n]]

            def quad_gather(k):
                for j in range(TQ):
                    gather(pool, rows[:, k, j, 0:width], src, src_idx[:, k, j:j + 1], s.rows_in[k].sem)

            for b in range(CB):
                wait(pool, ph.chunk_out[b], (32 if n == 0 else 16) * NB)
            for k in range(GQ):
                wait(pool, s.idx_in[k], 16)
                quad_gather(k)

            def body(i, last):
                for k in range(GQ):
                    wait(pool, s.idx_in[k], (i + 2) * 16)
                    if n == 0:
                        wait(pool, s.msg_done, i * GQ + k + 1)
                    else:
                        wait(pool, s.agg_done, (i * GQ + k + 1) * TQ)
                    pool.sem_inc(held, 1)
                    quad_gather(k)

            groups(pool, body, NG - 1)

        def node_phase_pool(pool, n, width):
            ph = phases[n]
            if n == "search":
                src, to = a["dst_tiles"], tile_dst
            else:
                at = {1: 0, 2: 1, 4: 2, 5: 3}[n]
                src, to = sums[at], got
                for k in range(GQ):
                    wait(pool, passes[at].out[k], 16 * NG)

            def body(i, last):
                for b in range(CB):
                    wait(pool, ph.node_idx_in[b], (i + 1) * 16)
                    wait(pool, ph.used, i * CB + b - 1)
                    pool.sem_inc(held, 1)
                    for t in range(CT):
                        gather(pool, to[:, b, t, 0:width], src, node_idx[:, b, t:t + 1], ph.got_in[b].sem)

            groups(pool, body, NB)

        @block.gpsimd
        def _(pool):
            pool.memset(ident[:], 0.0).then_inc(made_steps, 1)
            pool.wait_ge(made_steps, 1)
            pool.affine_select(out=ident[:], in_=ident[:], compare_op=ALU.not_equal, fill=1.0, base=0,
                               pattern=[[-1, P]], channel_multiplier=1).then_inc(made, 1)
            pool.iota(iota_row[:], [[1, P]], base=0, channel_multiplier=0, allow_small_or_imprecise_dtypes=True).then_inc(made, 1)
            pool.iota(iota_col[:], [[0, 1]], base=0, channel_multiplier=1, allow_small_or_imprecise_dtypes=True).then_inc(made, 1)
            pool.iota(node_id[:], [[P, NT]], base=0, channel_multiplier=1, allow_small_or_imprecise_dtypes=True).then_inc(made, 1)

            edge_pass_pool(pool, 0)
            wait(pool, search, SEARCH)

            node_phase_pool(pool, "search", P)
            node_phase_pool(pool, 1, AGG)
            edge_pass_pool(pool, 1)
            node_phase_pool(pool, 2, PAIR)
            edge_pass_pool(pool, 2)
            node_phase_pool(pool, 4, F)
            edge_pass_pool(pool, 3)
            node_phase_pool(pool, 5, F)


        @block.tensor
        def _(pe):
            pe.wait_ge(s_weights, 16 * W_LOADS)
            pe.wait_ge(made, 4)
            pe.wait_ge(ready, 6)
            ph = phases[0]

            def qkv(i, last):
                for b in range(CB):
                    c = i * CB + b
                    wait(pe, ph.node_idx_in[b], (i + 1) * 16)
                    wait(pe, ph.act, c)
                    for t in range(CT):
                        mm = pe.matmul(bank[t][:, 0:3 * F], h_cols[:, b, t * P:(t + 1) * P], w_qkv[:], start=True, stop=True)
                    mm.then_inc(ph.pe.sem, 1)

            groups(pe, qkv, NB)
            wait(pe, prep, PREP)
            for j in range(RJ):
                tr = pe.transpose(bank[5 + j // 4][:, (j % 4) * P:(j % 4) * P + RP], rank_f[:, j * P:(j + 1) * P], ident[0:RP, 0:RP])
            tr.then_inc(turned, 1)

            def aggregate(s, q, i, k, n):
                width = AGG if n == 0 else F
                wait(pe, s.same_done, q + 1)
                if n == 0:
                    wait(pe, s.msg_done, q + 1)
                wait(pe, s.edge_in[k], (i + 1) * 32)
                for j in range(TQ):
                    acc = bank[4 + j % 2][:, 0:width]
                    wait(pe, s.copied, q * TQ + j - 1)
                    values = msg[:, k % 2, j, :] if n == 0 else rows[:, k, j, 0:F]
                    pe.matmul(acc, same[:, k % 2, j, :], values, start=True, stop=False)
                    wait(pe, s.copied, q * TQ + j)
                    pk, pj = (k, j - 1) if j else ((k - 1) % GQ, TQ - 1)
                    pe.matmul(acc, carry[:, k, j * P:(j + 1) * P], out_rows[:, pk, pj, 0:width],
                              start=False, stop=True).then_inc(s.agg_done.sem, 1)

            s0 = passes[0]

            def attention(i, last):
                for k in range(GQ):
                    q = i * GQ + k
                    wait(pe, s0.attr_in[k], (i + 1) * 16)
                    wait(pe, s0.prod_done, q - 1)
                    for j in range(TQ):
                        mm = pe.matmul(quad(bank[k % 2], F)[:, j, :], attr[:, k, j * P:(j + 1) * P], w_e[:], start=True, stop=True)
                    mm.then_inc(s0.e_done.sem, 1)
                    wait(pe, s0.pick_done, q + 1)
                    wait(pe, s0.win_in[k], (i + 1) * 16 * TQ)
                    for j in range(TQ):
                        for m in range(PARTS):
                            mm = pe.matmul(quad(bank[2 + k % 2], F)[:, j, :], pick[:, k % 2, j * P:(j + 1) * P],
                                           q_win[:, k, j, m * F:(m + 1) * F], start=(m == 0), stop=(m == PARTS - 1))
                    mm.then_inc(s0.q_done.sem, 1)
                    if not isinstance(q, int) or q > 0:
                        aggregate(s0, q - 1, i if k else i - 1, (k - 1) % GQ, 0)

            groups(pe, attention, NG)
            aggregate(s0, NQ - 1, NG - 1, GQ - 1, 0)

            def turn(b0, src, ph_sem=None):
                for t in range(CT):
                    tr = pe.transpose(bank[b0 + t // 4][0:F, (t % 4) * P:(t % 4 + 1) * P], src[:, t, :], ident[:])
                return tr

            ph = phases[1]

            def nodes1(i, last):
                for b in range(CB):
                    c = i * CB + b
                    wait(pe, ph.x_done, c + 1)
                    wait(pe, ph.act, c * 7)
                    turn(0, x_new[:, b]).then_inc(ph.pe.sem, 1)
                    wait(pe, ph.act, c * 7 + 2)
                    for t in range(CT):
                        pe.matmul(five(bank[2])[:, t, :], h_cols[:, 0, t * P:(t + 1) * P], w_pool[:], start=True, stop=True)
                    for m, w in enumerate((w_s1, w_s2)):
                        for h in range(2):
                            mm = pe.matmul(bank[3 + 2 * m + h][0:F, 0:HALF], w[:], h_cols[0:F, 0, h * HALF:(h + 1) * HALF], start=True, stop=True)
                    mm.then_inc(ph.pe.sem, 1)

            groups(pe, nodes1, NB)

            s1 = passes[1]
            hist = bank[7][:, 0:NT]
            pe.matmul(hist, zeros[:], iota_row[:, 0:NT], start=True, stop=False, skip_group_check=True)

            def sage(i, last):
                for k in range(GQ):
                    q = i * GQ + k
                    wait(pe, s1.rows_in[k], (i + 1) * 16 * TQ)
                    wait(pe, s1.scan_done, q - 1)
                    for j in range(TQ):
                        tr = pe.transpose(bank[k % 2][0:F, j * P:(j + 1) * P], rows[:, k, j, F:PAIR], ident[:])
                    tr.then_inc(s1.turn_done.sem, 1)
                    aggregate(s1, q, i, k, 1)
                    wait(pe, s1.hot_done, q + 1)
                    for j in range(TQ):
                        mm = pe.matmul(hist, hot_lo[:, k % 2, j, :], hot_hi[:, k % 2, j, :], start=False, stop=False, skip_group_check=True)
                    mm.then_inc(s1.hist_done.sem, 1)
                    wait(pe, s1.scan_done, q + 1)
                    wait(pe, s1.max_copied, q - 1)
                    for j in range(TQ):
                        tr = pe.transpose(quad(bank[2 + k % 2], F)[:, j, :], scanned[:, k % 2, j * P:(j + 1) * P], ident[0:F, 0:F])
                    tr.then_inc(s1.back_done.sem, 1)

            groups(pe, sage, NG)

            ph = phases[2]

            def nodes2(i, last):
                for b in range(CB):
                    c = i * CB + b
                    wait(pe, ph.h_done, c + 1)
                    wait(pe, ph.act, c)
                    turn(0, h_a)
                    turn(2, h_b).then_inc(ph.pe.sem, 1)
                    wait(pe, ph.act, c + 1)
                    wait(pe, ph.x_done, c)
                    for m, w in enumerate((w_n1, w_n2)):
                        for h in range(2):
                            mm = pe.matmul(bank[4 + 2 * m + h][0:F, 0:HALF], w[:], h_cols[0:F, m, h * HALF:(h + 1) * HALF], start=True, stop=True)
                    mm.then_inc(ph.pe.sem, 1)

            pe.wait_ge(deg_done, 1)
            groups(pe, nodes2, NB)

            ph = phases[3]

            def nodes3(i, last):
                for b in range(CB):
                    c = i * CB + b
                    wait(pe, ph.h_done, c + 1)
                    wait(pe, ph.used, c)
                    for t in range(CT):
                        tr = pe.transpose(five(bank[0])[:, t, :], h_cols[0:F, 0, t * P:(t + 1) * P], ident[0:F, 0:F])
                    tr.then_inc(ph.pe.sem, 1)

            groups(pe, nodes3, NB)

            def plain(n):
                s = passes[n]

                def body(i, last):
                    for k in range(GQ):
                        wait(pe, s.rows_in[k], (i + 1) * 16 * TQ)
                        aggregate(s, i * GQ + k, i, k, n)

                groups(pe, body, NG)

            plain(2)

            ph = phases[4]

            def nodes4(i, last):
                for b in range(CB):
                    c = i * CB + b
                    wait(pe, ph.h_done, c + 1)
                    wait(pe, ph.act, c * 4)
                    turn(0, h_a).then_inc(ph.pe.sem, 1)
                    wait(pe, ph.act, c * 4 + 1)
                    for t in range(CT):
                        mm = pe.matmul(five(bank[2])[:, t, :], h_cols[:, 0, t * P:(t + 1) * P], w_2[:], start=True, stop=True)
                    mm.then_inc(ph.pe.sem, 1)
                    wait(pe, ph.x_done, c + 1)
                    turn(4, x_new[:, b]).then_inc(ph.pe.sem, 1)
                    wait(pe, ph.act, c * 4 + 3)
                    for t in range(CT):
                        mm = pe.matmul(five(bank[3])[:, t, :], h_cols[0:F, 1, t * P:(t + 1) * P], w_3[:], start=True, stop=True)
                    mm.then_inc(ph.pe.sem, 1)

            groups(pe, nodes4, NB)
            plain(3)

        @block.scalar
        def _(act):
            ph = phases[0]

            def qkv(i, last):
                for b in range(CB):
                    c = i * CB + b
                    wait(act, ph.pe, c + 1)
                    wait(act, ph.used, c)
                    wait(act, ph.chunk_out[b], i * 32)
                    for t in range(CT):
                        act.mul(h_a[:, t, :], bank[t][:, 0:F], float(D) ** -0.5)
                    for t in range(CT):
                        cp = act.copy(table[:, b, t, :], bank[t][:, F:3 * F])
                    cp.then_inc(ph.act.sem, 1)

            groups(act, qkv, NB)

            def copy_tile(s, q, i, k, j, width):
                wait(act, s.agg_done, q * TQ + j + 1)
                if j == 0:
                    wait(act, s.out[k], i * 16)
                act.copy(out_rows[:, k, j, 0:width], bank[4 + j % 2][:, 0:width]).then_inc(s.copied.sem, 1)

            s0 = passes[0]

            def attention(i, last):
                for k in range(GQ):
                    q = i * GQ + k
                    behind = not isinstance(q, int) or q > 0
                    pk, pi = (k - 1) % GQ, (i if k else i - 1)
                    if behind:
                        copy_tile(s0, q - 1, pi, pk, 0, AGG)
                        copy_tile(s0, q - 1, pi, pk, 1, AGG)
                    wait(act, s0.clip_done, q + 1)
                    wait(act, s0.msg_done, q - 1)
                    act.activation(quad(bank[6], HEADS * 2)[:, :, (k % 2) * HEADS:(k % 2 + 1) * HEADS], score[:], ACT.Exp)
                    act.activation(msg[:, k % 2, :, F:AGG], score[:], ACT.Exp).then_inc(s0.exp_done.sem, 1)
                    if behind:
                        copy_tile(s0, q - 1, pi, pk, 2, AGG)
                        copy_tile(s0, q - 1, pi, pk, 3, AGG)

            groups(act, attention, NG)
            for j in range(TQ):
                copy_tile(s0, NQ - 1, NG - 1, GQ - 1, j, AGG)

            def root(ph, c):
                wait(act, ph.var_done, c)
                act.activation(dev[:], mean_var[:, :, 1], ACT.Sqrt, bias=eps_z[:, 0:1]).then_inc(ph.dev_done.sem, 1)

            def columns(b0, dst, m):
                act.copy(dst[0:F, m, 0:4 * P], bank[b0][0:F, :])
                return act.copy(dst[0:F, m, 4 * P:CN], bank[b0 + 1][0:F, 0:P])

            act.wait_ge(deg_ready, 1)
            act.activation(tmp_b, tmp_a, ACT.Sqrt).then_inc(deg_root, 1)

            ph = phases[1]

            def nodes1(i, last):
                for b in range(CB):
                    c = i * CB + b
                    root(ph, c + 1)
                    wait(act, ph.x_done, c + 1)
                    wait(act, ph.chunk_out[b], i * 16)
                    act.copy(x_nodes[:, bass.ds(c * CT, CT), :], x_new[:, b]).then_inc(ph.act.sem, 1)
                    wait(act, ph.pe, c * 2 + 1)
                    columns(0, h_cols, 0).then_inc(ph.act.sem, 1)
                    act.copy(table[:, b, :, 0:F], x_new[:, b])
                    wait(act, ph.pe, c * 2 + 2)
                    act.activation(table[:, b, :, F:PAIR], five(bank[2]), ACT.Relu).then_inc(ph.act.sem, 1)
                    for m in range(2):
                        for h in range(2):
                            act.copy(wide[0:F, m, bass.ds(c * CN + h * HALF, HALF)], bank[3 + 2 * m + h][0:F, 0:HALF]).then_inc(ph.act.sem, 1)

            groups(act, nodes1, NB)

            def plain(n):
                s = passes[n]

                def body(i, last):
                    for k in range(GQ):
                        q = i * GQ + k
                        for j in range(TQ):
                            copy_tile(s, q, i, k, j, F)
                        if n == 1:
                            wait(act, s.back_done, q + 1)
                            act.copy(out_rows[:, k, :, F:PAIR], quad(bank[2 + k % 2], F)).then_inc(s.max_copied.sem, 1)

                groups(act, body, NG)

            plain(1)
            act.wait_ge(deg_ready, 2)
            act.activation(tmp_b, tmp_a, ACT.Sqrt).then_inc(deg_root, 1)

            ph = phases[2]

            def nodes2(i, last):
                for b in range(CB):
                    c = i * CB + b
                    wait(act, ph.pe, c * 2 + 1)
                    columns(0, h_cols, 0)
                    columns(2, h_cols, 1).then_inc(ph.act.sem, 1)

            groups(act, nodes2, NB)
            act.wait_ge(bn_ready, 1)
            act.activation(bn_a[:, 0:2], bn_mv[:, :, 1], ACT.Sqrt, bias=eps_z[0:F, 0:1]).then_inc(bn_root, 1)

            ph = phases[3]

            def nodes3(i, last):
                for b in range(CB):
                    c = i * CB + b
                    root(ph, c + 1)
                    wait(act, ph.x_done, c + 1)
                    act.copy(x_nodes[:, bass.ds(c * CT, CT), :], x_new[:, b]).then_inc(ph.act.sem, 1)

            groups(act, nodes3, NB)
            plain(2)

            ph = phases[4]

            def nodes4(i, last):
                for b in range(CB):
                    c = i * CB + b
                    wait(act, ph.pe, c * 4 + 1)
                    columns(0, h_cols, 0).then_inc(ph.act.sem, 1)
                    root(ph, c + 1)
                    wait(act, ph.x_done, c + 1)
                    act.copy(x_nodes[:, bass.ds(c * CT, CT), :], x_new[:, b]).then_inc(ph.act.sem, 1)
                    wait(act, ph.pe, c * 4 + 3)
                    columns(4, h_cols, 1).then_inc(ph.act.sem, 1)
                    wait(act, ph.pe, c * 4 + 4)
                    wait(act, ph.chunk_out[b], i * 16)
                    act.copy(table[:, b, :, 0:F], five(bank[3])).then_inc(ph.act.sem, 1)

            groups(act, nodes4, NB)
            plain(3)

            ph = phases[5]

            def nodes5(i, last):
                for b in range(CB):
                    for m in range(2):
                        root(ph, (i * CB + b) * 2 + m + 1)

            groups(act, nodes5, NB)

        @block.vector
        def _(dve):
            dve.memset(carry[:], 0.0).then_inc(ready, 1)
            dve.memset(out_rows[:, GQ - 1, :, :], 0.0).then_inc(ready, 1)
            dve.memset(eps_z[:], LN_EPS).then_inc(ready, 1)
            dve.memset(zeros[:], 0.0).then_inc(ready, 1)
            dve.memset(attr[F:F + 1, :, :], 1.0).then_inc(ready, 1)
            dve.memset(h_cols[F:F + 1, :, :], 1.0).then_inc(ready, 1)
            dve.wait_ge(ready, 6)
            dve.wait_ge(made, 4)
            dve.sem_inc(pin, 1)


            def tiled(t):
                return t.rearrange("p (j e) -> p j e", j=RJ)

            st = Steps(dve, prep, 0, pin)
            dve.wait_ge(s_edges, 32)
            st.did(dve.tensor_tensor(keep_f, edge_i, prev_i, ALU.is_equal))
            st.did(dve.tensor_tensor(new_f, edge_i, prev_i, ALU.not_equal))
            st.did(dve.memset(hold_f, 1.0))
            st.settle()
            st.did(dve.memset(tiled(hold_f)[:, :, 0:1], 0.0))
            st.did(dve.memset(tiled(new_f)[:, :, 0:1], 0.0))
            st.settle()
            st.did(dve.tensor_tensor_scan(rank_f, hold_f, new_f, 0.0, ALU.mult, ALU.add))
            st.did(dve.tensor_copy(keep_b, keep_f))
            st.settle()
            st.did(dve.tensor_copy(rank_b, rank_f))
            st.did(dve.scalar_tensor_tensor(out=tiled(carry_f), in0=tiled(rank_f), scalar=0.0,
                                            in1=tiled(keep_f)[:, :, 0:1].to_broadcast([RP, RJ, P]),
                                            op0=ALU.is_equal, op1=ALU.mult))
            assert st.n == PREP

            ph = phases[0]

            def split(i, last):
                for b in range(CB):
                    c = i * CB + b
                    st = Steps(dve, ph.dve, c * 5, pin)
                    wait(dve, ph.act, c + 1)
                    wait(dve, ph.chunk_out[b], i * 32)
                    part = [q_parts[b][:, :, m * F:(m + 1) * F] for m in range(PARTS)]
                    st.did(dve.tensor_copy(part[0], h_a[:]))
                    st.settle()
                    st.did(dve.tensor_tensor(h_b[:], h_a[:], part[0], ALU.subtract))
                    st.settle()
                    st.did(dve.tensor_copy(part[1], h_b[:]))
                    st.settle()
                    st.did(dve.tensor_tensor(h_b[:], h_b[:], part[1], ALU.subtract))
                    st.settle()
                    st.did(dve.tensor_copy(part[2], h_b[:]))
                    st.settle()
                    dve.sem_inc(ph.used.sem, 1)
                    dve.sem_inc(ph.x_done.sem, 1)

            groups(dve, split, NB)

            dve.wait_ge(turned, 1)
            by_j = rank_col[:].rearrange("p (r j) -> p j r", j=RJ)
            for j in range(RJ):
                cp = dve.tensor_copy(by_j[:, j, :], bank[5 + j // 4][:, (j % 4) * P:(j % 4) * P + RP])
            cp.then_inc(ranked, 1)

            dve.wait_ge(s_first, 32)
            dve.tensor_copy(first_f[:], first_f[:].bitcast(I32)).then_inc(ranked, 1)
            dve.wait_ge(ranked, 2)

            def count_tiles(i, last):
                for t in range(CT * CB):
                    at = i * CT * CB + t
                    wait(dve, junk_free, at)
                    dve.tensor_scalar(junk[:, 0:ET], first_f[:], node_id[:, bass.ds(at, 1)], None, ALU.is_le, ALU.add,
                                      accum_out=tiles_le[:, bass.ds(at, 1)]).then_inc(junk_free.sem, 1)

            groups(dve, count_tiles, NB)
            st = Steps(dve, search, 0, pin)
            wait(dve, junk_free, NT)
            st.did(dve.tensor_scalar(tiles_le[:], tiles_le[:], -1.0, 0.0, ALU.add, ALU.max))
            st.settle()
            st.did(dve.tensor_copy(tile_idx[:], tiles_le[:]))
            dve.wait_ge(s_src, 32)
            dve.tensor_scalar(src_lo[:].bitcast(I32), src_all[:], P - 1, None, ALU.bitwise_and).then_inc(src_step, 1)
            dve.tensor_scalar(src_hi[:].bitcast(I32), src_all[:], 7, None, ALU.arith_shift_right).then_inc(src_step, 1)
            dve.wait_ge(src_step, 2)
            dve.tensor_copy(src_lo[:], src_lo[:].bitcast(I32)).then_inc(src_step, 1)
            dve.tensor_copy(src_hi[:], src_hi[:].bitcast(I32)).then_inc(src_step, 1)
            dve.wait_ge(src_step, 4)
            st.settle()
            assert st.n == SEARCH

            def same_runs(s, q, i, k, n):
                wait(dve, s.agg_done, (q - 1) * TQ)
                for j in range(TQ):
                    at = bass.ds(q * TQ + j, 1)
                    mine, theirs = rank_col[:, at], rank_row[:, k, j * P:(j + 1) * P]
                    if n == 3:
                        ins = dve.tensor_scalar(same[:, k % 2, j, :], theirs, mine, weight_col[:, at], ALU.is_equal, ALU.mult)
                    else:
                        ins = dve.tensor_scalar(same[:, k % 2, j, :], theirs, mine, None, ALU.is_equal)
                ins.then_inc(s.same_done.sem, 1)

            s0 = passes[0]

            def attention(i, last):
                for k in range(GQ):
                    q = i * GQ + k
                    wait(dve, s0.edge_in[k], (i + 1) * 32)
                    dve.tensor_scalar(pick[:, k % 2, :], rank_row[:, k, :], iota_col[:, 0:1], None, ALU.is_equal).then_inc(s0.pick_done.sem, 1)
                    wait(dve, s0.rows_in[k], (i + 1) * 16 * TQ)
                    wait(dve, s0.q_done, q + 1)
                    dve.tensor_tensor(prod[:], quad(bank[2 + k % 2], F), rows[:, k, :, 0:F], ALU.mult).then_inc(s0.prod_step.sem, 1)
                    wait(dve, s0.prod_step, q + 1)
                    dve.tensor_tensor(prod[:], quad(bank[k % 2], F), prod[:], ALU.mult).then_inc(s0.prod_done.sem, 1)
                    wait(dve, s0.prod_done, q + 1)
                    dve.tensor_reduce(score[:], prod[:].rearrange("p j (h d) -> p j h d", h=HEADS), AX_X, ALU.add).then_inc(s0.score_step.sem, 1)
                    wait(dve, s0.score_step, q + 1)
                    dve.tensor_scalar(score[:], score[:], 5.0, -5.0, ALU.min, ALU.max).then_inc(s0.clip_done.sem, 1)
                    same_runs(s0, q, i, k, 0)
                    wait(dve, s0.exp_done, q + 1)
                    dve.tensor_tensor(msg[:, k % 2, :, 0:F].rearrange("p j (h d) -> p j h d", h=HEADS),
                                      rows[:, k, :, F:KV].rearrange("p j (h d) -> p j h d", h=HEADS),
                                      quad(bank[6], HEADS * 2)[:, :, (k % 2) * HEADS:(k % 2 + 1) * HEADS]
                                      .rearrange("p j (h o) -> p j h o", o=1).to_broadcast([P, TQ, HEADS, D]),
                                      ALU.mult).then_inc(s0.msg_done.sem, 1)

            groups(dve, attention, NG)

            ph = phases["search"]

            def count_inside(i, last):
                for b in range(CB):
                    wait(dve, ph.got_in[b], (i + 1) * 16 * CT)
                    for t in range(CT):
                        at = (i * CB + b) * CT + t
                        wait(dve, junk_free, NT + at)
                        dve.tensor_scalar(junk[:, 0:P], tile_dst[:, b, t, :], node_id[:, bass.ds(at, 1)], None, ALU.is_le, ALU.add,
                                          accum_out=inside[:, bass.ds(at, 1)]).then_inc(junk_free.sem, 1)
                    wait(dve, junk_free, NT + (i * CB + b + 1) * CT)
                    dve.sem_inc(ph.used.sem, 1)

            groups(dve, count_inside, NB)
            wait(dve, junk_free, 2 * NT)
            dve.scalar_tensor_tensor(out=count[:], in0=tiles_le[:], scalar=float(P), in1=inside[:], op0=ALU.mult, op1=ALU.add).then_inc(counted, 1)
            dve.wait_ge(counted, 1)
            st = Steps(dve, deg_step, 0, pin)
            e_i, part_i, tile_i, row_i = (last_edge[:, m, :] for m in range(4))
            st.did(dve.tensor_scalar(tmp_a, count[:], -1.0, 0.0, ALU.add, ALU.max))
            st.settle()
            st.did(dve.tensor_copy(e_i, tmp_a))
            st.settle()
            st.did(dve.tensor_scalar(part_i, e_i, P - 1, TQ.bit_length() - 1, ALU.bitwise_and, ALU.logical_shift_left))
            st.did(dve.tensor_scalar(tile_i, e_i, P.bit_length() - 1, TQ - 1, ALU.logical_shift_right, ALU.bitwise_and))
            st.settle()
            st.did(dve.tensor_tensor(part_i, part_i, tile_i, ALU.bitwise_or))
            st.did(dve.tensor_scalar(e_i, e_i, QE.bit_length() - 1, QE.bit_length() - 1, ALU.logical_shift_right, ALU.logical_shift_left))
            st.settle()
            st.did(dve.tensor_tensor(row_i, part_i, e_i, ALU.bitwise_or))
            dve.wait_ge(count_back, 16)
            st.did(dve.tensor_tensor(deg_in, count[:], before[:], ALU.subtract))
            st.settle()
            st.did(dve.tensor_scalar(has_in, deg_in, 0.0, None, ALU.is_gt))
            st.did(dve.tensor_scalar(no_in, deg_in, 0.0, None, ALU.is_le))
            st.did(dve.tensor_scalar(tmp_a, deg_in, 1.0, None, ALU.max))
            st.settle()
            st.did(dve.reciprocal(r_mean, tmp_a))
            dve.sem_inc(deg_ready, 1)
            st.settle()
            st.did(dve.tensor_tensor(r_mean, r_mean, has_in, ALU.mult))
            dve.wait_ge(deg_root, 1)
            st.did(dve.reciprocal(c_in, tmp_b))
            st.settle()
            st.did(dve.tensor_tensor(c_in, c_in, has_in, ALU.mult))
            st.settle()
            dve.sem_inc(last_found, 1)

            def per_tile(t, c):
                return t[:, bass.ds(c * CT, CT)].rearrange("p (t o) -> p t o", o=1).to_broadcast([P, CT, F])

            def layer_norm(st, ph, out, src, rounds):
                for t in range(CT):
                    ins = dve.bn_stats(stats[:, t, :], src[:, t, :])
                st.did(ins)
                st.settle(True)
                for t in range(CT):
                    ins = dve.bn_aggr(mean_var[:, t, :], stats[:, t, :])
                st.did(ins)
                st.settle()
                dve.sem_inc(ph.var_done.sem, 1)
                wait(dve, ph.dev_done, rounds)
                st.did(dve.reciprocal(rdev[:], dev[:]))
                st.settle()
                for t in range(CT):
                    ins = dve.tensor_scalar(out[:, t, :], src[:, t, :], mean_var[:, t, 0:1], rdev[:, t:t + 1], ALU.subtract, ALU.mult)
                return ins

            ph = phases[1]

            def nodes1(i, last):
                for b in range(CB):
                    c = i * CB + b
                    st = Steps(dve, ph.dve, c * 7, pin)
                    wait(dve, ph.got_in[b], (i + 1) * 16 * CT)
                    st.did(dve.tensor_scalar(z_inv[:], got[:, b, :, F:AGG], 1e-6, None, ALU.add))
                    st.settle()
                    st.did(dve.reciprocal(z_inv[:], z_inv[:]))
                    st.settle()
                    st.did(dve.tensor_tensor(z_inv[:], z_inv[:], per_tile(has_in, c)[:, :, 0:HEADS], ALU.mult))
                    st.settle()
                    st.did(dve.tensor_tensor(h_a[:].rearrange("p t (h d) -> p t h d", h=HEADS),
                                             got[:, b, :, 0:F].rearrange("p t (h d) -> p t h d", h=HEADS),
                                             z_inv[:].rearrange("p t (h o) -> p t h o", o=1).to_broadcast([P, CT, HEADS, D]), ALU.mult))
                    st.settle()
                    dve.tensor_tensor(h_b[:], h_a[:], x_nodes[:, bass.ds(c * CT, CT), :], ALU.add).then_inc(ph.used.sem, 1)
                    wait(dve, ph.used, c + 1)
                    wait(dve, ph.act, (c - 1) * 7)
                    layer_norm(st, ph, x_new[:, b], h_b, c + 1).then_inc(ph.x_done.sem, 1)
                    assert st.n == 7

            dve.wait_ge(s_nodes, 16)
            groups(dve, lambda i, last: nodes1(i, last), NB)

            s1 = passes[1]

            def sage(i, last):
                for k in range(GQ):
                    q = i * GQ + k
                    wait(dve, s1.edge_in[k], (i + 1) * 32)
                    wait(dve, s1.keep_in[k], (i + 1) * 16)
                    same_runs(s1, q, i, k, 1)
                    wait(dve, s1.turn_done, q + 1)
                    wait(dve, s1.scan_done, q)
                    wait(dve, s1.back_done, q - 1)
                    first = isinstance(q, int) and q == 0
                    dve.tensor_tensor_scan(scanned[:, k % 2, :], keep_row[:, k, :], bank[k % 2][0:F, :],
                                           0.0 if first else scanned[:, (k - 1) % 2, QE - 1:QE],
                                           ALU.mult, ALU.max).then_inc(s1.scan_done.sem, 1)
                    wait(dve, s1.hist_done, q - 1)
                    for j in range(TQ):
                        at = bass.ds(q * TQ + j, 1)
                        dve.tensor_scalar(hot_lo[:, k % 2, j, :], iota_row[:], src_lo[:, at], None, ALU.is_equal)
                        ins = dve.tensor_scalar(hot_hi[:, k % 2, j, :], iota_row[:, 0:NT], src_hi[:, at], None, ALU.is_equal)
                    ins.then_inc(s1.hot_done.sem, 1)

            groups(dve, sage, NG)
            wait(dve, s1.hist_done, NQ)
            dve.tensor_scalar(tmp_a, bank[7][:, 0:NT], 1.0, None, ALU.max).then_inc(deg_ready, 1)
            dve.wait_ge(deg_ready, 2)
            dve.sem_inc(deg_done, 1)
            dve.wait_ge(deg_root, 2)
            dve.reciprocal(c_out, tmp_b).then_inc(deg_done, 1)

            ph = phases[2]

            def nodes2(i, last):
                for b in range(CB):
                    c = i * CB + b
                    wait(dve, ph.got_in[b], (i + 1) * 16 * CT)
                    wait(dve, ph.pe, (c - 1) * 2 + 1)
                    dve.tensor_tensor(h_a[:], got[:, b, :, 0:F], per_tile(r_mean, c), ALU.mult)
                    dve.tensor_tensor(h_b[:], got[:, b, :, F:PAIR], per_tile(has_in, c), ALU.mult).then_inc(ph.h_done.sem, 1)
                    wait(dve, ph.h_done, c + 1)
                    dve.sem_inc(ph.used.sem, 1)
                    wait(dve, ph.pe, c * 2 + 2)
                    for m in range(2):
                        for h in range(2):
                            part = wide[0:F, m, bass.ds(c * CN + h * HALF, HALF)]
                            ins = dve.tensor_tensor(part, bank[4 + 2 * m + h][0:F, 0:HALF], part, ALU.add)
                    ins.then_inc(ph.x_done.sem, 1)
                    wait(dve, ph.x_done, c + 1)
                    for m in range(2):
                        for h in range(2):
                            valid = min(HALF, N - (c * CN + h * HALF)) if last else HALF
                            if valid > 0:
                                ins = dve.bn_stats(bn_stat[:, m, bass.ds(c * 2 + h, 1), :].rearrange("p o s -> p (o s)"),
                                                   wide[0:F, m, bass.ds(c * CN + h * HALF, valid)])
                    if last:
                        ins.then_inc(bn_step.sem, 1)

            groups(dve, nodes2, NB)
            halves = -(-N // HALF)
            st = Steps(dve, bn_step, CB, pin)
            st.settle()
            for m in range(2):
                ins = dve.bn_aggr(bn_mv[:, m, :], bn_stat[:, m, 0:halves, :].rearrange("p c s -> p (c s)"))
            st.did(ins)
            st.settle()
            dve.sem_inc(bn_ready, 1)
            dve.wait_ge(bn_root, 1)
            st.did(dve.reciprocal(bn_a[:, 2:4], bn_a[:, 0:2]))
            st.settle()
            st.did(dve.tensor_tensor(bn_a[:, 2:4], bn_a[:, 2:4], bn_par[:, 0:2], ALU.mult))
            st.settle()
            st.did(dve.tensor_tensor(bn_a[:, 4:6], bn_mv[:, :, 0], bn_a[:, 2:4], ALU.mult))
            st.settle()
            st.did(dve.tensor_tensor(bn_a[:, 4:6], bn_par[:, 2:4], bn_a[:, 4:6], ALU.subtract))
            st.settle()
            st.did(dve.tensor_tensor(bn_a[:, 6:7], bn_a[:, 4:5], bn_a[:, 5:6], ALU.add))
            st.settle()

            ph = phases[3]

            def nodes3(i, last):
                for b in range(CB):
                    c = i * CB + b
                    st = Steps(dve, ph.dve, c * 6, pin)
                    cols = h_cols[0:F, 0, :]
                    wait(dve, ph.pe, c)
                    st.did(dve.tensor_scalar(cols, wide[0:F, 0, bass.ds(c * CN, CN)], bn_a[:, 2:3], bn_a[:, 6:7], ALU.mult, ALU.add))
                    st.settle()
                    st.did(dve.scalar_tensor_tensor(out=cols, in0=wide[0:F, 1, bass.ds(c * CN, CN)], scalar=bn_a[:, 3:4], in1=cols, op0=ALU.mult, op1=ALU.add))
                    st.settle()
                    dve.scalar_tensor_tensor(out=cols, in0=cols, scalar=0.01, in1=cols, op0=ALU.mult, op1=ALU.max).then_inc(ph.h_done.sem, 1)
                    wait(dve, ph.pe, c + 1)
                    dve.tensor_tensor(h_b[:], five(bank[0]), x_nodes[:, bass.ds(c * CT, CT), :], ALU.add).then_inc(ph.used.sem, 1)
                    wait(dve, ph.used, c + 1)
                    wait(dve, ph.act, c - 1)
                    st.did(layer_norm(st, ph, x_new[:, b], h_b, c + 1))
                    st.settle()
                    wait(dve, ph.chunk_out[b], i * 16)
                    dve.tensor_tensor(table[:, b, :, 0:F], x_new[:, b], per_tile(c_out, c), ALU.mult).then_inc(ph.x_done.sem, 1)
                    assert st.n == 6

            dve.wait_ge(deg_done, 2)
            groups(dve, nodes3, NB)

            def plain(n):
                s = passes[n]

                def body(i, last):
                    for k in range(GQ):
                        wait(dve, s.edge_in[k], (i + 1) * 32)
                        same_runs(s, i * GQ + k, i, k, n)

                groups(dve, body, NG)

            plain(2)

            ph = phases[4]

            def nodes4(i, last):
                for b in range(CB):
                    c = i * CB + b
                    st = Steps(dve, ph.dve, c * 6, pin)
                    wait(dve, ph.got_in[b], (i + 1) * 16 * CT)
                    wait(dve, ph.pe, (c - 1) * 4 + 1)
                    wait(dve, ph.x_done, c)
                    here = x_nodes[:, bass.ds(c * CT, CT), :]
                    st.did(dve.tensor_tensor(h_b[:], got[:, b, :, 0:F], per_tile(c_in, c), ALU.mult))
                    st.did(dve.tensor_tensor(h_a[:], here, per_tile(no_in, c), ALU.mult))
                    st.settle()
                    dve.tensor_tensor(h_a[:], h_a[:], h_b[:], ALU.add).then_inc(ph.h_done.sem, 1)
                    wait(dve, ph.h_done, c + 1)
                    dve.sem_inc(ph.used.sem, 1)
                    wait(dve, ph.pe, c * 4 + 2)
                    st.did(dve.tensor_tensor(h_b[:], five(bank[2]), here, ALU.add))
                    st.settle()
                    wait(dve, ph.act, (c - 1) * 4)
                    layer_norm(st, ph, x_new[:, b], h_b, c + 1).then_inc(ph.x_done.sem, 1)
                    assert st.n == 6

            groups(dve, nodes4, NB)
            plain(3)

            ph = phases[5]

            def over_tiles(m):
                return row_par[:, m:m + 1, :].to_broadcast([P, CT, F])

            def nodes5(i, last):
                for b in range(CB):
                    c = i * CB + b
                    st = Steps(dve, ph.dve, c * 11, pin)
                    wait(dve, ph.x_done, c)
                    wait(dve, ph.got_in[b], (i + 1) * 16 * CT)
                    st.did(dve.tensor_tensor(h_a[:], got[:, b, :, 0:F], per_tile(has_in, c), ALU.mult))
                    st.settle()
                    dve.tensor_tensor(h_a[:], h_a[:], over_tiles(0), ALU.add).then_inc(ph.used.sem, 1)
                    wait(dve, ph.used, c + 1)
                    st.did(layer_norm(st, ph, h_b, h_a, c * 2 + 1))
                    st.settle()
                    st.did(dve.tensor_tensor(h_b[:], h_b[:], over_tiles(1), ALU.mult))
                    st.settle()
                    st.did(dve.tensor_tensor(h_b[:], h_b[:], over_tiles(2), ALU.add))
                    st.settle()
                    st.did(dve.tensor_tensor(h_a[:], h_b[:], x_nodes[:, bass.ds(c * CT, CT), :], ALU.add))
                    st.settle()
                    wait(dve, ph.chunk_out[b], i * 16)
                    layer_norm(st, ph, table[:, b, :, 0:F], h_a, c * 2 + 2).then_inc(ph.x_done.sem, 1)
                    assert st.n == 11

            groups(dve, nodes5, NB)


_WEIGHTS = ['L0_gnn_Wq', 'L0_gnn_bq', 'L0_gnn_Wk', 'L0_gnn_bk', 'L0_gnn_We', 'L0_gnn_be', 'L0_gnn_Wv', 'L0_gnn_bv',
            'L1_gnn_W_self1', 'L1_gnn_W_neigh1', 'L1_gnn_W_pool', 'L1_gnn_b_pool', 'L1_gnn_W_self2',
            'L1_gnn_W_neigh2', 'L1_gnn_g1', 'L1_gnn_beta1', 'L1_gnn_g2', 'L1_gnn_beta2', 'L2_gnn_weight',
            'L2_gnn_bias', 'L3_gnn_W', 'L3_gnn_bias', 'L3_gnn_gamma', 'L3_gnn_beta']


def laid_out(inputs):
    import numpy as np

    x = np.asarray(inputs["x"])
    src, dst = np.asarray(inputs["src"]), np.asarray(inputs["dst"])
    attr, weight = np.asarray(inputs["edge_attr_96"]), np.asarray(inputs["edge_weight"])
    n, f = x.shape
    e = src.shape[0]
    nt, et = node_tiles(n), edge_tiles(e)

    def padded(v, rows, value):
        out = np.full((rows,) + v.shape[1:], value, v.dtype)
        out[:v.shape[0]] = v
        return out

    xp = padded(x, nt * P, 0)
    dp = padded(dst, et * P, n)
    before = np.full((et * P,), -1, dst.dtype)
    before[1:] = dp[:-1]
    tiles = dp.reshape(et, P)
    return n, e, f, {
        "x_nodes": np.ascontiguousarray(xp.reshape(nt, P, f).transpose(1, 0, 2)),
        "x_cols": np.ascontiguousarray(xp.T),
        "dst_tiles": tiles,
        "dst_before": before.reshape(et, P),
        "tile_first": np.ascontiguousarray(tiles[:, 0]).reshape(1, et),
        "src_cols": np.ascontiguousarray(padded(src, et * P, n).reshape(et // TQ, TQ, P).transpose(0, 2, 1)),
        "weight_cols": np.ascontiguousarray(padded(weight, et * P, 0).reshape(et, P).T),
        "attr_cols": np.ascontiguousarray(padded(attr, et * P, 0).T),
        **{name: np.ascontiguousarray(inputs[name]) for name in _WEIGHTS},
    }


def kernel(**inputs):
    import concourse.bacc as _bacc
    from concourse.bass_utils import run_bass_kernel_spmd as _run

    nc = _bacc.Bacc("TRN2", target_bir_lowering=False, num_devices=1)
    n, e, f, arrays = laid_out(inputs)
    args = {name: nc.dram_tensor("in_" + name, v.shape, mybir.dt.from_np(v.dtype), kind="ExternalInput").ap()
            for name, v in arrays.items()}
    nt = node_tiles(n)
    args["out"] = nc.dram_tensor("out", (P, nt, f), F32, kind="ExternalOutput").ap()
    gnn_kernel(nc, n, e, {"F": f}, args)
    got = _run(nc, [{"in_" + name: v for name, v in arrays.items()}], core_ids=[0]).results[0]["out"]
    return got.transpose(1, 0, 2).reshape(nt * P, f)[:n]
```

```python
from contextlib import ExitStack

import concourse.bass as bass
from concourse import mybir

P = 128
TQ = 4
QE = TQ * P
GQ = 4
GP = GQ // 2
GT = GQ * TQ
CT = 5
CN = CT * P
CB = 2
HEADS = 8
RJ = 8
PARTS = 3
LN_EPS = 1e-5
BN_EPS = 1e-5
BN_DIM = 6

ALU = mybir.AluOpType
ACT = mybir.ActivationFunctionType
F32 = mybir.dt.float32
BF16 = mybir.dt.bfloat16
I32 = mybir.dt.int32
AX_X = mybir.AxisListType.X


def node_tiles(n):
    body = CT * CB * P
    return -(-(n + P) // body) * CT * CB


def edge_tiles(e):
    return -(-e // (P * GT)) * GT


class Signal:

    def __init__(self, sem, base):
        self.sem, self.base = sem, base


def wait(eng, signal, value):
    if not isinstance(value, int) or value > 0:
        eng.wait_ge(signal.sem, value + signal.base)


def groups(eng, body, n):
    body(0, n == 1)
    if n > 2:
        with eng.Fori(1, n - 1) as i:
            body(i, False)
    if n > 1:
        body(n - 1, True)


class Steps:

    def __init__(self, eng, signal, base, pin):
        self.eng, self.sem, self.base, self.n, self.pin = eng, signal.sem, base + signal.base, 0, pin

    def did(self, ins):
        ins.then_inc(self.sem, 1)
        self.n += 1

    def settle(self, pinned=False):
        self.eng.wait_ge(self.sem, self.base + self.n)
        if pinned:
            self.eng.sem_inc(self.pin, 1)


def gnn_kernel(nc, N, E, dims, a):
    F = dims["F"]
    NT, ET = node_tiles(N), edge_tiles(E)
    NP, EP = NT * P, ET * P
    NQ, NG = ET // TQ, ET // GT
    NCH, NB = NT // CT, NT // CT // CB
    RP = ET // RJ
    D = F // HEADS
    KV, AGG, PAIR = 2 * F, F + HEADS, 2 * F
    HALF = CN // 2
    assert RP <= P and F % 32 == 0 and F + 1 <= P and NG >= 3 and NB >= 3 and N + P <= NP

    ctx = ExitStack()
    with ctx:
        def sb(name, shape, dt=F32):
            return ctx.enter_context(nc.sbuf_tensor(name, shape, dt))

        def sem(name):
            return ctx.enter_context(nc.semaphore(name))

        def dram(name, shape, dt=F32):
            return nc.dram_tensor(name, shape, dt, kind="Internal").ap()

        kv_table = dram("kv_table", (NP, KV))
        q_table = dram("q_table", (NP, PARTS * F), BF16)
        pair_table = dram("pair_table", (NP, PAIR))
        ci_table = dram("ci_table", (NP, F))
        h_table = dram("h_table", (NP, F))
        sums = [dram(f"sums{n}", (EP, w)) for n, w in enumerate((AGG, PAIR, F, F))]
        rank_rows = dram("rank_rows", (NQ, QE), BF16)
        keep_rows = dram("keep_rows", (NQ, QE), BF16)
        carry_rows = dram("carry_rows", (NQ, QE))

        ident = sb("ident", [P, P])
        iota_row = sb("iota_row", [P, P], BF16)
        zeros = sb("zeros", [P, P], BF16)
        upto = sb("upto", [P, P])
        ones = sb("ones", [P, P])
        iota_col = sb("iota_col", [P, 1])
        x_nodes = sb("x_nodes", [P, NT, F])
        rank_col = sb("rank_col", [P, ET])
        weight_col = sb("weight_col", [P, ET])
        src_lo = sb("src_lo", [P, ET])
        src_hi = sb("src_hi", [P, ET])
        dst_lo = sb("dst_lo", [P, ET])
        dst_hi = sb("dst_hi", [P, ET])
        starts = sb("starts", [1, ET], I32)
        wide = sb("wide", [P, 2, NP])
        w_qkv = sb("w_qkv", [F + 1, 3 * F])
        w_e = sb("w_e", [F + 1, F])
        w_pool = sb("w_pool", [F + 1, F])
        w_s1 = sb("w_s1", [F, F])
        w_s2 = sb("w_s2", [F, F])
        w_n1 = sb("w_n1", [F, F])
        w_n2 = sb("w_n2", [F, F])
        w_2 = sb("w_2", [F + 1, F])
        w_3 = sb("w_3", [F, F])
        bn_par = sb("bn_par", [F, 4])
        row_par = sb("row_par", [P, 3, F])
        src_idx = sb("src_idx", [P, GQ, TQ], I32)
        rows = sb("rows", [P, GQ, TQ, KV])
        attr = sb("attr", [F + 1, GQ, QE])
        rank_row = sb("rank_row", [P, GQ, QE], BF16)
        keep_row = sb("keep_row", [F, GQ, QE], BF16)
        carry = sb("carry", [P, GQ, QE])
        q_win = sb("q_win", [P, GQ, TQ, PARTS * F], BF16)
        out_rows = sb("out_rows", [P, GQ, TQ, KV])
        pick = sb("pick", [P, 2, QE], BF16)
        same = sb("same", [P, 2, TQ, P])
        prod = sb("prod", [P, TQ, F])
        score = sb("score", [P, TQ, HEADS])
        msg = sb("msg", [P, 2, TQ, AGG])
        scanned = sb("scanned", [F, 2, QE])
        hot_lo = sb("hot_lo", [P, 2, TQ, P], BF16)
        hot_hi = sb("hot_hi", [P, 2, TQ, NT], BF16)
        node_idx = sb("node_idx", [P, CB, CT], I32)
        got = sb("got", [P, CB, CT, KV])
        table = sb("table", [P, CB, CT, KV])
        q_parts = [got[:, b].bitcast(BF16)[:, :, 0:PARTS * F] for b in range(CB)]
        z_inv = sb("z_inv", [P, CT, HEADS])
        h_a = sb("h_a", [P, CT, F])
        h_b = sb("h_b", [P, CT, F])
        x_new = sb("x_new", [P, CB, CT, F])
        stats = sb("stats", [P, CT, BN_DIM])
        mean_var = sb("mean_var", [P, CT, 2])
        dev = sb("dev", [P, CT])
        rdev = sb("rdev", [P, CT])
        h_cols = sb("h_cols", [F + 1, 2, CN])
        bn_stat = sb("bn_stat", [F, 2, NCH * 2, BN_DIM])
        bn_mv = sb("bn_mv", [F, 2, 2])
        bn_a = sb("bn_a", [F, 8])
        count = sb("count", [P, NT])
        running = sb("running", [P, NT])
        degree = sb("degree", [P, 8, NT])
        last_edge = sb("last_edge", [P, 4, NT], I32)
        eps_z = sb("eps_z", [P, 1])
        has_in, no_in, r_mean, c_in, c_out, deg_in, tmp_a, tmp_b = (degree[:, n, :] for n in range(8))
        row_of_node = last_edge[:, 3, :]

        bank = [ctx.enter_context(nc.psum_tensor(f"bank{n}", [P, 512], F32)) for n in range(8)]

        W = RJ * P
        flat = wide[0:RP].rearrange("p a n -> p (a n)")
        edge_i = flat[:, 0:W].bitcast(I32)
        prev_i = flat[:, W:2 * W].bitcast(I32)
        carry_f = flat[:, W:2 * W]
        rank_f, new_f, hold_f, keep_f = (flat[:, m * W:(m + 1) * W] for m in range(2, 6))
        rank_b = flat[:, 6 * W:13 * W // 2].bitcast(BF16)
        keep_b = flat[:, 13 * W // 2:7 * W].bitcast(BF16)

        def quad(b, w):
            return b[:, 0:TQ * w].rearrange("p (j f) -> p j f", j=TQ)

        def five(b):
            return b[:, 0:CT * F].rearrange("p (j f) -> p j f", j=CT)

        made = sem("made")
        made_steps = sem("made_steps")
        ready = sem("ready")
        pin = sem("pin")
        held = sem("held")
        held_sp = sem("held_sp")
        s_edges = sem("s_edges")
        s_first = sem("s_first")
        s_src = sem("s_src")
        s_weights = sem("s_weights")
        s_nodes = sem("s_nodes")
        prep = Signal(sem("prep"), 0)
        rows_out = sem("rows_out")
        turned = sem("turned")
        last_found = sem("last_found")
        ranked = sem("ranked")
        deg_sums = sem("deg_sums")
        src_step = sem("src_step")
        deg_step = Signal(sem("deg_step"), 0)
        deg_ready = sem("deg_ready")
        deg_root = sem("deg_root")
        deg_done = sem("deg_done")
        bn_step = Signal(sem("bn_step"), 0)
        bn_ready = sem("bn_ready")
        bn_root = sem("bn_root")

        sems = {}

        def shared(name, n, totals, slots=0):
            if name not in sems:
                sems[name] = [sem(f"{name}{b}" if slots else name) for b in range(max(slots, 1))]
            found = [Signal(x, sum(totals[:n])) for x in sems[name]]
            return found if slots else found[0]

        class Pass:

            def __init__(self, n):
                def each(name, total):
                    return shared(name, n, [total] * 4, GQ)

                def pairs(name, total):
                    return shared(name, n, [total] * 4, GP)

                self.idx_in = pairs("idx_in", NG * 16)
                self.rows_in = each("rows_in", NG * 16 * TQ)
                self.rank_in = pairs("rank_in", NG * 16)
                self.carry_in = pairs("carry_in", NG * 16)
                self.out = pairs("out", NG * 16)
                self.same_done = shared("same_done", n, [NQ] * 4)
                self.agg_done = shared("agg_done", n, [ET] * 4)
                self.copied = shared("copied", n, [ET] * 4)
                self.hot_done = shared("hot_done", n, [NQ] * 4)
                self.hist_done = shared("hist_done", n, [NQ] * 4)
                if n == 0:
                    self.attr_in = shared("attr_in", 0, [0], GP)
                    self.win_in = shared("win_in", 0, [0], GQ)
                    self.pick_done = shared("pick_done", 0, [0])
                    self.q_done = shared("q_done", 0, [0])
                    self.prod_step = shared("prod_step", 0, [0])
                    self.prod_done = shared("prod_done", 0, [0])
                    self.score_step = shared("score_step", 0, [0])
                    self.clip_done = shared("clip_done", 0, [0])
                    self.exp_done = shared("exp_done", 0, [0])
                    self.msg_done = shared("msg_done", 0, [0])
                if n == 1:
                    self.keep_in = shared("keep_in", 0, [0], GP)
                    self.turn_done = shared("turn_done", 0, [0])
                    self.scan_done = shared("scan_done", 0, [0])
                    self.back_done = shared("back_done", 0, [0])
                    self.max_copied = shared("max_copied", 0, [0])

        class Phase:

            def __init__(self, n):
                def two(name, total, steps):
                    return shared(name, n, [NB * total * m for m in steps], CB)

                def one(name, steps):
                    return shared(name, n, [NCH * m for m in steps])

                self.node_idx_in = two("node_idx_in", 16,         (1, 1, 1, 0, 1, 1))
                self.got_in = two("got_in", 16 * CT,              (0, 1, 1, 0, 1, 1))
                self.chunk_out = two("chunk_out", 16,             (2, 1, 0, 1, 1, 1))
                self.dve = one("dve",                             (5, 7, 0, 6, 6, 11))
                self.used = one("used",                           (1, 1, 1, 1, 1, 1))
                self.x_done = one("x_done",                       (1, 1, 1, 1, 1, 1))
                self.pe = one("pe",                               (1, 2, 2, 1, 4, 0))
                self.act = one("act",                             (1, 7, 1, 1, 4, 0))
                self.h_done = one("h_done",                       (0, 0, 1, 1, 1, 0))
                self.var_done = one("var_done",                   (0, 1, 0, 1, 1, 2))
                self.dev_done = one("dev_done",                   (0, 1, 0, 1, 1, 2))

        passes = [Pass(n) for n in range(4)]
        phases = {name: Phase(n) for n, name in enumerate(range(6))}

        W_LOADS = 6 + 6 + 5 + 4 + 3
        PREP = 9
        WIN_SP = 3
        ACT_STEPS = {1: 7, 4: 4}

        block = ctx.enter_context(nc.Block())

        def rows_of(t, c):
            return t.rearrange("(t p) w -> p t w", p=P)[:, bass.ds(c * CT, CT), :]

        def pair_rows(t, g):
            return t.rearrange("(g p j) w -> g p (j w)", p=P, j=2 * TQ)[bass.ds(g, 1)].rearrange("o p w -> (o p) w")

        def pair_row(t, g):
            return t.rearrange("(g h) e -> g (h e)", h=2)[bass.ds(g, 1), :]

        def load_window(eng, q, k, j):
            start = eng.value_load(starts[0:1, bass.ds(q * TQ + j, 1)], min_val=0, max_val=NP - P)
            eng.dma_start(q_win[:, k, j, :], q_table[bass.ds(start, P), :]).then_inc(passes[0].win_in[k].sem, 16)

        def edge_pass_sp(sp, n):
            s = passes[n]
            width = (AGG, PAIR, F, F)[n]

            def load_idx(g, h):
                sp.dma_start(src_idx[:, 2 * h:2 * h + 2, :], a["src_cols"][bass.ds(g * 2, 2)].rearrange("q p t -> p q t")).then_inc(s.idx_in[h].sem, 16)

            def load_rank(g, h):
                sp.dma_start(rank_row[:, 2 * h:2 * h + 2, :], pair_row(rank_rows, g).to_broadcast([P, 2 * QE])).then_inc(s.rank_in[h].sem, 16)

            def load_carry(g, h):
                sp.dma_start(carry[P - 1:P, 2 * h:2 * h + 2, :], pair_row(carry_rows, g)).then_inc(s.carry_in[h].sem, 16)

            def load_keep(g, h):
                sp.dma_start(keep_row[:, 2 * h:2 * h + 2, :], pair_row(keep_rows, g).to_broadcast([F, 2 * QE])).then_inc(s.keep_in[h].sem, 16)

            def load_attr(g, h):
                sp.dma_start(attr[0:F, 2 * h:2 * h + 2, :], a["attr_cols"][:, bass.ds(g * (2 * QE), 2 * QE)]).then_inc(s.attr_in[h].sem, 16)

            def load_windows(g, h, m, windows):
                for j in range(windows):
                    load_window(sp, g * 2 + m, 2 * h + m, j)

            if n == 0:
                sp.wait_ge(s_first, 16)
                sp.wait_ge(rows_out, 48)
                for b in range(CB):
                    wait(sp, phases[0].chunk_out[b], 32 * NB)
            for h in range(GP):
                load_idx(h, h)
            for h in range(GP):
                load_rank(h, h)
                load_carry(h, h)
                if n == 0:
                    load_attr(h, h)
                    for m in range(2):
                        load_windows(h, h, m, TQ)
                if n == 1:
                    load_keep(h, h)

            def body(i, last):
                for h in range(GP):
                    g = i * GP + h
                    if not last:
                        for m in range(2):
                            wait(sp, s.rows_in[2 * h + m], (i + 1) * 16 * TQ)
                        load_idx(g + GP, h)
                        if n == 0:
                            wait(sp, s.q_done, (g + 1) * 2)
                            sp.sem_inc(held_sp, 1)
                            load_attr(g + GP, h)
                            load_windows(g + GP, h, 0, WIN_SP)
                        wait(sp, s.same_done, (g + 1) * 2)
                        sp.sem_inc(held_sp, 1)
                        load_rank(g + GP, h)
                        if n == 0:
                            load_windows(g + GP, h, 1, WIN_SP)
                        if n == 1:
                            wait(sp, s.scan_done, (g + 1) * 2)
                            sp.sem_inc(held_sp, 1)
                            load_keep(g + GP, h)
                    wait(sp, s.copied, (g + 1) * 2 * TQ)
                    if not last:
                        sp.sem_inc(held_sp, 1)
                        load_carry(g + GP, h)
                    if n == 1:
                        wait(sp, s.max_copied, (g + 1) * 2)
                    sp.dma_start(pair_rows(sums[n], g), out_rows[:, 2 * h:2 * h + 2, :, 0:width].rearrange("p k j w -> p (k j) w")).then_inc(s.out[h].sem, 16)

            groups(sp, body, NG)

        def node_phase_sp(sp, n, index, out_table, width):
            ph = phases[n]

            def load(c, b):
                sp.dma_start(node_idx[:, b, :], index[:, bass.ds(c * CT, CT)]).then_inc(ph.node_idx_in[b].sem, 16)

            if index is not None:
                for b in range(CB):
                    load(b, b)

            def body(i, last):
                for b in range(CB):
                    c = i * CB + b
                    if index is not None and not last:
                        wait(sp, ph.got_in[b], (i + 1) * 16 * CT)
                        load(c + CB, b)
                    if out_table is not None:
                        wait(sp, ph.x_done, c + 1)
                        if n in (1, 4):
                            wait(sp, ph.act, (c + 1) * ACT_STEPS[n])
                        dst = out_table[:, bass.ds(c * CT, CT), :] if n == 5 else rows_of(out_table, c)
                        sp.dma_start(dst, table[:, b, :, 0:width]).then_inc(ph.chunk_out[b].sem, 16)

            if index is not None or out_table is not None:
                groups(sp, body, NB)

        @block.sync
        def _(sp):
            sp.dma_start(edge_i, a["dst_tiles"].rearrange("(p j) e -> p (j e)", j=RJ)).then_inc(s_edges, 16)
            sp.dma_start(prev_i, a["dst_before"].rearrange("(p j) e -> p (j e)", j=RJ)).then_inc(s_edges, 16)
            F1 = F + 1
            n = 0
            for m, (w, b) in enumerate((("L0_gnn_Wq", "L0_gnn_bq"), ("L0_gnn_Wk", "L0_gnn_bk"),
                                        ("L0_gnn_Wv", "L0_gnn_bv"))):
                sp.dma_start(w_qkv[0:F, m * F:(m + 1) * F], a[w]).then_inc(s_weights, 16)
                sp.dma_start(w_qkv[F:F1, m * F:(m + 1) * F], a[b].rearrange("(o f) -> o f", o=1)).then_inc(s_weights, 16)
                n += 2
            for t, w, b in ((w_e, "L0_gnn_We", "L0_gnn_be"), (w_pool, "L1_gnn_W_pool", "L1_gnn_b_pool"),
                            (w_2, "L2_gnn_weight", "L2_gnn_bias"), (w_s1, "L1_gnn_W_self1", None),
                            (w_s2, "L1_gnn_W_self2", None), (w_n1, "L1_gnn_W_neigh1", None),
                            (w_n2, "L1_gnn_W_neigh2", None), (w_3, "L3_gnn_W", None)):
                sp.dma_start(t[0:F, :], a[w]).then_inc(s_weights, 16)
                n += 1
                if b:
                    sp.dma_start(t[F:F1, :], a[b].rearrange("(o f) -> o f", o=1)).then_inc(s_weights, 16)
                    n += 1
            for m, v in enumerate(("L1_gnn_g1", "L1_gnn_g2", "L1_gnn_beta1", "L1_gnn_beta2")):
                sp.dma_start(bn_par[:, m:m + 1], a[v].rearrange("(f o) -> f o", o=1)).then_inc(s_weights, 16)
                n += 1
            for m, v in enumerate(("L3_gnn_bias", "L3_gnn_gamma", "L3_gnn_beta")):
                sp.dma_start(row_par[:, m, :], a[v].rearrange("(o f) -> o f", o=1).to_broadcast([P, F])).then_inc(s_weights, 16)
                n += 1
            assert n == W_LOADS

            ph = phases[0]

            def load_x(c, b):
                sp.dma_start(h_cols[0:F, b, :], a["x_cols"][:, bass.ds(c * CN, CN)]).then_inc(ph.node_idx_in[b].sem, 16)

            for b in range(CB):
                load_x(b, b)
            sp.dma_start(starts[:], a["tile_first"]).then_inc(s_first, 16)
            sp.dma_start(src_lo[:].bitcast(I32).rearrange("p (g t) -> p g t", t=TQ), a["src_cols"].rearrange("g p t -> p g t")).then_inc(s_src, 16)
            sp.dma_start(dst_lo[:].bitcast(I32), a["dst_cols"]).then_inc(s_src, 16)
            sp.dma_start(weight_col[:], a["weight_cols"]).then_inc(s_nodes, 16)
            sp.dma_start(x_nodes[:], a["x_nodes"]).then_inc(s_nodes, 16)
            wait(sp, prep, PREP)
            for t, s in ((rank_rows, rank_b), (keep_rows, keep_b), (carry_rows, carry_f)):
                sp.dma_start(t.rearrange("q (o e) -> (q o) e", o=1).rearrange("(p r) e -> p (r e)", p=RP), s).then_inc(rows_out, 16)

            def qkv_out(i, last):
                for b in range(CB):
                    c = i * CB + b
                    wait(sp, ph.x_done, c + 1)
                    wait(sp, ph.act, c + 1)
                    if not last:
                        load_x(c + CB, b)
                    sp.dma_start(rows_of(q_table, c), q_parts[b]).then_inc(ph.chunk_out[b].sem, 16)
                    sp.dma_start(rows_of(kv_table, c), table[:, b]).then_inc(ph.chunk_out[b].sem, 16)

            groups(sp, qkv_out, NB)

            edge_pass_sp(sp, 0)
            sp.wait_ge(last_found, 2)
            node_phase_sp(sp, 1, row_of_node, pair_table, PAIR)
            edge_pass_sp(sp, 1)
            node_phase_sp(sp, 2, row_of_node, None, PAIR)
            node_phase_sp(sp, 3, None, ci_table, F)
            edge_pass_sp(sp, 2)
            node_phase_sp(sp, 4, row_of_node, h_table, F)
            edge_pass_sp(sp, 3)
            node_phase_sp(sp, 5, row_of_node, a["out"], F)
            for b in range(CB):
                wait(sp, phases[5].chunk_out[b], 16 * NB)

        def gather(pool, out, src, idx, done):
            pool.indirect_dma_start(out, None, src, bass.IndirectOffsetOnAxis(ap=idx, axis=0)).then_inc(done, 16)

        def edge_pass_pool(pool, n):
            s = passes[n]
            src = (kv_table, pair_table, ci_table, h_table)[n]
            width = (KV, PAIR, F, F)[n]
            ph = phases[(0, 1, 3, 4)[n]]

            def quad_gather(k):
                for j in range(TQ):
                    gather(pool, rows[:, k, j, 0:width], src, src_idx[:, k, j:j + 1], s.rows_in[k].sem)

            for b in range(CB):
                wait(pool, ph.chunk_out[b], (32 if n == 0 else 16) * NB)
            for k in range(GQ):
                wait(pool, s.idx_in[k // 2], 16)
                quad_gather(k)

            def body(i, last):
                for k in range(GQ):
                    wait(pool, s.idx_in[k // 2], (i + 2) * 16)
                    if n == 0:
                        wait(pool, s.msg_done, i * GQ + k + 1)
                    else:
                        wait(pool, s.agg_done, (i * GQ + k + 1) * TQ)
                    pool.sem_inc(held, 1)
                    quad_gather(k)

            groups(pool, body, NG - 1)

        def node_phase_pool(pool, n, width):
            ph = phases[n]
            at = {1: 0, 2: 1, 4: 2, 5: 3}[n]
            for h in range(GP):
                wait(pool, passes[at].out[h], 16 * NG)

            def body(i, last):
                for b in range(CB):
                    wait(pool, ph.node_idx_in[b], (i + 1) * 16)
                    wait(pool, ph.used, i * CB + b - 1)
                    pool.sem_inc(held, 1)
                    for t in range(CT):
                        gather(pool, got[:, b, t, 0:width], sums[at], node_idx[:, b, t:t + 1], ph.got_in[b].sem)

            groups(pool, body, NB)

        @block.gpsimd
        def _(pool):
            pool.memset(ident[:], 0.0).then_inc(made_steps, 1)
            pool.wait_ge(made_steps, 1)
            pool.affine_select(out=ident[:], in_=ident[:], compare_op=ALU.not_equal, fill=1.0, base=0,
                               pattern=[[-1, P]], channel_multiplier=1).then_inc(made, 1)
            pool.iota(iota_row[:], [[1, P]], base=0, channel_multiplier=0, allow_small_or_imprecise_dtypes=True).then_inc(made, 1)
            pool.iota(iota_col[:], [[0, 1]], base=0, channel_multiplier=1, allow_small_or_imprecise_dtypes=True).then_inc(made, 1)
            pool.wait_ge(ready, 7)
            pool.affine_select(out=upto[:], in_=ones[:], compare_op=ALU.is_ge, fill=0.0, base=0,
                               pattern=[[1, P]], channel_multiplier=-1).then_inc(made, 1)

            edge_pass_pool(pool, 0)
            node_phase_pool(pool, 1, AGG)
            edge_pass_pool(pool, 1)
            node_phase_pool(pool, 2, PAIR)
            edge_pass_pool(pool, 2)
            node_phase_pool(pool, 4, F)
            edge_pass_pool(pool, 3)
            node_phase_pool(pool, 5, F)


        @block.tensor
        def _(pe):
            pe.wait_ge(s_weights, 16 * W_LOADS)
            pe.wait_ge(made, 4)
            pe.wait_ge(ready, 7)
            ph = phases[0]

            def qkv(i, last):
                for b in range(CB):
                    c = i * CB + b
                    wait(pe, ph.node_idx_in[b], (i + 1) * 16)
                    wait(pe, ph.act, c)
                    for t in range(CT):
                        mm = pe.matmul(bank[t][:, 0:3 * F], h_cols[:, b, t * P:(t + 1) * P], w_qkv[:], start=True, stop=True)
                    mm.then_inc(ph.pe.sem, 1)

            groups(pe, qkv, NB)
            wait(pe, prep, PREP)
            for j in range(RJ):
                tr = pe.transpose(bank[5 + j // 4][:, (j % 4) * P:(j % 4) * P + RP], rank_f[:, j * P:(j + 1) * P], ident[0:RP, 0:RP])
            tr.then_inc(turned, 1)

            def aggregate(s, q, i, k, n, between=None):
                width = AGG if n == 0 else F
                wait(pe, s.same_done, q + 1)
                if n == 0:
                    wait(pe, s.msg_done, q + 1)
                wait(pe, s.carry_in[k // 2], (i + 1) * 16)
                for j in range(TQ):
                    acc = bank[4 + j % 2][:, 0:width]
                    wait(pe, s.copied, q * TQ + j - 1)
                    values = msg[:, k % 2, j, :] if n == 0 else rows[:, k, j, 0:F]
                    pe.matmul(acc, same[:, k % 2, j, :], values, start=True, stop=False)
                    if between:
                        between(j)
                    wait(pe, s.copied, q * TQ + j)
                    pk, pj = (k, j - 1) if j else ((k - 1) % GQ, TQ - 1)
                    pe.matmul(acc, carry[:, k, j * P:(j + 1) * P], out_rows[:, pk, pj, 0:width],
                              start=False, stop=True).then_inc(s.agg_done.sem, 1)

            hist = bank[7][:, 0:NT]

            def clear_counts():
                pe.matmul(hist, zeros[:], iota_row[:, 0:NT], start=True, stop=False, skip_group_check=True)

            def count_nodes(s, q, k):
                wait(pe, s.hot_done, q + 1)
                for j in range(TQ):
                    mm = pe.matmul(hist, hot_lo[:, k % 2, j, :], hot_hi[:, k % 2, j, :], start=False, stop=False, skip_group_check=True)
                mm.then_inc(s.hist_done.sem, 1)

            s0 = passes[0]
            clear_counts()

            def factors(q, i, k, j):
                if j == 0:
                    wait(pe, s0.attr_in[k // 2], (i + 1) * 16)
                    wait(pe, s0.prod_done, q - 1)
                    wait(pe, s0.pick_done, q + 1)
                    wait(pe, s0.win_in[k], (i + 1) * 16 * TQ)
                pe.matmul(quad(bank[k % 2], F)[:, j, :], attr[:, k, j * P:(j + 1) * P], w_e[:], start=True, stop=True)
                for m in range(PARTS):
                    mm = pe.matmul(quad(bank[2 + k % 2], F)[:, j, :], pick[:, k % 2, j * P:(j + 1) * P],
                                   q_win[:, k, j, m * F:(m + 1) * F], start=(m == 0), stop=(m == PARTS - 1))
                if j == TQ - 1:
                    mm.then_inc(s0.q_done.sem, 1)

            def attention(i, last):
                for k in range(GQ):
                    q = i * GQ + k
                    more = not (last and k == GQ - 1)

                    def ahead(j, q=q, k=k):
                        factors(q + 1, i if k < GQ - 1 else i + 1, (k + 1) % GQ, j)

                    if isinstance(q, int) and q == 0:
                        for j in range(TQ):
                            ahead(j)
                    else:
                        aggregate(s0, q - 1, i if k else i - 1, (k - 1) % GQ, 0, ahead if more else None)
                        count_nodes(s0, q - 1, (k - 1) % GQ)

            for j in range(TQ):
                factors(0, 0, 0, j)
            groups(pe, attention, NG)
            aggregate(s0, NQ - 1, NG - 1, GQ - 1, 0)
            count_nodes(s0, NQ - 1, GQ - 1)
            pe.wait_ge(last_found, 1)
            pe.matmul(bank[6][:, 0:NT], upto[:], deg_in, start=True, stop=True)
            pe.matmul(bank[6][:, NT:2 * NT], ones[:], deg_in, start=True, stop=True).then_inc(deg_sums, 1)

            def turn(b0, src, ph_sem=None):
                for t in range(CT):
                    tr = pe.transpose(bank[b0 + t // 4][0:F, (t % 4) * P:(t % 4 + 1) * P], src[:, t, :], ident[:])
                return tr

            ph = phases[1]

            def nodes1(i, last):
                for b in range(CB):
                    c = i * CB + b
                    wait(pe, ph.x_done, c + 1)
                    wait(pe, ph.act, c * 7)
                    turn(0, x_new[:, b]).then_inc(ph.pe.sem, 1)
                    wait(pe, ph.act, c * 7 + 2)
                    for t in range(CT):
                        pe.matmul(five(bank[2])[:, t, :], h_cols[:, 0, t * P:(t + 1) * P], w_pool[:], start=True, stop=True)
                    for m, w in enumerate((w_s1, w_s2)):
                        for h in range(2):
                            mm = pe.matmul(bank[3 + 2 * m + h][0:F, 0:HALF], w[:], h_cols[0:F, 0, h * HALF:(h + 1) * HALF], start=True, stop=True)
                    mm.then_inc(ph.pe.sem, 1)

            groups(pe, nodes1, NB)

            s1 = passes[1]
            clear_counts()

            def sage(i, last):
                for k in range(GQ):
                    q = i * GQ + k
                    wait(pe, s1.rows_in[k], (i + 1) * 16 * TQ)
                    wait(pe, s1.scan_done, q - 1)
                    for j in range(TQ):
                        tr = pe.transpose(bank[k % 2][0:F, j * P:(j + 1) * P], rows[:, k, j, F:PAIR], ident[:])
                    tr.then_inc(s1.turn_done.sem, 1)
                    aggregate(s1, q, i, k, 1)
                    count_nodes(s1, q, k)
                    wait(pe, s1.scan_done, q + 1)
                    wait(pe, s1.max_copied, q - 1)
                    for j in range(TQ):
                        tr = pe.transpose(quad(bank[2 + k % 2], F)[:, j, :], scanned[:, k % 2, j * P:(j + 1) * P], ident[0:F, 0:F])
                    tr.then_inc(s1.back_done.sem, 1)

            groups(pe, sage, NG)

            ph = phases[2]

            def nodes2(i, last):
                for b in range(CB):
                    c = i * CB + b
                    wait(pe, ph.h_done, c + 1)
                    wait(pe, ph.act, c)
                    turn(0, h_a)
                    turn(2, h_b).then_inc(ph.pe.sem, 1)
                    wait(pe, ph.act, c + 1)
                    wait(pe, ph.x_done, c)
                    for m, w in enumerate((w_n1, w_n2)):
                        for h in range(2):
                            mm = pe.matmul(bank[4 + 2 * m + h][0:F, 0:HALF], w[:], h_cols[0:F, m, h * HALF:(h + 1) * HALF], start=True, stop=True)
                    mm.then_inc(ph.pe.sem, 1)

            pe.wait_ge(deg_done, 1)
            groups(pe, nodes2, NB)

            ph = phases[3]

            def nodes3(i, last):
                for b in range(CB):
                    c = i * CB + b
                    wait(pe, ph.h_done, c + 1)
                    wait(pe, ph.used, c)
                    for t in range(CT):
                        tr = pe.transpose(five(bank[0])[:, t, :], h_cols[0:F, 0, t * P:(t + 1) * P], ident[0:F, 0:F])
                    tr.then_inc(ph.pe.sem, 1)

            groups(pe, nodes3, NB)

            def plain(n):
                s = passes[n]

                def body(i, last):
                    for k in range(GQ):
                        wait(pe, s.rows_in[k], (i + 1) * 16 * TQ)
                        aggregate(s, i * GQ + k, i, k, n)

                groups(pe, body, NG)

            plain(2)

            ph = phases[4]

            def nodes4(i, last):
                for b in range(CB):
                    c = i * CB + b
                    wait(pe, ph.h_done, c + 1)
                    wait(pe, ph.act, c * 4)
                    turn(0, h_a).then_inc(ph.pe.sem, 1)
                    wait(pe, ph.act, c * 4 + 1)
                    for t in range(CT):
                        mm = pe.matmul(five(bank[2])[:, t, :], h_cols[:, 0, t * P:(t + 1) * P], w_2[:], start=True, stop=True)
                    mm.then_inc(ph.pe.sem, 1)
                    wait(pe, ph.x_done, c + 1)
                    turn(4, x_new[:, b]).then_inc(ph.pe.sem, 1)
                    wait(pe, ph.act, c * 4 + 3)
                    for t in range(CT):
                        mm = pe.matmul(five(bank[3])[:, t, :], h_cols[0:F, 1, t * P:(t + 1) * P], w_3[:], start=True, stop=True)
                    mm.then_inc(ph.pe.sem, 1)

            groups(pe, nodes4, NB)
            plain(3)

        @block.scalar
        def _(act):
            ph = phases[0]

            def qkv(i, last):
                for b in range(CB):
                    c = i * CB + b
                    wait(act, ph.pe, c + 1)
                    wait(act, ph.used, c)
                    wait(act, ph.chunk_out[b], i * 32)
                    for t in range(CT):
                        act.mul(h_a[:, t, :], bank[t][:, 0:F], float(D) ** -0.5)
                    for t in range(CT):
                        cp = act.copy(table[:, b, t, :], bank[t][:, F:3 * F])
                    cp.then_inc(ph.act.sem, 1)

            groups(act, qkv, NB)

            def copy_tile(s, q, i, k, j, width):
                wait(act, s.agg_done, q * TQ + j + 1)
                if j == 0:
                    wait(act, s.out[k // 2], i * 16)
                act.copy(out_rows[:, k, j, 0:width], bank[4 + j % 2][:, 0:width]).then_inc(s.copied.sem, 1)

            s0 = passes[0]
            act.wait_ge(s_first, 16)

            def attention(i, last):
                for k in range(GQ):
                    q = i * GQ + k
                    behind = not isinstance(q, int) or q > 0
                    pk, pi = (k - 1) % GQ, (i if k else i - 1)
                    wait(act, s0.clip_done, q + 1)
                    wait(act, s0.msg_done, q - 1)
                    act.activation(quad(bank[6], HEADS * 2)[:, :, (k % 2) * HEADS:(k % 2 + 1) * HEADS], score[:], ACT.Exp)
                    act.activation(msg[:, k % 2, :, F:AGG], score[:], ACT.Exp).then_inc(s0.exp_done.sem, 1)
                    for j in range(TQ):
                        if behind:
                            copy_tile(s0, q - 1, pi, pk, j, AGG)
                        if j == 1 and not last:
                            wait(act, s0.q_done, q + 1)
                            for w in range(WIN_SP, TQ):
                                load_window(act, q + GQ, k, w)

            groups(act, attention, NG)
            for j in range(TQ):
                copy_tile(s0, NQ - 1, NG - 1, GQ - 1, j, AGG)

            def root(ph, c):
                wait(act, ph.var_done, c)
                act.activation(dev[:], mean_var[:, :, 1], ACT.Sqrt, bias=eps_z[:, 0:1]).then_inc(ph.dev_done.sem, 1)

            def columns(b0, dst, m):
                act.copy(dst[0:F, m, 0:4 * P], bank[b0][0:F, :])
                return act.copy(dst[0:F, m, 4 * P:CN], bank[b0 + 1][0:F, 0:P])

            act.wait_ge(deg_ready, 1)
            act.activation(tmp_b, tmp_a, ACT.Sqrt).then_inc(deg_root, 1)

            ph = phases[1]

            def nodes1(i, last):
                for b in range(CB):
                    c = i * CB + b
                    root(ph, c + 1)
                    wait(act, ph.x_done, c + 1)
                    wait(act, ph.chunk_out[b], i * 16)
                    act.copy(x_nodes[:, bass.ds(c * CT, CT), :], x_new[:, b]).then_inc(ph.act.sem, 1)
                    wait(act, ph.pe, c * 2 + 1)
                    columns(0, h_cols, 0).then_inc(ph.act.sem, 1)
                    act.copy(table[:, b, :, 0:F], x_new[:, b])
                    wait(act, ph.pe, c * 2 + 2)
                    act.activation(table[:, b, :, F:PAIR], five(bank[2]), ACT.Relu).then_inc(ph.act.sem, 1)
                    for m in range(2):
                        for h in range(2):
                            act.copy(wide[0:F, m, bass.ds(c * CN + h * HALF, HALF)], bank[3 + 2 * m + h][0:F, 0:HALF]).then_inc(ph.act.sem, 1)

            groups(act, nodes1, NB)

            def plain(n):
                s = passes[n]

                def body(i, last):
                    for k in range(GQ):
                        q = i * GQ + k
                        for j in range(TQ):
                            copy_tile(s, q, i, k, j, F)
                        if n == 1:
                            wait(act, s.back_done, q + 1)
                            act.copy(out_rows[:, k, :, F:PAIR], quad(bank[2 + k % 2], F)).then_inc(s.max_copied.sem, 1)

                groups(act, body, NG)

            plain(1)
            act.wait_ge(deg_ready, 2)
            act.activation(tmp_b, tmp_a, ACT.Sqrt).then_inc(deg_root, 1)

            ph = phases[2]

            def nodes2(i, last):
                for b in range(CB):
                    c = i * CB + b
                    wait(act, ph.pe, c * 2 + 1)
                    columns(0, h_cols, 0)
                    columns(2, h_cols, 1).then_inc(ph.act.sem, 1)

            groups(act, nodes2, NB)
            act.wait_ge(bn_ready, 1)
            act.activation(bn_a[:, 0:2], bn_mv[:, :, 1], ACT.Sqrt, bias=eps_z[0:F, 0:1]).then_inc(bn_root, 1)

            ph = phases[3]

            def nodes3(i, last):
                for b in range(CB):
                    c = i * CB + b
                    root(ph, c + 1)
                    wait(act, ph.x_done, c + 1)
                    act.copy(x_nodes[:, bass.ds(c * CT, CT), :], x_new[:, b]).then_inc(ph.act.sem, 1)

            groups(act, nodes3, NB)
            plain(2)

            ph = phases[4]

            def nodes4(i, last):
                for b in range(CB):
                    c = i * CB + b
                    wait(act, ph.pe, c * 4 + 1)
                    columns(0, h_cols, 0).then_inc(ph.act.sem, 1)
                    root(ph, c + 1)
                    wait(act, ph.x_done, c + 1)
                    act.copy(x_nodes[:, bass.ds(c * CT, CT), :], x_new[:, b]).then_inc(ph.act.sem, 1)
                    wait(act, ph.pe, c * 4 + 3)
                    columns(4, h_cols, 1).then_inc(ph.act.sem, 1)
                    wait(act, ph.pe, c * 4 + 4)
                    wait(act, ph.chunk_out[b], i * 16)
                    act.copy(table[:, b, :, 0:F], five(bank[3])).then_inc(ph.act.sem, 1)

            groups(act, nodes4, NB)
            plain(3)

            ph = phases[5]

            def nodes5(i, last):
                for b in range(CB):
                    for m in range(2):
                        root(ph, (i * CB + b) * 2 + m + 1)

            groups(act, nodes5, NB)

        @block.vector
        def _(dve):
            dve.memset(ones[:], 1.0).then_inc(ready, 1)
            dve.memset(carry[:], 0.0).then_inc(ready, 1)
            dve.memset(out_rows[:, GQ - 1, :, :], 0.0).then_inc(ready, 1)
            dve.memset(eps_z[:], LN_EPS).then_inc(ready, 1)
            dve.memset(zeros[:], 0.0).then_inc(ready, 1)
            dve.memset(attr[F:F + 1, :, :], 1.0).then_inc(ready, 1)
            dve.memset(h_cols[F:F + 1, :, :], 1.0).then_inc(ready, 1)
            dve.wait_ge(ready, 7)
            dve.wait_ge(made, 4)
            dve.sem_inc(pin, 1)


            def tiled(t):
                return t.rearrange("p (j e) -> p j e", j=RJ)

            st = Steps(dve, prep, 0, pin)
            dve.wait_ge(s_edges, 32)
            st.did(dve.tensor_tensor(keep_f, edge_i, prev_i, ALU.is_equal))
            st.did(dve.tensor_tensor(new_f, edge_i, prev_i, ALU.not_equal))
            st.did(dve.memset(hold_f, 1.0))
            st.settle()
            st.did(dve.memset(tiled(hold_f)[:, :, 0:1], 0.0))
            st.did(dve.memset(tiled(new_f)[:, :, 0:1], 0.0))
            st.settle()
            st.did(dve.tensor_tensor_scan(rank_f, hold_f, new_f, 0.0, ALU.mult, ALU.add))
            st.did(dve.tensor_copy(keep_b, keep_f))
            st.settle()
            st.did(dve.tensor_copy(rank_b, rank_f))
            st.did(dve.scalar_tensor_tensor(out=tiled(carry_f), in0=tiled(rank_f), scalar=0.0,
                                            in1=tiled(keep_f)[:, :, 0:1].to_broadcast([RP, RJ, P]),
                                            op0=ALU.is_equal, op1=ALU.mult))
            assert st.n == PREP

            ph = phases[0]

            def split(i, last):
                for b in range(CB):
                    c = i * CB + b
                    st = Steps(dve, ph.dve, c * 5, pin)
                    wait(dve, ph.act, c + 1)
                    wait(dve, ph.chunk_out[b], i * 32)
                    part = [q_parts[b][:, :, m * F:(m + 1) * F] for m in range(PARTS)]
                    st.did(dve.tensor_copy(part[0], h_a[:]))
                    st.settle()
                    st.did(dve.tensor_tensor(h_b[:], h_a[:], part[0], ALU.subtract))
                    st.settle()
                    st.did(dve.tensor_copy(part[1], h_b[:]))
                    st.settle()
                    st.did(dve.tensor_tensor(h_b[:], h_b[:], part[1], ALU.subtract))
                    st.settle()
                    st.did(dve.tensor_copy(part[2], h_b[:]))
                    st.settle()
                    dve.sem_inc(ph.used.sem, 1)
                    dve.sem_inc(ph.x_done.sem, 1)

            groups(dve, split, NB)

            dve.wait_ge(turned, 1)
            by_j = rank_col[:].rearrange("p (r j) -> p j r", j=RJ)
            for j in range(RJ):
                cp = dve.tensor_copy(by_j[:, j, :], bank[5 + j // 4][:, (j % 4) * P:(j % 4) * P + RP])
            cp.then_inc(ranked, 1)

            dve.wait_ge(s_src, 32)
            for lo, hi in ((src_lo, src_hi), (dst_lo, dst_hi)):
                dve.tensor_scalar(hi[:].bitcast(I32), lo[:].bitcast(I32), P.bit_length() - 1, None, ALU.arith_shift_right).then_inc(src_step, 1)
            dve.wait_ge(src_step, 2)
            for lo in (src_lo, dst_lo):
                dve.tensor_scalar(lo[:].bitcast(I32), lo[:].bitcast(I32), P - 1, None, ALU.bitwise_and).then_inc(src_step, 1)
            dve.wait_ge(src_step, 4)
            for part in (src_lo, src_hi, dst_lo, dst_hi):
                dve.tensor_copy(part[:], part[:].bitcast(I32)).then_inc(src_step, 1)
            dve.wait_ge(src_step, 8)
            dve.wait_ge(ranked, 1)

            def same_runs(s, q, i, k, n):
                wait(dve, s.agg_done, (q - 1) * TQ)
                for j in range(TQ):
                    at = bass.ds(q * TQ + j, 1)
                    mine, theirs = rank_col[:, at], rank_row[:, k, j * P:(j + 1) * P]
                    if n == 3:
                        ins = dve.tensor_scalar(same[:, k % 2, j, :], theirs, mine, weight_col[:, at], ALU.is_equal, ALU.mult)
                    else:
                        ins = dve.tensor_scalar(same[:, k % 2, j, :], theirs, mine, None, ALU.is_equal)
                ins.then_inc(s.same_done.sem, 1)

            def one_hot(s, q, k, lo, hi):
                wait(dve, s.hist_done, q - 1)
                for j in range(TQ):
                    at = bass.ds(q * TQ + j, 1)
                    dve.tensor_scalar(hot_lo[:, k % 2, j, :], iota_row[:], lo[:, at], None, ALU.is_equal)
                    ins = dve.tensor_scalar(hot_hi[:, k % 2, j, :], iota_row[:, 0:NT], hi[:, at], None, ALU.is_equal)
                ins.then_inc(s.hot_done.sem, 1)

            s0 = passes[0]

            def picks(q, i, k):
                wait(dve, s0.rank_in[k // 2], (i + 1) * 16)
                wait(dve, s0.q_done, q - 1)
                dve.tensor_scalar(pick[:, k % 2, :], rank_row[:, k, :], iota_col[:, 0:1], None, ALU.is_equal).then_inc(s0.pick_done.sem, 1)

            def attention(i, last):
                for k in range(GQ):
                    q = i * GQ + k
                    if not (last and k == GQ - 1):
                        picks(q + 1, i if k < GQ - 1 else i + 1, (k + 1) % GQ)
                    wait(dve, s0.rows_in[k], (i + 1) * 16 * TQ)
                    wait(dve, s0.q_done, q + 1)
                    dve.tensor_tensor(prod[:], quad(bank[2 + k % 2], F), rows[:, k, :, 0:F], ALU.mult).then_inc(s0.prod_step.sem, 1)
                    wait(dve, s0.prod_step, q + 1)
                    dve.tensor_tensor(prod[:], quad(bank[k % 2], F), prod[:], ALU.mult).then_inc(s0.prod_done.sem, 1)
                    wait(dve, s0.prod_done, q + 1)
                    dve.tensor_reduce(score[:], prod[:].rearrange("p j (h d) -> p j h d", h=HEADS), AX_X, ALU.add).then_inc(s0.score_step.sem, 1)
                    wait(dve, s0.score_step, q + 1)
                    dve.tensor_scalar(score[:], score[:], 5.0, -5.0, ALU.min, ALU.max).then_inc(s0.clip_done.sem, 1)
                    same_runs(s0, q, i, k, 0)
                    one_hot(s0, q, k, dst_lo, dst_hi)
                    wait(dve, s0.exp_done, q + 1)
                    dve.tensor_tensor(msg[:, k % 2, :, 0:F].rearrange("p j (h d) -> p j h d", h=HEADS),
                                      rows[:, k, :, F:KV].rearrange("p j (h d) -> p j h d", h=HEADS),
                                      quad(bank[6], HEADS * 2)[:, :, (k % 2) * HEADS:(k % 2 + 1) * HEADS]
                                      .rearrange("p j (h o) -> p j h o", o=1).to_broadcast([P, TQ, HEADS, D]),
                                      ALU.mult).then_inc(s0.msg_done.sem, 1)

            picks(0, 0, 0)
            groups(dve, attention, NG)

            wait(dve, s0.hist_done, NQ)
            st = Steps(dve, deg_step, 0, pin)
            st.did(dve.tensor_copy(deg_in, bank[7][:, 0:NT]))
            st.settle()
            dve.sem_inc(last_found, 1)
            dve.wait_ge(deg_sums, 1)
            st.did(dve.tensor_tensor_scan(running[:], ones[:, 0:NT], bank[6][:, NT:2 * NT], 0.0, ALU.mult, ALU.add))
            st.did(dve.tensor_copy(count[:], bank[6][:, 0:NT]))
            st.settle()
            st.did(dve.tensor_tensor(count[:], count[:], running[:], ALU.add))
            st.settle()
            st.did(dve.tensor_tensor(count[:], count[:], bank[6][:, NT:2 * NT], ALU.subtract))
            st.settle()
            e_i, part_i, tile_i, row_i = (last_edge[:, m, :] for m in range(4))
            st.did(dve.tensor_scalar(tmp_a, count[:], -1.0, 0.0, ALU.add, ALU.max))
            st.settle()
            st.did(dve.tensor_copy(e_i, tmp_a))
            st.settle()
            st.did(dve.tensor_scalar(part_i, e_i, P - 1, (2 * TQ).bit_length() - 1, ALU.bitwise_and, ALU.logical_shift_left))
            st.did(dve.tensor_scalar(tile_i, e_i, P.bit_length() - 1, 2 * TQ - 1, ALU.logical_shift_right, ALU.bitwise_and))
            st.settle()
            st.did(dve.tensor_tensor(part_i, part_i, tile_i, ALU.bitwise_or))
            st.did(dve.tensor_scalar(e_i, e_i, (2 * QE).bit_length() - 1, (2 * QE).bit_length() - 1, ALU.logical_shift_right, ALU.logical_shift_left))
            st.settle()
            st.did(dve.tensor_tensor(row_i, part_i, e_i, ALU.bitwise_or))
            st.did(dve.tensor_scalar(has_in, deg_in, 0.0, None, ALU.is_gt))
            st.did(dve.tensor_scalar(no_in, deg_in, 0.0, None, ALU.is_le))
            st.did(dve.tensor_scalar(tmp_a, deg_in, 1.0, None, ALU.max))
            st.settle()
            st.did(dve.reciprocal(r_mean, tmp_a))
            dve.sem_inc(deg_ready, 1)
            st.settle()
            st.did(dve.tensor_tensor(r_mean, r_mean, has_in, ALU.mult))
            dve.wait_ge(deg_root, 1)
            st.did(dve.reciprocal(c_in, tmp_b))
            st.settle()
            st.did(dve.tensor_tensor(c_in, c_in, has_in, ALU.mult))
            st.settle()
            dve.sem_inc(last_found, 1)

            def per_tile(t, c):
                return t[:, bass.ds(c * CT, CT)].rearrange("p (t o) -> p t o", o=1).to_broadcast([P, CT, F])

            def layer_norm(st, ph, out, src, rounds):
                for t in range(CT):
                    ins = dve.bn_stats(stats[:, t, :], src[:, t, :])
                st.did(ins)
                st.settle(True)
                for t in range(CT):
                    ins = dve.bn_aggr(mean_var[:, t, :], stats[:, t, :])
                st.did(ins)
                st.settle()
                dve.sem_inc(ph.var_done.sem, 1)
                wait(dve, ph.dev_done, rounds)
                st.did(dve.reciprocal(rdev[:], dev[:]))
                st.settle()
                for t in range(CT):
                    ins = dve.tensor_scalar(out[:, t, :], src[:, t, :], mean_var[:, t, 0:1], rdev[:, t:t + 1], ALU.subtract, ALU.mult)
                return ins

            ph = phases[1]

            def nodes1(i, last):
                for b in range(CB):
                    c = i * CB + b
                    st = Steps(dve, ph.dve, c * 7, pin)
                    wait(dve, ph.got_in[b], (i + 1) * 16 * CT)
                    st.did(dve.tensor_scalar(z_inv[:], got[:, b, :, F:AGG], 1e-6, None, ALU.add))
                    st.settle()
                    st.did(dve.reciprocal(z_inv[:], z_inv[:]))
                    st.settle()
                    st.did(dve.tensor_tensor(z_inv[:], z_inv[:], per_tile(has_in, c)[:, :, 0:HEADS], ALU.mult))
                    st.settle()
                    st.did(dve.tensor_tensor(h_a[:].rearrange("p t (h d) -> p t h d", h=HEADS),
                                             got[:, b, :, 0:F].rearrange("p t (h d) -> p t h d", h=HEADS),
                                             z_inv[:].rearrange("p t (h o) -> p t h o", o=1).to_broadcast([P, CT, HEADS, D]), ALU.mult))
                    st.settle()
                    dve.tensor_tensor(h_b[:], h_a[:], x_nodes[:, bass.ds(c * CT, CT), :], ALU.add).then_inc(ph.used.sem, 1)
                    wait(dve, ph.used, c + 1)
                    wait(dve, ph.act, (c - 1) * 7)
                    layer_norm(st, ph, x_new[:, b], h_b, c + 1).then_inc(ph.x_done.sem, 1)
                    assert st.n == 7

            dve.wait_ge(s_nodes, 32)
            groups(dve, lambda i, last: nodes1(i, last), NB)

            s1 = passes[1]

            def sage(i, last):
                for k in range(GQ):
                    q = i * GQ + k
                    wait(dve, s1.rank_in[k // 2], (i + 1) * 16)
                    wait(dve, s1.keep_in[k // 2], (i + 1) * 16)
                    same_runs(s1, q, i, k, 1)
                    wait(dve, s1.turn_done, q + 1)
                    wait(dve, s1.scan_done, q)
                    wait(dve, s1.back_done, q - 1)
                    first = isinstance(q, int) and q == 0
                    dve.tensor_tensor_scan(scanned[:, k % 2, :], keep_row[:, k, :], bank[k % 2][0:F, :],
                                           0.0 if first else scanned[:, (k - 1) % 2, QE - 1:QE],
                                           ALU.mult, ALU.max).then_inc(s1.scan_done.sem, 1)
                    one_hot(s1, q, k, src_lo, src_hi)

            groups(dve, sage, NG)
            wait(dve, s1.hist_done, NQ)
            dve.tensor_scalar(tmp_a, bank[7][:, 0:NT], 1.0, None, ALU.max).then_inc(deg_ready, 1)
            dve.wait_ge(deg_ready, 2)
            dve.sem_inc(deg_done, 1)
            dve.wait_ge(deg_root, 2)
            dve.reciprocal(c_out, tmp_b).then_inc(deg_done, 1)

            ph = phases[2]

            def nodes2(i, last):
                for b in range(CB):
                    c = i * CB + b
                    wait(dve, ph.got_in[b], (i + 1) * 16 * CT)
                    wait(dve, ph.pe, (c - 1) * 2 + 1)
                    dve.tensor_tensor(h_a[:], got[:, b, :, 0:F], per_tile(r_mean, c), ALU.mult)
                    dve.tensor_tensor(h_b[:], got[:, b, :, F:PAIR], per_tile(has_in, c), ALU.mult).then_inc(ph.h_done.sem, 1)
                    wait(dve, ph.h_done, c + 1)
                    dve.sem_inc(ph.used.sem, 1)
                    wait(dve, ph.pe, c * 2 + 2)
                    for m in range(2):
                        for h in range(2):
                            part = wide[0:F, m, bass.ds(c * CN + h * HALF, HALF)]
                            ins = dve.tensor_tensor(part, bank[4 + 2 * m + h][0:F, 0:HALF], part, ALU.add)
                    ins.then_inc(ph.x_done.sem, 1)
                    wait(dve, ph.x_done, c + 1)
                    for m in range(2):
                        for h in range(2):
                            valid = min(HALF, N - (c * CN + h * HALF)) if last else HALF
                            if valid > 0:
                                ins = dve.bn_stats(bn_stat[:, m, bass.ds(c * 2 + h, 1), :].rearrange("p o s -> p (o s)"),
                                                   wide[0:F, m, bass.ds(c * CN + h * HALF, valid)])
                    if last:
                        ins.then_inc(bn_step.sem, 1)

            groups(dve, nodes2, NB)
            halves = -(-N // HALF)
            st = Steps(dve, bn_step, CB, pin)
            st.settle()
            for m in range(2):
                ins = dve.bn_aggr(bn_mv[:, m, :], bn_stat[:, m, 0:halves, :].rearrange("p c s -> p (c s)"))
            st.did(ins)
            st.settle()
            dve.sem_inc(bn_ready, 1)
            dve.wait_ge(bn_root, 1)
            st.did(dve.reciprocal(bn_a[:, 2:4], bn_a[:, 0:2]))
            st.settle()
            st.did(dve.tensor_tensor(bn_a[:, 2:4], bn_a[:, 2:4], bn_par[:, 0:2], ALU.mult))
            st.settle()
            st.did(dve.tensor_tensor(bn_a[:, 4:6], bn_mv[:, :, 0], bn_a[:, 2:4], ALU.mult))
            st.settle()
            st.did(dve.tensor_tensor(bn_a[:, 4:6], bn_par[:, 2:4], bn_a[:, 4:6], ALU.subtract))
            st.settle()
            st.did(dve.tensor_tensor(bn_a[:, 6:7], bn_a[:, 4:5], bn_a[:, 5:6], ALU.add))
            st.settle()

            ph = phases[3]

            def nodes3(i, last):
                for b in range(CB):
                    c = i * CB + b
                    st = Steps(dve, ph.dve, c * 6, pin)
                    cols = h_cols[0:F, 0, :]
                    wait(dve, ph.pe, c)
                    st.did(dve.tensor_scalar(cols, wide[0:F, 0, bass.ds(c * CN, CN)], bn_a[:, 2:3], bn_a[:, 6:7], ALU.mult, ALU.add))
                    st.settle()
                    st.did(dve.scalar_tensor_tensor(out=cols, in0=wide[0:F, 1, bass.ds(c * CN, CN)], scalar=bn_a[:, 3:4], in1=cols, op0=ALU.mult, op1=ALU.add))
                    st.settle()
                    dve.scalar_tensor_tensor(out=cols, in0=cols, scalar=0.01, in1=cols, op0=ALU.mult, op1=ALU.max).then_inc(ph.h_done.sem, 1)
                    wait(dve, ph.pe, c + 1)
                    dve.tensor_tensor(h_b[:], five(bank[0]), x_nodes[:, bass.ds(c * CT, CT), :], ALU.add).then_inc(ph.used.sem, 1)
                    wait(dve, ph.used, c + 1)
                    wait(dve, ph.act, c - 1)
                    st.did(layer_norm(st, ph, x_new[:, b], h_b, c + 1))
                    st.settle()
                    wait(dve, ph.chunk_out[b], i * 16)
                    dve.tensor_tensor(table[:, b, :, 0:F], x_new[:, b], per_tile(c_out, c), ALU.mult).then_inc(ph.x_done.sem, 1)
                    assert st.n == 6

            dve.wait_ge(deg_done, 2)
            groups(dve, nodes3, NB)

            def plain(n):
                s = passes[n]

                def body(i, last):
                    for k in range(GQ):
                        wait(dve, s.rank_in[k // 2], (i + 1) * 16)
                        same_runs(s, i * GQ + k, i, k, n)

                groups(dve, body, NG)

            plain(2)

            ph = phases[4]

            def nodes4(i, last):
                for b in range(CB):
                    c = i * CB + b
                    st = Steps(dve, ph.dve, c * 6, pin)
                    wait(dve, ph.got_in[b], (i + 1) * 16 * CT)
                    wait(dve, ph.pe, (c - 1) * 4 + 1)
                    wait(dve, ph.x_done, c)
                    here = x_nodes[:, bass.ds(c * CT, CT), :]
                    st.did(dve.tensor_tensor(h_b[:], got[:, b, :, 0:F], per_tile(c_in, c), ALU.mult))
                    st.did(dve.tensor_tensor(h_a[:], here, per_tile(no_in, c), ALU.mult))
                    st.settle()
                    dve.tensor_tensor(h_a[:], h_a[:], h_b[:], ALU.add).then_inc(ph.h_done.sem, 1)
                    wait(dve, ph.h_done, c + 1)
                    dve.sem_inc(ph.used.sem, 1)
                    wait(dve, ph.pe, c * 4 + 2)
                    st.did(dve.tensor_tensor(h_b[:], five(bank[2]), here, ALU.add))
                    st.settle()
                    wait(dve, ph.act, (c - 1) * 4)
                    layer_norm(st, ph, x_new[:, b], h_b, c + 1).then_inc(ph.x_done.sem, 1)
                    assert st.n == 6

            groups(dve, nodes4, NB)
            plain(3)

            ph = phases[5]

            def over_tiles(m):
                return row_par[:, m:m + 1, :].to_broadcast([P, CT, F])

            def nodes5(i, last):
                for b in range(CB):
                    c = i * CB + b
                    st = Steps(dve, ph.dve, c * 11, pin)
                    wait(dve, ph.x_done, c)
                    wait(dve, ph.got_in[b], (i + 1) * 16 * CT)
                    st.did(dve.tensor_tensor(h_a[:], got[:, b, :, 0:F], per_tile(has_in, c), ALU.mult))
                    st.settle()
                    dve.tensor_tensor(h_a[:], h_a[:], over_tiles(0), ALU.add).then_inc(ph.used.sem, 1)
                    wait(dve, ph.used, c + 1)
                    st.did(layer_norm(st, ph, h_b, h_a, c * 2 + 1))
                    st.settle()
                    st.did(dve.tensor_tensor(h_b[:], h_b[:], over_tiles(1), ALU.mult))
                    st.settle()
                    st.did(dve.tensor_tensor(h_b[:], h_b[:], over_tiles(2), ALU.add))
                    st.settle()
                    st.did(dve.tensor_tensor(h_a[:], h_b[:], x_nodes[:, bass.ds(c * CT, CT), :], ALU.add))
                    st.settle()
                    wait(dve, ph.chunk_out[b], i * 16)
                    layer_norm(st, ph, table[:, b, :, 0:F], h_a, c * 2 + 2).then_inc(ph.x_done.sem, 1)
                    assert st.n == 11

            groups(dve, nodes5, NB)


_WEIGHTS = ['L0_gnn_Wq', 'L0_gnn_bq', 'L0_gnn_Wk', 'L0_gnn_bk', 'L0_gnn_We', 'L0_gnn_be', 'L0_gnn_Wv', 'L0_gnn_bv',
            'L1_gnn_W_self1', 'L1_gnn_W_neigh1', 'L1_gnn_W_pool', 'L1_gnn_b_pool', 'L1_gnn_W_self2',
            'L1_gnn_W_neigh2', 'L1_gnn_g1', 'L1_gnn_beta1', 'L1_gnn_g2', 'L1_gnn_beta2', 'L2_gnn_weight',
            'L2_gnn_bias', 'L3_gnn_W', 'L3_gnn_bias', 'L3_gnn_gamma', 'L3_gnn_beta']


def laid_out(inputs):
    import numpy as np

    x = np.asarray(inputs["x"])
    src, dst = np.asarray(inputs["src"]), np.asarray(inputs["dst"])
    attr, weight = np.asarray(inputs["edge_attr_96"]), np.asarray(inputs["edge_weight"])
    n, f = x.shape
    e = src.shape[0]
    nt, et = node_tiles(n), edge_tiles(e)

    def padded(v, rows, value):
        out = np.full((rows,) + v.shape[1:], value, v.dtype)
        out[:v.shape[0]] = v
        return out

    xp = padded(x, nt * P, 0)
    dp = padded(dst, et * P, n)
    before = np.full((et * P,), -1, dst.dtype)
    before[1:] = dp[:-1]
    tiles = dp.reshape(et, P)
    return n, e, f, {
        "x_nodes": np.ascontiguousarray(xp.reshape(nt, P, f).transpose(1, 0, 2)),
        "x_cols": np.ascontiguousarray(xp.T),
        "dst_tiles": tiles,
        "dst_before": before.reshape(et, P),
        "tile_first": np.ascontiguousarray(tiles[:, 0]).reshape(1, et),
        "dst_cols": np.ascontiguousarray(tiles.T),
        "src_cols": np.ascontiguousarray(padded(src, et * P, n).reshape(et // TQ, TQ, P).transpose(0, 2, 1)),
        "weight_cols": np.ascontiguousarray(padded(weight, et * P, 0).reshape(et, P).T),
        "attr_cols": np.ascontiguousarray(padded(attr, et * P, 0).T),
        **{name: np.ascontiguousarray(inputs[name]) for name in _WEIGHTS},
    }


def kernel(**inputs):
    import concourse.bacc as _bacc
    from concourse.bass_utils import run_bass_kernel_spmd as _run

    nc = _bacc.Bacc("TRN2", target_bir_lowering=False, num_devices=1)
    n, e, f, arrays = laid_out(inputs)
    args = {name: nc.dram_tensor("in_" + name, v.shape, mybir.dt.from_np(v.dtype), kind="ExternalInput").ap()
            for name, v in arrays.items()}
    nt = node_tiles(n)
    args["out"] = nc.dram_tensor("out", (P, nt, f), F32, kind="ExternalOutput").ap()
    gnn_kernel(nc, n, e, {"F": f}, args)
    got = _run(nc, [{"in_" + name: v for name, v in arrays.items()}], core_ids=[0]).results[0]["out"]
    return got.transpose(1, 0, 2).reshape(nt * P, f)[:n]
```

```python
from contextlib import ExitStack

import concourse.bass as bass
from concourse import mybir

P = 128
TQ = 4
QE = TQ * P
GQ = 4
GP = GQ // 2
GT = GQ * TQ
CT = 5
CN = CT * P
CB = 2
HEADS = 8
RJ = 8
PARTS = 3
LN_EPS = 1e-5
BN_EPS = 1e-5
BN_DIM = 6

ALU = mybir.AluOpType
ACT = mybir.ActivationFunctionType
F32 = mybir.dt.float32
BF16 = mybir.dt.bfloat16
I32 = mybir.dt.int32
AX_X = mybir.AxisListType.X


def node_tiles(n):
    body = CT * CB * P
    return -(-(n + P) // body) * CT * CB


def edge_tiles(e):
    return -(-e // (P * GT)) * GT


class Signal:

    def __init__(self, sem, base):
        self.sem, self.base = sem, base


def wait(eng, signal, value):
    if not isinstance(value, int) or value > 0:
        eng.wait_ge(signal.sem, value + signal.base)


def groups(eng, body, n):
    body(0, n == 1)
    if n > 2:
        with eng.Fori(1, n - 1) as i:
            body(i, False)
    if n > 1:
        body(n - 1, True)


def staged(eng, front, back, n, back_first=False):
    def body(i, last):
        for b in range(CB):
            c = i * CB + b
            if not back_first:
                front(c, b, i)
            if not isinstance(c, int) or c > 0:
                back(c - 1, (b - 1) % CB, i if b else i - 1)
            if back_first:
                front(c, b, i)

    groups(eng, body, n)
    back(n * CB - 1, CB - 1, n - 1)


class Steps:

    def __init__(self, eng, signal, base, pin):
        self.eng, self.sem, self.base, self.n, self.pin = eng, signal.sem, base + signal.base, 0, pin

    def did(self, ins):
        ins.then_inc(self.sem, 1)
        self.n += 1

    def settle(self, pinned=False):
        self.eng.wait_ge(self.sem, self.base + self.n)
        if pinned:
            self.eng.sem_inc(self.pin, 1)


def gnn_kernel(nc, N, E, dims, a):
    F = dims["F"]
    NT, ET = node_tiles(N), edge_tiles(E)
    NP, EP = NT * P, ET * P
    NQ, NG = ET // TQ, ET // GT
    NCH, NB = NT // CT, NT // CT // CB
    RP = ET // RJ
    D = F // HEADS
    KV, AGG, PAIR = 2 * F, F + HEADS, 2 * F
    HALF = CN // 2
    assert RP <= P and F % 32 == 0 and F + 1 <= P and NG >= 3 and NB >= 3 and N + P <= NP

    ctx = ExitStack()
    with ctx:
        def sb(name, shape, dt=F32):
            return ctx.enter_context(nc.sbuf_tensor(name, shape, dt))

        def sem(name):
            return ctx.enter_context(nc.semaphore(name))

        def dram(name, shape, dt=F32):
            return nc.dram_tensor(name, shape, dt, kind="Internal").ap()

        kv_table = dram("kv_table", (NP, KV))
        q_table = dram("q_table", (NP, PARTS * F), BF16)
        pair_table = dram("pair_table", (NP, PAIR))
        ci_table = dram("ci_table", (NP, F))
        h_table = dram("h_table", (NP, F))
        sums = [dram(f"sums{n}", (EP, w)) for n, w in enumerate((AGG, PAIR, F, F))]
        rank_rows = dram("rank_rows", (NQ, QE), BF16)
        keep_rows = dram("keep_rows", (NQ, QE), BF16)
        carry_rows = dram("carry_rows", (NQ, QE))

        ident = sb("ident", [P, P])
        iota_row = sb("iota_row", [P, P], BF16)
        zeros_row = sb("zeros_row", [P, 2 * P], BF16)
        zeros = zeros_row[:, 0:P]
        upto = sb("upto", [P, P])
        ones = sb("ones", [P, P])
        iota_col = sb("iota_col", [P, 1])
        x_nodes = sb("x_nodes", [P, NT, F])
        rank_col = sb("rank_col", [P, ET])
        weight_col = sb("weight_col", [P, ET])
        src_lo = sb("src_lo", [P, ET])
        src_hi = sb("src_hi", [P, ET])
        dst_lo = sb("dst_lo", [P, ET])
        dst_hi = sb("dst_hi", [P, ET])
        starts = sb("starts", [1, ET], I32)
        wide = sb("wide", [P, 2, NP])
        w_qkv = sb("w_qkv", [F + 1, 3 * F])
        w_e = sb("w_e", [F + 1, F])
        w_pool = sb("w_pool", [F + 1, F])
        w_s1 = sb("w_s1", [F, F])
        w_s2 = sb("w_s2", [F, F])
        w_n1 = sb("w_n1", [F, F])
        w_n2 = sb("w_n2", [F, F])
        w_2 = sb("w_2", [F + 1, F])
        w_3 = sb("w_3", [F, F])
        bn_par = sb("bn_par", [F, 4])
        row_par = sb("row_par", [P, 3, F])
        src_idx = sb("src_idx", [P, GQ, TQ], I32)
        rows = sb("rows", [P, GQ, TQ, KV])
        attr = sb("attr", [F + 1, GQ, QE])
        rank_row = sb("rank_row", [P, GQ, QE], BF16)
        keep_row = sb("keep_row", [F, GQ, QE], BF16)
        carry = sb("carry", [P, GQ, QE])
        q_win = sb("q_win", [P, GQ, TQ, PARTS * F], BF16)
        out_rows = sb("out_rows", [P, GQ, TQ, KV])
        pick = sb("pick", [P, 2, QE], BF16)
        same = sb("same", [P, 2, TQ, P])
        prod = sb("prod", [P, TQ, F])
        score = sb("score", [P, TQ, HEADS])
        msg = sb("msg", [P, 2, TQ, AGG])
        scanned = sb("scanned", [F, 2, QE])
        hot_lo = sb("hot_lo", [P, 2, TQ, P], BF16)
        hot_hi = sb("hot_hi", [P, 2, TQ, NT], BF16)
        node_idx = sb("node_idx", [P, CB, CT], I32)
        got = sb("got", [P, CB, CT, KV])
        table = sb("table", [P, CB, CT, KV])
        q_parts = [got[:, b].bitcast(BF16)[:, :, 0:PARTS * F] for b in range(CB)]
        z_inv = sb("z_inv", [P, CT, HEADS])
        h_a = sb("h_a", [P, CT, F])
        h_b = sb("h_b", [P, CT, F])
        x_new = sb("x_new", [P, CB, CT, F])
        stats = sb("stats", [P, 2, CT, BN_DIM])
        mean_var = sb("mean_var", [P, 2, CT, 2])
        dev = sb("dev", [P, 2, CT])
        rdev = sb("rdev", [P, 2, CT])
        shift = sb("shift", [P, 2, CT])
        h_cols = sb("h_cols", [F + 1, 2, CN])
        cols = [h_cols[:, 0, :], h_cols[:, 1, :]] + [attr[:].rearrange("f k e -> f (k e)")[:, m * CN:(m + 1) * CN] for m in range(2)]
        bn_stat = sb("bn_stat", [F, 2, NCH * 2, BN_DIM])
        bn_mv = sb("bn_mv", [F, 2, 2])
        bn_a = sb("bn_a", [F, 8])
        count = sb("count", [P, NT])
        running = sb("running", [P, NT])
        degree = sb("degree", [P, 8, NT])
        last_edge = sb("last_edge", [P, 4, NT], I32)
        eps_z = sb("eps_z", [P, 1])
        has_in, no_in, r_mean, c_in, c_out, deg_in, tmp_a, tmp_b = (degree[:, n, :] for n in range(8))
        row_of_node = last_edge[:, 3, :]

        bank = [ctx.enter_context(nc.psum_tensor(f"bank{n}", [P, 512], F32)) for n in range(8)]

        W = RJ * P
        flat = wide[0:RP].rearrange("p a n -> p (a n)")
        edge_i = flat[:, 0:W].bitcast(I32)
        prev_i = flat[:, W:2 * W].bitcast(I32)
        carry_f = flat[:, W:2 * W]
        rank_f, new_f, hold_f, keep_f = (flat[:, m * W:(m + 1) * W] for m in range(2, 6))
        rank_b = same[0:RP, 0].rearrange("p j e -> p (j e)").bitcast(BF16)
        keep_b = same[0:RP, 1].rearrange("p j e -> p (j e)").bitcast(BF16)

        whole = [h_a, h_b]

        def quad(b, w):
            return b[:, 0:TQ * w].rearrange("p (j f) -> p j f", j=TQ)

        def five(b):
            return b[:, 0:CT * F].rearrange("p (j f) -> p j f", j=CT)

        made = sem("made")
        made_steps = sem("made_steps")
        ready = sem("ready")
        pin = sem("pin")
        held = sem("held")
        held_sp = sem("held_sp")
        held_act = sem("held_act")
        s_edges = sem("s_edges")
        s_first = sem("s_first")
        s_src = sem("s_src")
        s_weights = sem("s_weights")
        s_qkv = sem("s_qkv")
        s_nodes = sem("s_nodes")
        prep = Signal(sem("prep"), 0)
        rows_out = sem("rows_out")
        ranks_turned = sem("ranks_turned")
        last_found = sem("last_found")
        ranked = sem("ranked")
        deg_sums = sem("deg_sums")
        src_step = sem("src_step")
        deg_step = Signal(sem("deg_step"), 0)
        deg_ready = sem("deg_ready")
        deg_root = sem("deg_root")
        deg_done = sem("deg_done")
        bn_step = Signal(sem("bn_step"), 0)
        bn_ready = sem("bn_ready")
        bn_root = sem("bn_root")

        sems = {}

        def shared(name, n, totals, slots=0):
            if name not in sems:
                sems[name] = [sem(f"{name}{b}" if slots else name) for b in range(max(slots, 1))]
            found = [Signal(x, sum(totals[:n])) for x in sems[name]]
            return found if slots else found[0]

        class Pass:

            def __init__(self, n):
                def each(name, total):
                    return shared(name, n, [total] * 4, GQ)

                def pairs(name, total):
                    return shared(name, n, [total] * 4, GP)

                self.idx_in = pairs("idx_in", NG * 16)
                self.rows_in = each("rows_in", NG * 16 * TQ)
                self.rank_in = pairs("rank_in", NG * 16)
                self.carry_in = pairs("carry_in", NG * 16)
                self.out = pairs("out", NG * 16)
                self.same_done = shared("same_done", n, [NQ] * 4)
                self.agg_done = shared("agg_done", n, [ET] * 4)
                self.copied = shared("copied", n, [ET] * 4)
                self.hot_done = shared("hot_done", n, [NQ] * 4)
                self.hist_done = shared("hist_done", n, [NQ] * 4)
                if n == 0:
                    self.attr_in = shared("attr_in", 0, [0], GP)
                    self.win_in = shared("win_in", 0, [0], GQ)
                    self.pick_done = shared("pick_done", 0, [0])
                    self.q_done = shared("q_done", 0, [0])
                    self.prod_step = shared("prod_step", 0, [0])
                    self.prod_done = shared("prod_done", 0, [0])
                    self.score_step = shared("score_step", 0, [0])
                    self.clip_done = shared("clip_done", 0, [0])
                    self.exp_done = shared("exp_done", 0, [0])
                    self.msg_done = shared("msg_done", 0, [0])
                if n == 1:
                    self.keep_in = shared("keep_in", 0, [0], GP)
                    self.turn_done = shared("turn_done", 0, [0])
                    self.scan_done = shared("scan_done", 0, [0])
                    self.back_done = shared("back_done", 0, [0])
                    self.max_copied = shared("max_copied", 0, [0])

        class Phase:

            def __init__(self, n):
                def two(name, total, steps):
                    return shared(name, n, [NB * total * m for m in steps], CB)

                def one(name, steps):
                    return shared(name, n, [NCH * m for m in steps])

                self.x_in = two("x_in", 16,                       (1, 0, 0, 0, 0, 0))
                self.idx_ready = one("idx_ready",                 (0, 1, 1, 0, 1, 1))
                self.got_in = two("got_in", 16 * CT,              (0, 1, 1, 0, 1, 1))
                self.chunk_out = two("chunk_out", 16,             (2, 1, 0, 1, 1, 1))
                self.dve = one("dve",                             (5, 7, 0, 3, 4, 5))
                self.dve_2 = one("dve_2",                         (0, 0, 0, 0, 0, 6))
                self.dve_cols = one("dve_cols",                   (0, 0, 0, 1, 2, 0))
                self.used = one("used",                           (1, 1, 1, 1, 1, 1))
                self.x_done = one("x_done",                       (1, 1, 1, 1, 1, 1))
                self.pe = one("pe",                               (CT, 0, 0, 1, 0, 0))
                self.act = one("act",                             (CT, 0, 0, 1, 0, 1))
                self.turned = one("turned",                       (0, 1, 1, 0, 1, 0))
                self.cols = one("cols",                           (0, 1, 1, 1, 1, 0))
                self.mult = one("mult",                           (0, 1, 1, 0, 1, 0))
                self.turned_x = one("turned_x",                   (0, 0, 0, 0, 1, 0))
                self.cols_x = one("cols_x",                       (0, 0, 0, 0, 1, 0))
                self.mult_x = one("mult_x",                       (0, 0, 0, 0, 1, 0))
                self.kept = one("kept",                           (0, 1, 0, 0, 1, 0))
                self.table_done = one("table_done",               (0, 1, 0, 0, 1, 0))
                self.h_done = one("h_done",                       (0, 0, 1, 1, 1, 0))
                self.var_done = one("var_done",                   (0, 1, 0, 1, 1, 1))
                self.dev_done = one("dev_done",                   (0, 1, 0, 1, 1, 1))
                self.scale_done = one("scale_done",               (0, 0, 0, 1, 0, 1))
                self.var_done_2 = one("var_done_2",               (0, 0, 0, 0, 0, 1))
                self.dev_done_2 = one("dev_done_2",               (0, 0, 0, 0, 0, 1))
                self.scale_done_2 = one("scale_done_2",           (0, 0, 0, 0, 0, 1))

        passes = [Pass(n) for n in range(4)]
        phases = {name: Phase(n) for n, name in enumerate(range(6))}

        W_LOADS = 6 + 5 + 4 + 3
        PREP = 9
        WIN_SP = 2

        block = ctx.enter_context(nc.Block())

        def rows_of(t, c):
            return t.rearrange("(t p) w -> p t w", p=P)[:, bass.ds(c * CT, CT), :]

        def pair_rows(t, g):
            return t.rearrange("(g p j) w -> g p (j w)", p=P, j=2 * TQ)[bass.ds(g, 1)].rearrange("o p w -> (o p) w")

        def pair_row(t, g):
            return t.rearrange("(g h) e -> g (h e)", h=2)[bass.ds(g, 1), :]

        def load_window(eng, q, k, j):
            start = eng.value_load(starts[0:1, bass.ds(q * TQ + j, 1)], min_val=0, max_val=NP - P)
            eng.dma_start(q_win[:, k, j, :], q_table[bass.ds(start, P), :]).then_inc(passes[0].win_in[k].sem, 16)

        def load_rank(eng, s, g, h):
            eng.dma_start(rank_row[:, 2 * h:2 * h + 2, :], pair_row(rank_rows, g).to_broadcast([P, 2 * QE])).then_inc(s.rank_in[h].sem, 16)

        def edge_pass_sp(sp, n):
            s = passes[n]
            width = (AGG, PAIR, F, F)[n]

            def load_idx(g, h):
                sp.dma_start(src_idx[:, 2 * h:2 * h + 2, :], a["src_cols"][bass.ds(g * 2, 2)].rearrange("q p t -> p q t")).then_inc(s.idx_in[h].sem, 16)

            def load_carry(g, h):
                sp.dma_start(carry[P - 1:P, 2 * h:2 * h + 2, :], pair_row(carry_rows, g)).then_inc(s.carry_in[h].sem, 16)

            def load_keep(g, h):
                sp.dma_start(keep_row[:, 2 * h:2 * h + 2, :], pair_row(keep_rows, g).to_broadcast([F, 2 * QE])).then_inc(s.keep_in[h].sem, 16)

            def load_attr(g, h):
                sp.dma_start(attr[0:F, 2 * h:2 * h + 2, :], a["attr_cols"][:, bass.ds(g * (2 * QE), 2 * QE)]).then_inc(s.attr_in[h].sem, 16)

            def load_windows(g, h, m, windows):
                for j in range(windows):
                    load_window(sp, g * 2 + m, 2 * h + m, j)

            if n == 0:
                sp.wait_ge(s_first, 16)
                sp.wait_ge(rows_out, 48)
                for b in range(CB):
                    wait(sp, phases[0].chunk_out[b], 32 * NB)
            for h in range(GP):
                load_idx(h, h)
            for h in range(GP):
                load_rank(sp, s, h, h)
                load_carry(h, h)
                if n == 0:
                    load_attr(h, h)
                    for m in range(2):
                        load_windows(h, h, m, TQ)
                if n == 1:
                    load_keep(h, h)
            if n == 0:
                sp.dma_start(weight_col[:], a["weight_cols"]).then_inc(s_nodes, 16)
                sp.dma_start(x_nodes[:], a["x_nodes"]).then_inc(s_nodes, 16)

            def body(i, last):
                for h in range(GP):
                    g = i * GP + h
                    if not last:
                        for m in range(2):
                            wait(sp, s.rows_in[2 * h + m], (i + 1) * 16 * TQ)
                        load_idx(g + GP, h)
                        if n == 0:
                            wait(sp, s.q_done, (g + 1) * 2)
                            sp.sem_inc(held_sp, 1)
                            load_attr(g + GP, h)
                            load_windows(g + GP, h, 0, WIN_SP)
                        if n == 0:
                            load_windows(g + GP, h, 1, WIN_SP)
                        else:
                            wait(sp, s.same_done, (g + 1) * 2)
                            sp.sem_inc(held_sp, 1)
                            load_rank(sp, s, g + GP, h)
                        if n == 1:
                            wait(sp, s.scan_done, (g + 1) * 2)
                            sp.sem_inc(held_sp, 1)
                            load_keep(g + GP, h)
                    wait(sp, s.copied, (g + 1) * 2 * TQ)
                    if not last:
                        sp.sem_inc(held_sp, 1)
                        load_carry(g + GP, h)
                    if n == 1:
                        wait(sp, s.max_copied, (g + 1) * 2)
                    sp.dma_start(pair_rows(sums[n], g), out_rows[:, 2 * h:2 * h + 2, :, 0:width].rearrange("p k j w -> p (k j) w")).then_inc(s.out[h].sem, 16)

            groups(sp, body, NG)

        def node_phase_sp(sp, n, out_table, width):
            ph = phases[n]

            def body(i, last):
                for b in range(CB):
                    c = i * CB + b
                    wait(sp, ph.table_done if n in (1, 4) else ph.x_done, c + 1)
                    dst = out_table[:, bass.ds(c * CT, CT), :] if n == 5 else rows_of(out_table, c)
                    sp.dma_start(dst, table[:, b, :, 0:width]).then_inc(ph.chunk_out[b].sem, 16)

            groups(sp, body, NB)

        @block.sync
        def _(sp):
            sp.dma_start(edge_i, a["dst_tiles"].rearrange("(p j) e -> p (j e)", j=RJ)).then_inc(s_edges, 16)
            sp.dma_start(prev_i, a["dst_before"].rearrange("(p j) e -> p (j e)", j=RJ)).then_inc(s_edges, 16)
            F1 = F + 1
            for m, (w, b) in enumerate((("L0_gnn_Wq", "L0_gnn_bq"), ("L0_gnn_Wk", "L0_gnn_bk"),
                                        ("L0_gnn_Wv", "L0_gnn_bv"))):
                sp.dma_start(w_qkv[0:F, m * F:(m + 1) * F], a[w]).then_inc(s_qkv, 16)
                sp.dma_start(w_qkv[F:F1, m * F:(m + 1) * F], a[b].rearrange("(o f) -> o f", o=1)).then_inc(s_qkv, 16)

            def load_x(c, b):
                sp.dma_start(h_cols[0:F, b, :], a["x_cols"][:, bass.ds(c * CN, CN)]).then_inc(phases[0].x_in[b].sem, 16)

            for b in range(CB):
                load_x(b, b)
            sp.dma_start(src_lo[:].bitcast(I32).rearrange("p (g t) -> p g t", t=TQ), a["src_cols"].rearrange("g p t -> p g t")).then_inc(s_src, 16)
            sp.dma_start(dst_lo[:].bitcast(I32), a["dst_cols"]).then_inc(s_src, 16)
            ph = phases[0]

            sp.dma_start(starts[:], a["tile_first"]).then_inc(s_first, 16)
            def load_weights():
                n = 0
                for t, w, b in ((w_e, "L0_gnn_We", "L0_gnn_be"), (w_pool, "L1_gnn_W_pool", "L1_gnn_b_pool"),
                                (w_2, "L2_gnn_weight", "L2_gnn_bias"), (w_s1, "L1_gnn_W_self1", None),
                                (w_s2, "L1_gnn_W_self2", None), (w_n1, "L1_gnn_W_neigh1", None),
                                (w_n2, "L1_gnn_W_neigh2", None), (w_3, "L3_gnn_W", None)):
                    sp.dma_start(t[0:F, :], a[w]).then_inc(s_weights, 16)
                    n += 1
                    if b:
                        sp.dma_start(t[F:F1, :], a[b].rearrange("(o f) -> o f", o=1)).then_inc(s_weights, 16)
                        n += 1
                for m, v in enumerate(("L1_gnn_g1", "L1_gnn_g2", "L1_gnn_beta1", "L1_gnn_beta2")):
                    sp.dma_start(bn_par[:, m:m + 1], a[v].rearrange("(f o) -> f o", o=1)).then_inc(s_weights, 16)
                    n += 1
                for m, v in enumerate(("L3_gnn_bias", "L3_gnn_gamma", "L3_gnn_beta")):
                    sp.dma_start(row_par[:, m, :], a[v].rearrange("(o f) -> o f", o=1).to_broadcast([P, F])).then_inc(s_weights, 16)
                    n += 1
                assert n == W_LOADS

            def next_x(c, b, i):
                if not isinstance(c, int) or c < NCH - CB:
                    wait(sp, ph.pe, (c + 1) * CT)
                    load_x(c + CB, b)
                if isinstance(c, int) and c == 1:
                    load_weights()

            def qkv_out(c, b, i):
                wait(sp, ph.x_done, c + 1)
                sp.dma_start(rows_of(q_table, c), q_parts[b]).then_inc(ph.chunk_out[b].sem, 16)
                sp.dma_start(rows_of(kv_table, c), table[:, b]).then_inc(ph.chunk_out[b].sem, 16)

            staged(sp, next_x, qkv_out, NB)
            wait(sp, prep, PREP)
            for t, s in ((rank_rows, rank_b), (keep_rows, keep_b), (carry_rows, carry_f)):
                sp.dma_start(t.rearrange("q (o e) -> (q o) e", o=1).rearrange("(p r) e -> p (r e)", p=RP), s).then_inc(rows_out, 16)

            edge_pass_sp(sp, 0)
            node_phase_sp(sp, 1, pair_table, PAIR)
            edge_pass_sp(sp, 1)
            node_phase_sp(sp, 3, ci_table, F)
            edge_pass_sp(sp, 2)
            node_phase_sp(sp, 4, h_table, F)
            edge_pass_sp(sp, 3)
            node_phase_sp(sp, 5, a["out"], F)
            for b in range(CB):
                wait(sp, phases[5].chunk_out[b], 16 * NB)

        def gather(pool, out, src, idx, done):
            pool.indirect_dma_start(out, None, src, bass.IndirectOffsetOnAxis(ap=idx, axis=0)).then_inc(done, 16)

        def edge_pass_pool(pool, n):
            s = passes[n]
            src = (kv_table, pair_table, ci_table, h_table)[n]
            width = (KV, PAIR, F, F)[n]
            ph = phases[(0, 1, 3, 4)[n]]

            def quad_gather(k):
                for j in range(TQ):
                    gather(pool, rows[:, k, j, 0:width], src, src_idx[:, k, j:j + 1], s.rows_in[k].sem)

            for b in range(CB):
                wait(pool, ph.chunk_out[b], (32 if n == 0 else 16) * NB)
            for k in range(GQ):
                wait(pool, s.idx_in[k // 2], 16)
                quad_gather(k)

            def body(i, last):
                for k in range(GQ):
                    wait(pool, s.idx_in[k // 2], (i + 2) * 16)
                    if n == 0:
                        wait(pool, s.msg_done, i * GQ + k + 1)
                    else:
                        wait(pool, s.agg_done, (i * GQ + k + 1) * TQ)
                    pool.sem_inc(held, 1)
                    quad_gather(k)

            groups(pool, body, NG - 1)

        def node_phase_pool(pool, n, width):
            ph = phases[n]
            at = {1: 0, 2: 1, 4: 2, 5: 3}[n]
            for h in range(GP):
                wait(pool, passes[at].out[h], 16 * NG)

            def body(i, last):
                for b in range(CB):
                    wait(pool, ph.idx_ready, i * CB + b + 1)
                    pool.sem_inc(held, 1)
                    for t in range(CT):
                        gather(pool, got[:, b, t, 0:width], sums[at], node_idx[:, b, t:t + 1], ph.got_in[b].sem)

            groups(pool, body, NB)

        @block.gpsimd
        def _(pool):
            pool.memset(ident[:], 0.0).then_inc(made_steps, 1)
            pool.wait_ge(made_steps, 1)
            pool.affine_select(out=ident[:], in_=ident[:], compare_op=ALU.not_equal, fill=1.0, base=0,
                               pattern=[[-1, P]], channel_multiplier=1).then_inc(made, 1)
            pool.iota(iota_row[:], [[1, P]], base=0, channel_multiplier=0, allow_small_or_imprecise_dtypes=True).then_inc(made, 1)
            pool.iota(iota_col[:], [[0, 1]], base=0, channel_multiplier=1, allow_small_or_imprecise_dtypes=True).then_inc(made, 1)
            pool.wait_ge(ready, 7)
            pool.affine_select(out=upto[:], in_=ones[:], compare_op=ALU.is_ge, fill=0.0, base=0,
                               pattern=[[1, P]], channel_multiplier=-1).then_inc(made, 1)

            edge_pass_pool(pool, 0)
            node_phase_pool(pool, 1, AGG)
            edge_pass_pool(pool, 1)
            node_phase_pool(pool, 2, PAIR)
            edge_pass_pool(pool, 2)
            node_phase_pool(pool, 4, F)
            edge_pass_pool(pool, 3)
            node_phase_pool(pool, 5, F)


        @block.tensor
        def _(pe):
            pe.wait_ge(s_qkv, 16 * 6)
            pe.wait_ge(made, 4)
            pe.wait_ge(ready, 7)
            ph = phases[0]

            def qkv(i, last):
                for b in range(CB):
                    c = i * CB + b
                    wait(pe, ph.x_in[b], (i + 1) * 16)
                    for t in range(CT):
                        wait(pe, ph.act, (c - 1) * CT + t + 1)
                        pe.matmul(bank[t][:, 0:3 * F], h_cols[:, b, t * P:(t + 1) * P], w_qkv[:], start=True, stop=True).then_inc(ph.pe.sem, 1)

            groups(pe, qkv, NB)
            pe.wait_ge(s_weights, 16 * W_LOADS)
            wait(pe, prep, PREP)
            for j in range(RJ):
                tr = pe.transpose(bank[5 + j // 4][:, (j % 4) * P:(j % 4) * P + RP], rank_f[:, j * P:(j + 1) * P], ident[0:RP, 0:RP])
            tr.then_inc(ranks_turned, 1)

            def aggregate(s, q, i, k, n, between=None):
                width = AGG if n == 0 else F
                wait(pe, s.same_done, q + 1)
                if n == 0:
                    wait(pe, s.msg_done, q + 1)
                wait(pe, s.carry_in[k // 2], (i + 1) * 16)
                for j in range(TQ):
                    acc = bank[4 + j % 2][:, 0:width]
                    wait(pe, s.copied, q * TQ + j - 1)
                    values = msg[:, k % 2, j, :] if n == 0 else rows[:, k, j, 0:F]
                    pe.matmul(acc, same[:, k % 2, j, :], values, start=True, stop=False)
                    if between:
                        between(j)
                    wait(pe, s.copied, q * TQ + j)
                    pk, pj = (k, j - 1) if j else ((k - 1) % GQ, TQ - 1)
                    pe.matmul(acc, carry[:, k, j * P:(j + 1) * P], out_rows[:, pk, pj, 0:width],
                              start=False, stop=True).then_inc(s.agg_done.sem, 1)

            hist = bank[7][:, 0:NT]

            def clear_counts():
                pe.matmul(bank[7][:, 0:2 * P], zeros, zeros_row[:], start=True, stop=False, skip_group_check=True)

            def keep_clock(n):
                for _ in range(n):
                    pe.matmul(bank[7][:, 0:2 * P], zeros, zeros_row[:], start=False, stop=False, skip_group_check=True)

            def count_nodes(s, q, k):
                wait(pe, s.hot_done, q + 1)
                for j in range(TQ):
                    mm = pe.matmul(hist, hot_lo[:, k % 2, j, :], hot_hi[:, k % 2, j, :], start=False, stop=False, skip_group_check=True)
                mm.then_inc(s.hist_done.sem, 1)

            s0 = passes[0]
            clear_counts()

            def factors(q, i, k, j):
                if j == 0:
                    wait(pe, s0.attr_in[k // 2], (i + 1) * 16)
                    wait(pe, s0.prod_done, q - 1)
                    wait(pe, s0.pick_done, q + 1)
                    wait(pe, s0.win_in[k], (i + 1) * 16 * TQ)
                pe.matmul(quad(bank[k % 2], F)[:, j, :], attr[:, k, j * P:(j + 1) * P], w_e[:], start=True, stop=True)
                for m in range(PARTS):
                    mm = pe.matmul(quad(bank[2 + k % 2], F)[:, j, :], pick[:, k % 2, j * P:(j + 1) * P],
                                   q_win[:, k, j, m * F:(m + 1) * F], start=(m == 0), stop=(m == PARTS - 1))
                if j == TQ - 1:
                    mm.then_inc(s0.q_done.sem, 1)

            def attention(i, last):
                for k in range(GQ):
                    q = i * GQ + k
                    more = not (last and k == GQ - 1)

                    def ahead(j, q=q, k=k):
                        factors(q + 1, i if k < GQ - 1 else i + 1, (k + 1) % GQ, j)

                    if isinstance(q, int) and q == 0:
                        for j in range(TQ):
                            ahead(j)
                    else:
                        aggregate(s0, q - 1, i if k else i - 1, (k - 1) % GQ, 0, ahead if more else None)
                        count_nodes(s0, q - 1, (k - 1) % GQ)
                        keep_clock(2)

            for j in range(TQ):
                factors(0, 0, 0, j)
            groups(pe, attention, NG)
            aggregate(s0, NQ - 1, NG - 1, GQ - 1, 0)
            count_nodes(s0, NQ - 1, GQ - 1)
            pe.wait_ge(last_found, 1)
            pe.matmul(bank[6][:, 0:NT], upto[:], deg_in, start=True, stop=True)
            pe.matmul(bank[6][:, NT:2 * NT], ones[:], deg_in, start=True, stop=True).then_inc(deg_sums, 1)

            def turn(b0, src, ph_sem=None):
                for t in range(CT):
                    tr = pe.transpose(bank[b0 + t // 4][0:F, (t % 4) * P:(t % 4 + 1) * P], src[:, t, :], ident[:])
                return tr

            ph = phases[1]

            def turn1(c, b, i):
                wait(pe, ph.x_done, c + 1)
                wait(pe, ph.cols, c)
                turn(0, x_new[:, b]).then_inc(ph.turned.sem, 1)

            def products1(c, b, i):
                wait(pe, ph.cols, c + 1)
                wait(pe, ph.table_done, c)
                for t in range(CT):
                    pe.matmul(five(bank[2])[:, t, :], cols[b][:, t * P:(t + 1) * P], w_pool[:], start=True, stop=True)
                for m, w in enumerate((w_s1, w_s2)):
                    for h in range(2):
                        mm = pe.matmul(bank[3 + 2 * m + h][0:F, 0:HALF], w[:], cols[b][0:F, h * HALF:(h + 1) * HALF], start=True, stop=True)
                mm.then_inc(ph.mult.sem, 1)

            staged(pe, turn1, products1, NB)

            s1 = passes[1]
            clear_counts()

            def sage(i, last):
                for k in range(GQ):
                    q = i * GQ + k
                    wait(pe, s1.rows_in[k], (i + 1) * 16 * TQ)
                    wait(pe, s1.scan_done, q - 1)
                    for j in range(TQ):
                        tr = pe.transpose(bank[k % 2][0:F, j * P:(j + 1) * P], rows[:, k, j, F:PAIR], ident[:])
                    tr.then_inc(s1.turn_done.sem, 1)
                    aggregate(s1, q, i, k, 1)
                    count_nodes(s1, q, k)
                    wait(pe, s1.scan_done, q + 1)
                    wait(pe, s1.max_copied, q - 1)
                    for j in range(TQ):
                        tr = pe.transpose(quad(bank[2 + k % 2], F)[:, j, :], scanned[:, k % 2, j * P:(j + 1) * P], ident[0:F, 0:F])
                    tr.then_inc(s1.back_done.sem, 1)

            groups(pe, sage, NG)

            ph = phases[2]

            def turn2(c, b, i):
                wait(pe, ph.h_done, c + 1)
                wait(pe, ph.cols, c)
                turn(0, h_a)
                turn(2, h_b).then_inc(ph.turned.sem, 1)

            def products2(c, b, i):
                wait(pe, ph.cols, c + 1)
                wait(pe, ph.x_done, c)
                for m, w in enumerate((w_n1, w_n2)):
                    for h in range(2):
                        mm = pe.matmul(bank[4 + 2 * m + h][0:F, 0:HALF], w[:], cols[2 * b + m][0:F, h * HALF:(h + 1) * HALF], start=True, stop=True)
                mm.then_inc(ph.mult.sem, 1)

            pe.wait_ge(deg_done, 1)
            staged(pe, turn2, products2, NB, back_first=True)

            ph = phases[3]

            def nodes3(i, last):
                for b in range(CB):
                    c = i * CB + b
                    wait(pe, ph.h_done, c + 1)
                    wait(pe, ph.used, c - 1)
                    for t in range(CT):
                        tr = pe.transpose(five(bank[b])[:, t, :], cols[b][0:F, t * P:(t + 1) * P], ident[0:F, 0:F])
                    tr.then_inc(ph.pe.sem, 1)

            groups(pe, nodes3, NB)

            def plain(n):
                s = passes[n]

                def body(i, last):
                    for k in range(GQ):
                        wait(pe, s.rows_in[k], (i + 1) * 16 * TQ)
                        aggregate(s, i * GQ + k, i, k, n, lambda j: keep_clock(2))

                groups(pe, body, NG)

            plain(2)

            ph = phases[4]

            def products4(c, b, i):
                wait(pe, ph.h_done, c + 1)
                wait(pe, ph.cols, c)
                turn(0, h_a).then_inc(ph.turned.sem, 1)
                wait(pe, ph.cols, c + 1)
                wait(pe, ph.x_done, c - 1)
                for t in range(CT):
                    mm = pe.matmul(five(bank[2 + b])[:, t, :], cols[0][:, t * P:(t + 1) * P], w_2[:], start=True, stop=True)
                mm.then_inc(ph.mult.sem, 1)

            def products4_x(c, b, i):
                wait(pe, ph.x_done, c + 1)
                wait(pe, ph.cols_x, c)
                turn(4, x_new[:, b]).then_inc(ph.turned_x.sem, 1)
                wait(pe, ph.cols_x, c + 1)
                wait(pe, ph.table_done, c)
                for t in range(CT):
                    mm = pe.matmul(five(bank[6])[:, t, :], cols[1][0:F, t * P:(t + 1) * P], w_3[:], start=True, stop=True)
                mm.then_inc(ph.mult_x.sem, 1)

            staged(pe, products4, products4_x, NB)
            plain(3)

        @block.scalar
        def _(act):
            ph = phases[0]

            def qkv(i, last):
                for b in range(CB):
                    c = i * CB + b
                    wait(act, ph.used, c - 1)
                    wait(act, ph.chunk_out[b], i * 32)
                    for t in range(CT):
                        wait(act, ph.pe, c * CT + t + 1)
                        act.mul(whole[b][:, t, :], bank[t][:, 0:F], float(D) ** -0.5)
                        act.copy(table[:, b, t, :], bank[t][:, F:3 * F]).then_inc(ph.act.sem, 1)

            groups(act, qkv, NB)

            def copy_tile(s, q, i, k, j, width):
                wait(act, s.agg_done, q * TQ + j + 1)
                if j == 0:
                    wait(act, s.out[k // 2], i * 16)
                act.copy(out_rows[:, k, j, 0:width], bank[4 + j % 2][:, 0:width]).then_inc(s.copied.sem, 1)

            s0 = passes[0]
            act.wait_ge(s_first, 16)
            act.wait_ge(rows_out, 48)

            def attention(i, last):
                for k in range(GQ):
                    q = i * GQ + k
                    behind = not isinstance(q, int) or q > 0
                    pk, pi = (k - 1) % GQ, (i if k else i - 1)
                    if behind:
                        copy_tile(s0, q - 1, pi, pk, 0, AGG)
                    wait(act, s0.clip_done, q + 1)
                    wait(act, s0.msg_done, q - 1)
                    act.activation(quad(bank[6], HEADS * 2)[:, :, (k % 2) * HEADS:(k % 2 + 1) * HEADS], score[:], ACT.Exp)
                    act.activation(msg[:, k % 2, :, F:AGG], score[:], ACT.Exp).then_inc(s0.exp_done.sem, 1)
                    for j in range(TQ):
                        if behind and j > 0:
                            copy_tile(s0, q - 1, pi, pk, j, AGG)
                        if j == 1 and k % 2 and not last:
                            wait(act, s0.same_done, q + 1)
                            act.sem_inc(held_act, 1)
                            load_rank(act, s0, i * GP + k // 2 + GP, k // 2)
                        if j >= WIN_SP and not last:
                            wait(act, s0.q_done, q + 1)
                            load_window(act, q + GQ, k, j)

            groups(act, attention, NG)
            for j in range(TQ):
                copy_tile(s0, NQ - 1, NG - 1, GQ - 1, j, AGG)

            def root(ph, c, second=False):
                m = 1 if second else 0
                wait(act, ph.var_done_2 if second else ph.var_done, c)
                act.activation(dev[:, m], mean_var[:, m, :, 1], ACT.Sqrt, bias=eps_z[:, 0:1]).then_inc((ph.dev_done_2 if second else ph.dev_done).sem, 1)

            def normalise(ph, out, src, c, second=False):
                m = 1 if second else 0
                wait(act, ph.scale_done_2 if second else ph.scale_done, c)
                for t in range(CT):
                    ins = act.activation(out[:, t, :], src[:, t, :], ACT.Identity, bias=shift[:, m, t:t + 1], scale=rdev[:, m, t:t + 1])
                return ins

            def columns(b0, dst):
                act.copy(dst[0:F, 0:4 * P], bank[b0][0:F, :])
                return act.copy(dst[0:F, 4 * P:CN], bank[b0 + 1][0:F, 0:P])

            act.wait_ge(deg_ready, 1)
            act.activation(tmp_b, tmp_a, ACT.Sqrt).then_inc(deg_root, 1)

            ph = phases[1]

            def keep1(c, b, i):
                wait(act, ph.x_done, c + 1)
                wait(act, ph.chunk_out[b], i * 16)
                act.copy(table[:, b, :, 0:F], x_new[:, b])
                act.copy(x_nodes[:, bass.ds(c * CT, CT), :], x_new[:, b]).then_inc(ph.kept.sem, 1)
                wait(act, ph.turned, c + 1)
                wait(act, ph.mult, c - 1)
                columns(0, cols[b]).then_inc(ph.cols.sem, 1)
                if not isinstance(c, int) or c < NCH - 1:
                    root(ph, c + 2)

            def out1(c, b, i):
                wait(act, ph.mult, c + 1)
                act.activation(table[:, b, :, F:PAIR], five(bank[2]), ACT.Relu)
                for m in range(2):
                    for h in range(2):
                        cp = act.copy(wide[0:F, m, bass.ds(c * CN + h * HALF, HALF)], bank[3 + 2 * m + h][0:F, 0:HALF])
                cp.then_inc(ph.table_done.sem, 1)

            root(ph, 1)
            staged(act, keep1, out1, NB)

            def plain(n):
                s = passes[n]

                def body(i, last):
                    for k in range(GQ):
                        q = i * GQ + k
                        for j in range(TQ):
                            copy_tile(s, q, i, k, j, F)
                        if n == 1:
                            wait(act, s.back_done, q + 1)
                            act.copy(out_rows[:, k, :, F:PAIR], quad(bank[2 + k % 2], F)).then_inc(s.max_copied.sem, 1)

                groups(act, body, NG)

            plain(1)
            act.wait_ge(deg_ready, 2)
            act.activation(tmp_b, tmp_a, ACT.Sqrt).then_inc(deg_root, 1)

            ph = phases[2]

            def nodes2(i, last):
                for b in range(CB):
                    c = i * CB + b
                    wait(act, ph.turned, c + 1)
                    wait(act, ph.mult, c - 1)
                    columns(0, cols[2 * b])
                    columns(2, cols[2 * b + 1]).then_inc(ph.cols.sem, 1)

            groups(act, nodes2, NB)
            act.wait_ge(bn_ready, 1)
            act.activation(bn_a[:, 0:2], bn_mv[:, :, 1], ACT.Sqrt, bias=eps_z[0:F, 0:1]).then_inc(bn_root, 1)

            ph = phases[3]

            def scale3(c, b):
                wait(act, ph.pe, c - 1)
                act.activation(cols[b][0:F, :], wide[0:F, 0, bass.ds(c * CN, CN)], ACT.Identity, bias=bn_a[:, 6:7], scale=bn_a[:, 2:3]).then_inc(ph.cols.sem, 1)

            def next_scale3(c, b, i):
                if not isinstance(c, int) or c < NCH - 1:
                    scale3(c + 1, 1 - b)

            def norm3(c, b, i):
                root(ph, c + 1)
                here = x_nodes[:, bass.ds(c * CT, CT), :]
                normalise(ph, here, h_b, c + 1).then_inc(ph.act.sem, 1)
                wait(act, ph.act, c + 1)
                wait(act, ph.chunk_out[b], i * 16)
                for t in range(CT):
                    ins = act.mul(table[:, b, t, 0:F], x_nodes[:, bass.ds(c * CT + t, 1), :].rearrange("p o f -> p (o f)"), c_out[:, bass.ds(c * CT + t, 1)])
                ins.then_inc(ph.x_done.sem, 1)

            act.wait_ge(bn_ready, 2)
            act.wait_ge(deg_done, 2)
            scale3(0, 0)
            staged(act, next_scale3, norm3, NB)
            plain(2)

            ph = phases[4]

            def columns4(c, b, i):
                wait(act, ph.turned, c + 1)
                wait(act, ph.mult, c)
                columns(0, cols[0]).then_inc(ph.cols.sem, 1)

            def out4(c, b, i):
                root(ph, c + 1)
                wait(act, ph.x_done, c + 1)
                act.copy(x_nodes[:, bass.ds(c * CT, CT), :], x_new[:, b]).then_inc(ph.kept.sem, 1)
                wait(act, ph.turned_x, c + 1)
                columns(4, cols[1]).then_inc(ph.cols_x.sem, 1)
                wait(act, ph.mult_x, c + 1)
                wait(act, ph.chunk_out[b], i * 16)
                act.copy(table[:, b, :, 0:F], five(bank[6])).then_inc(ph.table_done.sem, 1)

            staged(act, columns4, out4, NB)
            plain(3)

            ph = phases[5]

            def nodes5(i, last):
                for b in range(CB):
                    c = i * CB + b
                    behind = not isinstance(c, int) or c > 0
                    root(ph, c + 1)
                    if behind:
                        root(ph, c, True)
                    wait(act, ph.x_done, c - 1)
                    normalise(ph, x_new[:, b], whole[b], c + 1).then_inc(ph.act.sem, 1)
                    if behind:
                        out5(c - 1, 1 - b, i if b else i - 1)

            def out5(c, b, i):
                wait(act, ph.chunk_out[b], i * 16)
                normalise(ph, table[:, b, :, 0:F], x_new[:, b], c + 1, True).then_inc(ph.x_done.sem, 1)

            groups(act, nodes5, NB)
            root(ph, NCH, True)
            out5(NCH - 1, CB - 1, NB - 1)

        @block.vector
        def _(dve):
            dve.memset(ones[:], 1.0).then_inc(ready, 1)
            dve.memset(carry[:], 0.0).then_inc(ready, 1)
            dve.memset(out_rows[:, GQ - 1, :, :], 0.0).then_inc(ready, 1)
            dve.memset(eps_z[:], LN_EPS).then_inc(ready, 1)
            dve.memset(zeros_row[:], 0.0).then_inc(ready, 1)
            dve.memset(attr[F:F + 1, :, :], 1.0).then_inc(ready, 1)
            dve.memset(h_cols[F:F + 1, :, :], 1.0).then_inc(ready, 1)
            dve.wait_ge(ready, 7)
            dve.wait_ge(made, 4)
            dve.sem_inc(pin, 1)


            def tiled(t):
                return t.rearrange("p (j e) -> p j e", j=RJ)

            st = Steps(dve, prep, 0, pin)
            dve.wait_ge(s_edges, 32)
            st.did(dve.tensor_tensor(keep_f, edge_i, prev_i, ALU.is_equal))
            st.did(dve.tensor_tensor(new_f, edge_i, prev_i, ALU.not_equal))
            st.did(dve.memset(hold_f, 1.0))
            st.settle()
            st.did(dve.memset(tiled(hold_f)[:, :, 0:1], 0.0))
            st.did(dve.memset(tiled(new_f)[:, :, 0:1], 0.0))
            st.settle()
            st.did(dve.tensor_tensor_scan(rank_f, hold_f, new_f, 0.0, ALU.mult, ALU.add))
            st.did(dve.tensor_copy(keep_b, keep_f))
            st.settle()
            st.did(dve.tensor_copy(rank_b, rank_f))
            st.did(dve.scalar_tensor_tensor(out=tiled(carry_f), in0=tiled(rank_f), scalar=0.0,
                                            in1=tiled(keep_f)[:, :, 0:1].to_broadcast([RP, RJ, P]),
                                            op0=ALU.is_equal, op1=ALU.mult))
            assert st.n == PREP

            ph = phases[0]

            def split(i, last):
                for b in range(CB):
                    c = i * CB + b
                    st = Steps(dve, ph.dve, c * 5, pin)
                    wait(dve, ph.act, (c + 1) * CT)
                    wait(dve, ph.chunk_out[b], i * 32)
                    rest = whole[b][:]
                    part = [q_parts[b][:, :, m * F:(m + 1) * F] for m in range(PARTS)]
                    st.did(dve.tensor_copy(part[0], rest))
                    st.settle()
                    st.did(dve.tensor_tensor(rest, rest, part[0], ALU.subtract))
                    st.settle()
                    st.did(dve.tensor_copy(part[1], rest))
                    st.settle()
                    st.did(dve.tensor_tensor(rest, rest, part[1], ALU.subtract))
                    st.settle()
                    st.did(dve.tensor_copy(part[2], rest))
                    st.settle()
                    dve.sem_inc(ph.used.sem, 1)
                    dve.sem_inc(ph.x_done.sem, 1)

            groups(dve, split, NB)

            dve.wait_ge(ranks_turned, 1)
            by_j = rank_col[:].rearrange("p (r j) -> p j r", j=RJ)
            for j in range(RJ):
                cp = dve.tensor_copy(by_j[:, j, :], bank[5 + j // 4][:, (j % 4) * P:(j % 4) * P + RP])
            cp.then_inc(ranked, 1)

            dve.wait_ge(s_src, 32)
            for lo, hi in ((src_lo, src_hi), (dst_lo, dst_hi)):
                dve.tensor_scalar(hi[:].bitcast(I32), lo[:].bitcast(I32), P.bit_length() - 1, None, ALU.arith_shift_right).then_inc(src_step, 1)
            dve.wait_ge(src_step, 2)
            for lo in (src_lo, dst_lo):
                dve.tensor_scalar(lo[:].bitcast(I32), lo[:].bitcast(I32), P - 1, None, ALU.bitwise_and).then_inc(src_step, 1)
            dve.wait_ge(src_step, 4)
            for part in (src_lo, src_hi, dst_lo, dst_hi):
                dve.tensor_copy(part[:], part[:].bitcast(I32)).then_inc(src_step, 1)
            dve.wait_ge(src_step, 8)
            dve.wait_ge(ranked, 1)

            def same_tile(s, q, k, j, n):
                if j == 0:
                    wait(dve, s.agg_done, (q - 1) * TQ)
                at = bass.ds(q * TQ + j, 1)
                mine, theirs = rank_col[:, at], rank_row[:, k, j * P:(j + 1) * P]
                if n == 3:
                    ins = dve.tensor_scalar(same[:, k % 2, j, :], theirs, mine, weight_col[:, at], ALU.is_equal, ALU.mult)
                else:
                    ins = dve.tensor_scalar(same[:, k % 2, j, :], theirs, mine, None, ALU.is_equal)
                if j == TQ - 1:
                    ins.then_inc(s.same_done.sem, 1)

            def same_runs(s, q, i, k, n):
                for j in range(TQ):
                    same_tile(s, q, k, j, n)

            def one_hot(s, q, k, lo, hi):
                wait(dve, s.hist_done, q - 1)
                for j in range(TQ):
                    at = bass.ds(q * TQ + j, 1)
                    dve.tensor_scalar(hot_lo[:, k % 2, j, :], iota_row[:], lo[:, at], None, ALU.is_equal)
                    ins = dve.tensor_scalar(hot_hi[:, k % 2, j, :], iota_row[:, 0:NT], hi[:, at], None, ALU.is_equal)
                ins.then_inc(s.hot_done.sem, 1)

            s0 = passes[0]

            def picks(q, i, k):
                wait(dve, s0.rank_in[k // 2], (i + 1) * 16)
                wait(dve, s0.q_done, q - 1)
                dve.tensor_scalar(pick[:, k % 2, :], rank_row[:, k, :], iota_col[:, 0:1], None, ALU.is_equal).then_inc(s0.pick_done.sem, 1)

            def attention(i, last):
                for k in range(GQ):
                    q = i * GQ + k
                    if not (last and k == GQ - 1):
                        picks(q + 1, i if k < GQ - 1 else i + 1, (k + 1) % GQ)
                    wait(dve, s0.rows_in[k], (i + 1) * 16 * TQ)
                    wait(dve, s0.q_done, q + 1)
                    dve.tensor_tensor(prod[:], quad(bank[2 + k % 2], F), rows[:, k, :, 0:F], ALU.mult).then_inc(s0.prod_step.sem, 1)
                    same_tile(s0, q, k, 0, 0)
                    wait(dve, s0.prod_step, q + 1)
                    dve.tensor_tensor(prod[:], quad(bank[k % 2], F), prod[:], ALU.mult).then_inc(s0.prod_done.sem, 1)
                    same_tile(s0, q, k, 1, 0)
                    wait(dve, s0.prod_done, q + 1)
                    dve.tensor_reduce(score[:], prod[:].rearrange("p j (h d) -> p j h d", h=HEADS), AX_X, ALU.add).then_inc(s0.score_step.sem, 1)
                    same_tile(s0, q, k, 2, 0)
                    wait(dve, s0.score_step, q + 1)
                    dve.tensor_scalar(score[:], score[:], 5.0, -5.0, ALU.min, ALU.max).then_inc(s0.clip_done.sem, 1)
                    same_tile(s0, q, k, 3, 0)
                    one_hot(s0, q, k, dst_lo, dst_hi)
                    wait(dve, s0.exp_done, q + 1)
                    dve.tensor_tensor(msg[:, k % 2, :, 0:F].rearrange("p j (h d) -> p j h d", h=HEADS),
                                      rows[:, k, :, F:KV].rearrange("p j (h d) -> p j h d", h=HEADS),
                                      quad(bank[6], HEADS * 2)[:, :, (k % 2) * HEADS:(k % 2 + 1) * HEADS]
                                      .rearrange("p j (h o) -> p j h o", o=1).to_broadcast([P, TQ, HEADS, D]),
                                      ALU.mult).then_inc(s0.msg_done.sem, 1)

            picks(0, 0, 0)
            groups(dve, attention, NG)

            wait(dve, s0.hist_done, NQ)
            st = Steps(dve, deg_step, 0, pin)
            st.did(dve.tensor_copy(deg_in, bank[7][:, 0:NT]))
            st.settle()
            dve.sem_inc(last_found, 1)
            dve.wait_ge(deg_sums, 1)
            st.did(dve.tensor_tensor_scan(running[:], ones[:, 0:NT], bank[6][:, NT:2 * NT], 0.0, ALU.mult, ALU.add))
            st.did(dve.tensor_copy(count[:], bank[6][:, 0:NT]))
            st.settle()
            st.did(dve.tensor_tensor(count[:], count[:], running[:], ALU.add))
            st.settle()
            st.did(dve.tensor_tensor(count[:], count[:], bank[6][:, NT:2 * NT], ALU.subtract))
            st.settle()
            e_i, part_i, tile_i, row_i = (last_edge[:, m, :] for m in range(4))
            st.did(dve.tensor_scalar(tmp_a, count[:], -1.0, 0.0, ALU.add, ALU.max))
            st.settle()
            st.did(dve.tensor_copy(e_i, tmp_a))
            st.settle()
            st.did(dve.tensor_scalar(part_i, e_i, P - 1, (2 * TQ).bit_length() - 1, ALU.bitwise_and, ALU.logical_shift_left))
            st.did(dve.tensor_scalar(tile_i, e_i, P.bit_length() - 1, 2 * TQ - 1, ALU.logical_shift_right, ALU.bitwise_and))
            st.settle()
            st.did(dve.tensor_tensor(part_i, part_i, tile_i, ALU.bitwise_or))
            st.did(dve.tensor_scalar(e_i, e_i, (2 * QE).bit_length() - 1, (2 * QE).bit_length() - 1, ALU.logical_shift_right, ALU.logical_shift_left))
            st.settle()
            st.did(dve.tensor_tensor(row_i, part_i, e_i, ALU.bitwise_or))
            st.did(dve.tensor_scalar(has_in, deg_in, 0.0, None, ALU.is_gt))
            st.did(dve.tensor_scalar(no_in, deg_in, 0.0, None, ALU.is_le))
            st.did(dve.tensor_scalar(tmp_a, deg_in, 1.0, None, ALU.max))
            st.settle()
            st.did(dve.reciprocal(r_mean, tmp_a))
            dve.sem_inc(deg_ready, 1)
            st.settle()
            st.did(dve.tensor_tensor(r_mean, r_mean, has_in, ALU.mult))
            dve.wait_ge(deg_root, 1)
            st.did(dve.reciprocal(c_in, tmp_b))
            st.settle()
            st.did(dve.tensor_tensor(c_in, c_in, has_in, ALU.mult))
            st.settle()
            dve.sem_inc(last_found, 1)

            def per_tile(t, c):
                return t[:, bass.ds(c * CT, CT)].rearrange("p (t o) -> p t o", o=1).to_broadcast([P, CT, F])

            def moments(st, ph, src, second=False):
                m = 1 if second else 0
                for t in range(CT):
                    ins = dve.bn_stats(stats[:, m, t, :], src[:, t, :])
                st.did(ins)
                st.settle(True)
                for t in range(CT):
                    ins = dve.bn_aggr(mean_var[:, m, t, :], stats[:, m, t, :])
                st.did(ins)
                st.settle()
                dve.sem_inc((ph.var_done_2 if second else ph.var_done).sem, 1)

            def scales(st, ph, rounds, second=False):
                m = 1 if second else 0
                wait(dve, ph.dev_done_2 if second else ph.dev_done, rounds)
                st.did(dve.reciprocal(rdev[:, m], dev[:, m]))
                st.settle()
                dve.scalar_tensor_tensor(out=shift[:, m], in0=mean_var[:, m, :, 0], scalar=-1.0, in1=rdev[:, m],
                                         op0=ALU.mult, op1=ALU.mult).then_inc((ph.scale_done_2 if second else ph.scale_done).sem, 1)

            def layer_norm(st, ph, out, src, rounds):
                moments(st, ph, src)
                wait(dve, ph.dev_done, rounds)
                st.did(dve.reciprocal(rdev[:, 0], dev[:, 0]))
                st.settle()
                for t in range(CT):
                    ins = dve.tensor_scalar(out[:, t, :], src[:, t, :], mean_var[:, 0, t, 0:1], rdev[:, 0, t:t + 1], ALU.subtract, ALU.mult)
                return ins

            def indices(ph, c, b):
                dve.tensor_copy(node_idx[:, b, :], row_of_node[:, bass.ds(c * CT, CT)]).then_inc(ph.idx_ready.sem, 1)

            def first_indices(ph):
                for b in range(CB):
                    indices(ph, b, b)

            def next_indices(ph, c, b):
                wait(dve, ph.used, c + 1)
                if not isinstance(c, int) or c < NCH - CB:
                    indices(ph, c + CB, b)

            ph = phases[1]
            first_indices(ph)

            def nodes1(i, last):
                for b in range(CB):
                    c = i * CB + b
                    st = Steps(dve, ph.dve, c * 7, pin)
                    wait(dve, ph.got_in[b], (i + 1) * 16 * CT)
                    st.did(dve.tensor_scalar(z_inv[:], got[:, b, :, F:AGG], 1e-6, None, ALU.add))
                    st.settle()
                    st.did(dve.reciprocal(z_inv[:], z_inv[:]))
                    st.settle()
                    st.did(dve.tensor_tensor(z_inv[:], z_inv[:], per_tile(has_in, c)[:, :, 0:HEADS], ALU.mult))
                    st.settle()
                    st.did(dve.tensor_tensor(h_a[:].rearrange("p t (h d) -> p t h d", h=HEADS),
                                             got[:, b, :, 0:F].rearrange("p t (h d) -> p t h d", h=HEADS),
                                             z_inv[:].rearrange("p t (h o) -> p t h o", o=1).to_broadcast([P, CT, HEADS, D]), ALU.mult))
                    st.settle()
                    dve.tensor_tensor(h_b[:], h_a[:], x_nodes[:, bass.ds(c * CT, CT), :], ALU.add).then_inc(ph.used.sem, 1)
                    next_indices(ph, c, b)
                    wait(dve, ph.kept, c - 1)
                    wait(dve, ph.turned, c - 1)
                    layer_norm(st, ph, x_new[:, b], h_b, c + 1).then_inc(ph.x_done.sem, 1)
                    assert st.n == 7

            dve.wait_ge(s_nodes, 32)
            groups(dve, lambda i, last: nodes1(i, last), NB)

            s1 = passes[1]

            def sage(i, last):
                for k in range(GQ):
                    q = i * GQ + k
                    wait(dve, s1.rank_in[k // 2], (i + 1) * 16)
                    wait(dve, s1.keep_in[k // 2], (i + 1) * 16)
                    same_runs(s1, q, i, k, 1)
                    wait(dve, s1.turn_done, q + 1)
                    wait(dve, s1.scan_done, q)
                    wait(dve, s1.back_done, q - 1)
                    first = isinstance(q, int) and q == 0
                    dve.tensor_tensor_scan(scanned[:, k % 2, :], keep_row[:, k, :], bank[k % 2][0:F, :],
                                           0.0 if first else scanned[:, (k - 1) % 2, QE - 1:QE],
                                           ALU.mult, ALU.max).then_inc(s1.scan_done.sem, 1)
                    one_hot(s1, q, k, src_lo, src_hi)

            groups(dve, sage, NG)
            wait(dve, s1.hist_done, NQ)
            dve.tensor_scalar(tmp_a, bank[7][:, 0:NT], 1.0, None, ALU.max).then_inc(deg_ready, 1)
            dve.wait_ge(deg_ready, 2)
            dve.sem_inc(deg_done, 1)
            dve.wait_ge(deg_root, 2)
            dve.reciprocal(c_out, tmp_b).then_inc(deg_done, 1)

            ph = phases[2]

            def means(c, b, i):
                wait(dve, ph.got_in[b], (i + 1) * 16 * CT)
                wait(dve, ph.turned, c)
                dve.tensor_tensor(h_a[:], got[:, b, :, 0:F], per_tile(r_mean, c), ALU.mult)
                dve.tensor_tensor(h_b[:], got[:, b, :, F:PAIR], per_tile(has_in, c), ALU.mult).then_inc(ph.h_done.sem, 1)
                wait(dve, ph.h_done, c + 1)
                dve.sem_inc(ph.used.sem, 1)
                next_indices(ph, c, b)

            def add2(c, b, i):
                wait(dve, ph.mult, c + 1)
                for m in range(2):
                    for h in range(2):
                        part = wide[0:F, m, bass.ds(c * CN + h * HALF, HALF)]
                        ins = dve.tensor_tensor(part, bank[4 + 2 * m + h][0:F, 0:HALF], part, ALU.add)
                ins.then_inc(ph.x_done.sem, 1)
                wait(dve, ph.x_done, c + 1)
                for m in range(2):
                    for h in range(2):
                        valid = min(HALF, N - (c * CN + h * HALF)) if isinstance(c, int) else HALF
                        if valid > 0:
                            ins = dve.bn_stats(bn_stat[:, m, bass.ds(c * 2 + h, 1), :].rearrange("p o s -> p (o s)"),
                                               wide[0:F, m, bass.ds(c * CN + h * HALF, valid)])
                if isinstance(c, int) and c >= NCH - CB:
                    ins.then_inc(bn_step.sem, 1)

            first_indices(ph)
            staged(dve, means, add2, NB)
            halves = -(-N // HALF)
            st = Steps(dve, bn_step, CB, pin)
            st.settle()
            for m in range(2):
                ins = dve.bn_aggr(bn_mv[:, m, :], bn_stat[:, m, 0:halves, :].rearrange("p c s -> p (c s)"))
            st.did(ins)
            st.settle()
            dve.sem_inc(bn_ready, 1)
            dve.wait_ge(bn_root, 1)
            st.did(dve.reciprocal(bn_a[:, 2:4], bn_a[:, 0:2]))
            st.settle()
            st.did(dve.tensor_tensor(bn_a[:, 2:4], bn_a[:, 2:4], bn_par[:, 0:2], ALU.mult))
            st.settle()
            st.did(dve.tensor_tensor(bn_a[:, 4:6], bn_mv[:, :, 0], bn_a[:, 2:4], ALU.mult))
            st.settle()
            st.did(dve.tensor_tensor(bn_a[:, 4:6], bn_par[:, 2:4], bn_a[:, 4:6], ALU.subtract))
            st.settle()
            st.did(dve.tensor_tensor(bn_a[:, 6:7], bn_a[:, 4:5], bn_a[:, 5:6], ALU.add))
            st.settle()
            dve.sem_inc(bn_ready, 1)

            ph = phases[3]

            def activate(c, b, i):
                st = Steps(dve, ph.dve_cols, c, pin)
                part = cols[b][0:F, :]
                wait(dve, ph.cols, c + 1)
                st.did(dve.scalar_tensor_tensor(out=part, in0=wide[0:F, 1, bass.ds(c * CN, CN)], scalar=bn_a[:, 3:4], in1=part, op0=ALU.mult, op1=ALU.add))
                st.settle()
                dve.scalar_tensor_tensor(out=part, in0=part, scalar=0.01, in1=part, op0=ALU.mult, op1=ALU.max).then_inc(ph.h_done.sem, 1)
                assert st.n == 1

            def norm3(c, b, i):
                st = Steps(dve, ph.dve, c * 3, pin)
                wait(dve, ph.pe, c + 1)
                wait(dve, ph.act, c)
                dve.tensor_tensor(h_b[:], five(bank[b]), x_nodes[:, bass.ds(c * CT, CT), :], ALU.add).then_inc(ph.used.sem, 1)
                wait(dve, ph.used, c + 1)
                moments(st, ph, h_b)
                scales(st, ph, c + 1)
                assert st.n == 3

            dve.wait_ge(deg_done, 2)
            staged(dve, activate, norm3, NB)

            def plain(n):
                s = passes[n]

                def body(i, last):
                    for k in range(GQ):
                        wait(dve, s.rank_in[k // 2], (i + 1) * 16)
                        same_runs(s, i * GQ + k, i, k, n)

                groups(dve, body, NG)

            plain(2)

            ph = phases[4]

            def sums4(c, b, i):
                st = Steps(dve, ph.dve_cols, c * 2, pin)
                wait(dve, ph.got_in[b], (i + 1) * 16 * CT)
                wait(dve, ph.turned, c)
                wait(dve, ph.x_done, c - 1)
                here = x_nodes[:, bass.ds(c * CT, CT), :]
                st.did(dve.tensor_tensor(h_b[:], got[:, b, :, 0:F], per_tile(c_in, c), ALU.mult))
                st.did(dve.tensor_tensor(h_a[:], here, per_tile(no_in, c), ALU.mult))
                st.settle()
                dve.tensor_tensor(h_a[:], h_a[:], h_b[:], ALU.add).then_inc(ph.h_done.sem, 1)
                wait(dve, ph.h_done, c + 1)
                dve.sem_inc(ph.used.sem, 1)
                next_indices(ph, c, b)
                assert st.n == 2

            def norm4(c, b, i):
                st = Steps(dve, ph.dve, c * 4, pin)
                wait(dve, ph.x_done, c)
                wait(dve, ph.mult, c + 1)
                st.did(dve.tensor_tensor(h_b[:], five(bank[2 + b]), x_nodes[:, bass.ds(c * CT, CT), :], ALU.add))
                st.settle()
                wait(dve, ph.kept, c - 1)
                wait(dve, ph.turned_x, c - 1)
                layer_norm(st, ph, x_new[:, b], h_b, c + 1).then_inc(ph.x_done.sem, 1)
                assert st.n == 4

            first_indices(ph)
            staged(dve, sums4, norm4, NB)
            plain(3)

            ph = phases[5]

            def over_tiles(m):
                return row_par[:, m:m + 1, :].to_broadcast([P, CT, F])

            def sum5(c, b, i):
                st = Steps(dve, ph.dve, c * 5, pin)
                y = whole[b][:]
                wait(dve, ph.got_in[b], (i + 1) * 16 * CT)
                wait(dve, ph.act, c - 1)
                st.did(dve.tensor_tensor(y, got[:, b, :, 0:F], per_tile(has_in, c), ALU.mult))
                st.settle()
                st.did(dve.tensor_tensor(y, y, over_tiles(0), ALU.add))
                st.settle()
                dve.sem_inc(ph.used.sem, 1)
                next_indices(ph, c, b)
                moments(st, ph, y)
                return st

            def residual5(c, b):
                st = Steps(dve, ph.dve_2, c * 6, pin)
                y = x_new[:, b]
                wait(dve, ph.act, c + 1)
                st.did(dve.tensor_tensor(y, y, over_tiles(1), ALU.mult))
                st.settle()
                st.did(dve.tensor_tensor(y, y, over_tiles(2), ALU.add))
                st.settle()
                st.did(dve.tensor_tensor(y, y, x_nodes[:, bass.ds(c * CT, CT), :], ALU.add))
                st.settle()
                wait(dve, ph.x_done, c)
                moments(st, ph, y, True)
                return st

            def nodes5(i, last):
                for b in range(CB):
                    c = i * CB + b
                    behind = not isinstance(c, int) or c > 0
                    first = sum5(c, b, i)
                    if behind:
                        second = residual5(c - 1, 1 - b)
                    scales(first, ph, c + 1)
                    assert first.n == 5
                    if behind:
                        scales(second, ph, c, True)
                        assert second.n == 6

            first_indices(ph)
            groups(dve, nodes5, NB)
            scales(residual5(NCH - 1, CB - 1), ph, NCH, True)


_WEIGHTS = ['L0_gnn_Wq', 'L0_gnn_bq', 'L0_gnn_Wk', 'L0_gnn_bk', 'L0_gnn_We', 'L0_gnn_be', 'L0_gnn_Wv', 'L0_gnn_bv',
            'L1_gnn_W_self1', 'L1_gnn_W_neigh1', 'L1_gnn_W_pool', 'L1_gnn_b_pool', 'L1_gnn_W_self2',
            'L1_gnn_W_neigh2', 'L1_gnn_g1', 'L1_gnn_beta1', 'L1_gnn_g2', 'L1_gnn_beta2', 'L2_gnn_weight',
            'L2_gnn_bias', 'L3_gnn_W', 'L3_gnn_bias', 'L3_gnn_gamma', 'L3_gnn_beta']


def laid_out(inputs):
    import numpy as np

    x = np.asarray(inputs["x"])
    src, dst = np.asarray(inputs["src"]), np.asarray(inputs["dst"])
    attr, weight = np.asarray(inputs["edge_attr_96"]), np.asarray(inputs["edge_weight"])
    n, f = x.shape
    e = src.shape[0]
    nt, et = node_tiles(n), edge_tiles(e)

    def padded(v, rows, value):
        out = np.full((rows,) + v.shape[1:], value, v.dtype)
        out[:v.shape[0]] = v
        return out

    xp = padded(x, nt * P, 0)
    dp = padded(dst, et * P, n)
    before = np.full((et * P,), -1, dst.dtype)
    before[1:] = dp[:-1]
    tiles = dp.reshape(et, P)
    return n, e, f, {
        "x_nodes": np.ascontiguousarray(xp.reshape(nt, P, f).transpose(1, 0, 2)),
        "x_cols": np.ascontiguousarray(xp.T),
        "dst_tiles": tiles,
        "dst_before": before.reshape(et, P),
        "tile_first": np.ascontiguousarray(tiles[:, 0]).reshape(1, et),
        "dst_cols": np.ascontiguousarray(tiles.T),
        "src_cols": np.ascontiguousarray(padded(src, et * P, n).reshape(et // TQ, TQ, P).transpose(0, 2, 1)),
        "weight_cols": np.ascontiguousarray(padded(weight, et * P, 0).reshape(et, P).T),
        "attr_cols": np.ascontiguousarray(padded(attr, et * P, 0).T),
        **{name: np.ascontiguousarray(inputs[name]) for name in _WEIGHTS},
    }


def kernel(**inputs):
    import concourse.bacc as _bacc
    from concourse.bass_utils import run_bass_kernel_spmd as _run

    nc = _bacc.Bacc("TRN2", target_bir_lowering=False, num_devices=1)
    n, e, f, arrays = laid_out(inputs)
    args = {name: nc.dram_tensor("in_" + name, v.shape, mybir.dt.from_np(v.dtype), kind="ExternalInput").ap()
            for name, v in arrays.items()}
    nt = node_tiles(n)
    args["out"] = nc.dram_tensor("out", (P, nt, f), F32, kind="ExternalOutput").ap()
    gnn_kernel(nc, n, e, {"F": f}, args)
    got = _run(nc, [{"in_" + name: v for name, v in arrays.items()}], core_ids=[0]).results[0]["out"]
    return got.transpose(1, 0, 2).reshape(nt * P, f)[:n]
```
